# Optimizing a Trainium2 kernel written in Bass

```python
import numpy as np
import jax
import jax.numpy as jnp

def _softmax(x, axis=-1):
    return jax.nn.softmax(x, axis=axis)

def _gelu(x):
    return jax.nn.gelu(x, approximate=True)

def _silu(x):
    return jax.nn.silu(x)

def _sigmoid(x):
    return jax.nn.sigmoid(x)

def _layernorm(x, axis=-1, eps=1e-05):
    m = jnp.mean(x, axis=axis, keepdims=True)
    v = jnp.var(x, axis=axis, keepdims=True)
    return (x - m) / jnp.sqrt(v + eps)

def _scatter_add(tgt, idx, src, axis=0):
    return tgt.at[idx].add(src)

def _segment_sum(src, seg, n):
    return jax.ops.segment_sum(src, seg, n)
kernel_name = 'mk_adj_resnorm_d4_adj_r2_1fc909'

def setup_inputs(seed: int=0):
    np.random.seed(seed)
    _w = jnp.asarray

    def _rec_inputs():
        import jax
        import jax.numpy as jnp
        _gk = jax.random.key(seed)
        x = -0.0002928 + 1 * jax.random.normal(jax.random.fold_in(_gk, 1), (4096, 256), jnp.float32)
        _a = jax.random.bernoulli(jax.random.fold_in(_gk, 2), 0.00195312, (4096, 4096))
        _a = jnp.logical_or(_a, jnp.swapaxes(_a, -1, -2))
        _a = jnp.logical_or(_a, jnp.eye(4096, dtype=bool))
        _af = _a.astype(jnp.float32)
        _af = _af * jax.random.uniform(jax.random.fold_in(_gk, 3), (4096, 4096), jnp.float32, 0.05, 5.41998)
        adj = _af
        return (x, adj)
    x, adj = _rec_inputs()

    def _L0_gnn_setup():
        import jax, jax.numpy as jnp
        import numpy as np
        N = 4096
        D = 256
        EPS = 1e-12
        key = jax.random.key(seed)
        k1, k2 = jax.random.split(key)
        cur = jax.random.normal(k1, (N, D), dtype=jnp.float32)
        incidence_m = jax.random.normal(k2, (N, N), dtype=jnp.float32)
        return {'cur': cur, 'incidence_m': incidence_m}
    _L0_gnn_all = _L0_gnn_setup()
    _L0_gnn_in = {k: v for k, v in _L0_gnn_all.items() if k in ()}
    del _L0_gnn_all

    def _L1_gnn_setup():
        import jax, jax.numpy as jnp
        import numpy as np
        KAPPA = -1.0
        EPS = 1e-10
        N, D_IN, D_OUT = (4096, 256, 256)

        def _artan_k(x):
            sc = np.sqrt(-KAPPA)
            return jnp.arctanh(jnp.clip(sc * x, -1.0 + 1e-07, 1.0 - 1e-07)) / sc

        def _tan_k(x):
            sc = np.sqrt(-KAPPA)
            return jnp.tanh(sc * x) / sc

        def _clamp_abs(x, eps=EPS):
            return jnp.where(x >= 0, 1.0, -1.0) * jnp.maximum(jnp.abs(x), eps)

        def _norm(x):
            return jnp.sqrt(jnp.maximum(jnp.sum(x * x, axis=-1, keepdims=True), EPS * EPS))

        def mobius_matvec(W, x):
            x_norm = _norm(x)
            mx = x @ W
            mx_norm = _norm(mx)
            res = _tan_k(mx_norm / x_norm * _artan_k(x_norm)) * (mx / mx_norm)
            return jnp.where(mx_norm <= EPS, 0.0, res)

        def mobius_scalar_mul(r, x):
            x_norm = _norm(x)
            return _tan_k(r * _artan_k(x_norm)) * (x / x_norm)

        def weighted_midpoint_lincomb(A, X):
            gamma = jnp.maximum(2.0 / (1.0 + KAPPA * jnp.sum(X * X, axis=-1, keepdims=True)), 1e-15)
            denom = _clamp_abs(A @ (gamma - 1.0))
            nom = A @ (gamma * X)
            two_mean = nom / denom
            sq = jnp.sum(two_mean * two_mean, axis=-1, keepdims=True)
            a_mean = two_mean / (1.0 + jnp.sqrt(jnp.maximum(1.0 + KAPPA * sq, EPS)))
            alpha = jnp.sum(A, axis=-1, keepdims=True)
            return mobius_scalar_mul(alpha, a_mean)

        def logmap0(x):
            xn = _norm(x)
            return _artan_k(xn) * x / xn

        def expmap0(u):
            un = _norm(u)
            return _tan_k(un) * u / un
        key = jax.random.key(seed)
        k1, k2, k3 = jax.random.split(key, 3)
        X = jax.random.normal(k1, (N, D_IN), dtype=jnp.float32) * 0.001
        A_hat = jax.random.uniform(k2, (N, N), dtype=jnp.float32) / N
        W = jax.random.normal(k3, (D_IN, D_OUT), dtype=jnp.float32) * 0.01
        return {'X': X, 'A_hat': A_hat, 'W': W}
    _L1_gnn_all = _L1_gnn_setup()
    _L1_gnn_in = {k: v for k, v in _L1_gnn_all.items() if k in ('W',)}
    del _L1_gnn_all

    def _L2_gnn_setup():
        import jax, jax.numpy as jnp
        import numpy as np
        N = 4096
        INPUT_DIM = 256
        HIDDEN_DIM = 128

        def gcn_layer(adj, x, w):
            return jax.nn.relu(adj @ (x @ w))
        key = jax.random.key(seed)
        ks = jax.random.split(key, 8)
        scale = 0.05
        X = jax.random.normal(ks[0], (N, INPUT_DIM), dtype=jnp.float32)
        adj_ = jax.random.uniform(ks[1], (N, N), dtype=jnp.float32) / N
        dims = [(INPUT_DIM, HIDDEN_DIM), (HIDDEN_DIM, HIDDEN_DIM), (HIDDEN_DIM, HIDDEN_DIM // 2), (HIDDEN_DIM // 2, HIDDEN_DIM), (HIDDEN_DIM, HIDDEN_DIM), (HIDDEN_DIM, INPUT_DIM)]
        Ws = [jax.random.normal(ks[2 + i], d, dtype=jnp.float32) * scale for i, d in enumerate(dims)]
        return {'X': X, 'adj_': adj_, 'W1': Ws[0], 'W2': Ws[1], 'W3': Ws[2], 'W4': Ws[3], 'W5': Ws[4], 'W6': Ws[5]}
    _L2_gnn_all = _L2_gnn_setup()
    _L2_gnn_in = {k: v for k, v in _L2_gnn_all.items() if k in ('W1', 'W2', 'W3', 'W4', 'W5', 'W6')}
    del _L2_gnn_all

    def _L3_gnn_setup():
        import jax, jax.numpy as jnp
        import numpy as np
        AVG_DEG = 32
        key = jax.random.key(seed)
        k1, k2, k3 = jax.random.split(key, 3)
        N, D_IN, D_OUT = (4096, 256, 256)
        x = jax.random.normal(k1, (N, D_IN), dtype=jnp.float32)
        u = jax.random.uniform(k2, (N, N), dtype=jnp.float32)
        A = (u < AVG_DEG / (2.0 * N)).astype(jnp.float32)
        A = A + A.T
        A = jnp.clip(A, 0.0, 1.0) * (1.0 - jnp.eye(N, dtype=jnp.float32))
        W = jax.random.normal(k3, (D_OUT, D_IN), dtype=jnp.float32) * (1.0 / np.sqrt(D_IN))
        b = jnp.zeros((D_OUT,), dtype=jnp.float32)
        return {'x': x, 'A': A, 'W': W, 'b': b}
    _L3_gnn_all = _L3_gnn_setup()
    _L3_gnn_in = {k: v for k, v in _L3_gnn_all.items() if k in ('W', 'b')}
    del _L3_gnn_all
    return {'x': x, 'adj': adj, 'L1_gnn_W': _L1_gnn_in['W'], 'L2_gnn_W1': _L2_gnn_in['W1'], 'L2_gnn_W2': _L2_gnn_in['W2'], 'L2_gnn_W3': _L2_gnn_in['W3'], 'L2_gnn_W4': _L2_gnn_in['W4'], 'L2_gnn_W5': _L2_gnn_in['W5'], 'L2_gnn_W6': _L2_gnn_in['W6'], 'L3_gnn_W': _L3_gnn_in['W'], 'L3_gnn_b': _L3_gnn_in['b']}

def reference(x, adj, L1_gnn_W, L2_gnn_W1, L2_gnn_W2, L2_gnn_W3, L2_gnn_W4, L2_gnn_W5, L2_gnn_W6, L3_gnn_W, L3_gnn_b):
    import jax
    import jax.numpy as jnp

    def _L0_gnn_ref(cur, incidence_m):
        import jax, jax.numpy as jnp
        import numpy as np
        N = 4096
        D = 256
        EPS = 1e-12
        mask = incidence_m > 0
        head = jax.lax.stop_gradient(mask.astype(incidence_m.dtype))
        head = head / jnp.maximum(jnp.sqrt(jnp.sum(head * head, axis=-1, keepdims=True)), EPS)
        inc = incidence_m + head
        edge_fea = inc @ cur
        edge_degree = jnp.sum(inc, axis=-1, keepdims=True)
        return edge_fea / edge_degree

    def _L1_gnn_ref(X, A_hat, W):
        import jax, jax.numpy as jnp
        import numpy as np
        KAPPA = -1.0
        EPS = 1e-10
        N, D_IN, D_OUT = (4096, 256, 256)

        def _artan_k(x):
            sc = np.sqrt(-KAPPA)
            return jnp.arctanh(jnp.clip(sc * x, -1.0 + 1e-07, 1.0 - 1e-07)) / sc

        def _tan_k(x):
            sc = np.sqrt(-KAPPA)
            return jnp.tanh(sc * x) / sc

        def _clamp_abs(x, eps=EPS):
            return jnp.where(x >= 0, 1.0, -1.0) * jnp.maximum(jnp.abs(x), eps)

        def _norm(x):
            return jnp.sqrt(jnp.maximum(jnp.sum(x * x, axis=-1, keepdims=True), EPS * EPS))

        def mobius_matvec(W, x):
            x_norm = _norm(x)
            mx = x @ W
            mx_norm = _norm(mx)
            res = _tan_k(mx_norm / x_norm * _artan_k(x_norm)) * (mx / mx_norm)
            return jnp.where(mx_norm <= EPS, 0.0, res)

        def mobius_scalar_mul(r, x):
            x_norm = _norm(x)
            return _tan_k(r * _artan_k(x_norm)) * (x / x_norm)

        def weighted_midpoint_lincomb(A, X):
            gamma = jnp.maximum(2.0 / (1.0 + KAPPA * jnp.sum(X * X, axis=-1, keepdims=True)), 1e-15)
            denom = _clamp_abs(A @ (gamma - 1.0))
            nom = A @ (gamma * X)
            two_mean = nom / denom
            sq = jnp.sum(two_mean * two_mean, axis=-1, keepdims=True)
            a_mean = two_mean / (1.0 + jnp.sqrt(jnp.maximum(1.0 + KAPPA * sq, EPS)))
            alpha = jnp.sum(A, axis=-1, keepdims=True)
            return mobius_scalar_mul(alpha, a_mean)

        def logmap0(x):
            xn = _norm(x)
            return _artan_k(xn) * x / xn

        def expmap0(u):
            un = _norm(u)
            return _tan_k(un) * u / un
        XW = mobius_matvec(W, X)
        AXW = weighted_midpoint_lincomb(A_hat, XW)
        return expmap0(jax.nn.relu(logmap0(AXW)))

    def _L2_gnn_ref(X, adj_, W1, W2, W3, W4, W5, W6):
        import jax, jax.numpy as jnp
        import numpy as np
        N = 4096
        INPUT_DIM = 256
        HIDDEN_DIM = 128

        def gcn_layer(adj, x, w):
            return jax.nn.relu(adj @ (x @ w))
        z = gcn_layer(adj_, X, W1)
        z = gcn_layer(adj_, z, W2)
        z = gcn_layer(adj_, z, W3)
        z = gcn_layer(adj_, z, W4)
        z = gcn_layer(adj_, z, W5)
        z = gcn_layer(adj_, z, W6)
        return z

    def _L3_gnn_ref(x, A, W, b):
        import jax, jax.numpy as jnp
        import numpy as np
        AVG_DEG = 32
        N = A.shape[0]
        A_t = A + jnp.eye(N, dtype=A.dtype)
        deg = jnp.sum(A_t, axis=1)
        d_inv_sqrt = jnp.where(deg > 0, jax.lax.rsqrt(deg), 0.0)
        adj_norm = A_t * d_inv_sqrt[:, None] * d_inv_sqrt[None, :]
        h = adj_norm @ x
        out = h @ W.T + b
        return jax.nn.relu(out)
    x = _layernorm(x + _L0_gnn_ref(x, adj), axis=-1)
    x = _layernorm(x + _L1_gnn_ref(x, adj, L1_gnn_W), axis=-1)
    x = _layernorm(x + _L2_gnn_ref(x, adj, L2_gnn_W1, L2_gnn_W2, L2_gnn_W3, L2_gnn_W4, L2_gnn_W5, L2_gnn_W6), axis=-1)
    x = _layernorm(x + _L3_gnn_ref(x, adj, L3_gnn_W, L3_gnn_b), axis=-1)
    return x

_drawn_inputs = setup_inputs


def setup_inputs(seed=0):
    import zlib

    import numpy as np

    out = dict(_drawn_inputs(seed))
    spreads = {'L3_gnn_b': (0.0, 0.1)}
    factors = {}
    for name, (base, spread) in spreads.items():
        noise = np.random.default_rng([zlib.crc32(name.encode()), seed]).standard_normal(out[name].shape)
        drawn = base * np.exp(spread * noise) if base else spread * noise
        out[name] = jnp.asarray(drawn.astype(out[name].dtype))
    for name, factor in factors.items():
        out[name] = (out[name] * factor).astype(out[name].dtype)
    return out
```

```python
from contextlib import ExitStack

import concourse.bass as bass
from concourse import mybir

ALU = mybir.AluOpType
ACT = mybir.ActivationFunctionType
AX = mybir.AxisListType
F32 = mybir.dt.float32
F16 = mybir.dt.float16
BF16 = mybir.dt.bfloat16
I32 = mybir.dt.int32

P = 128
LN_EPS = 1e-5
NORM_EPS = 1e-12
EPS = 1e-10
CLIP = 1.0 - 1e-7
TOP = 2.0 ** 14
TINY = 2.0 ** -100
EXPONENT = 0x7F800000

SLOTS = 4
GK = 8
MOB, G1, G2, G3, G4, G5, G6, NORM = range(8)
NAMES = ["mob", "g1", "g2", "g3", "g4", "g5", "g6", "norm"]


class Chain:

    def __init__(self, eng, sem, base=0):
        self.eng, self.sem, self.base, self.n = eng, sem, base, 0

    def __call__(self, ins):
        ins.then_inc(self.sem, 1)
        self.n += 1
        self.eng.wait_ge(self.sem, self.base + self.n)


def build(nc, x, adj, w_mob, w1, w2, w3, w4, w5, w6, w_norm_t, b_rows, out):
    N, D = x.shape
    T = N // P
    K = N // P
    NG = K // GK
    GROUPS = T // SLOTS
    H = w1.shape[1]
    H2 = w3.shape[1]
    WZ = D + 2
    WIDTH = {MOB: D, G1: H, G2: H, G3: H2, G4: H2, G5: H, G6: H, NORM: D}
    CHUNKS = T // 4

    ctx = ExitStack()
    with ctx:
        def sb(name, shape, dt=F32):
            return ctx.enter_context(nc.sbuf_tensor(name, shape, dt))

        made = {}

        def sem(name):
            if name not in made:
                made[name] = ctx.enter_context(nc.semaphore(name))
            return made[name]

        def total(name, stage):
            turning = ("inc", MOB, G6)
            if name in ("z_max_ready", "z_max_turned", "z_pair_ready", "z_pair_sent", "z_scale_ready"):
                return 1
            if name == "z_high_done":
                return T + 1 if stage == MOB else CHUNKS
            if name == "z_low_done":
                return T if stage == MOB else CHUNKS
            if name == "x_kept" and stage == MOB:
                return GROUPS
            if name == "dve_scales":
                return 0 if stage in ("inc", MOB) else 5
            if name == "dve_conv":
                return {G3: T, G5: T, G6: 3 * T}.get(stage, 0)
            given = {
                "acc_read": ("inc", *range(8)), "agg_done": tuple(range(8)), "xs_ready": (*turning, NORM),
                "xT_ready": turning, "xs_turned": turning, "x_kept": turning,
                "prod_ready": (*turning, G4), "prod_read": (*turning, G3, G4, G5),
                "var_ready": ("inc", G6, NORM), "dev_ready": ("inc", G6, NORM),
                "half_ready": (G1, G2, G3, G4, G5, G6), "rT_ready": (G1, G2, G4, G6),
                "r_turned": (G1, G2, G4, G6), "small_ready": (G1, G2, G4, G6), "small_read": (G1, G2, G4, G6),
                "z_turned": (G4,), "zT_ready": (G4,), "rows_ready": (G6,),
            }[name]
            return T if stage in given else 0

        def at(name, stage, value):
            before = ["inc", *range(8)]
            return sem(name), sum(total(name, s) for s in before[:before.index(stage)]) + value

        pairs_dram = nc.dram_tensor("adj_pairs", [T, P, K * 2 * P], F16, kind="Internal").ap()

        bank = ctx.enter_context(nc.psum_tensor("bank", [P, 8, 512], F32))

        X = sb("X", [P, T, D])
        Z = sb("Z", [P, T, WZ])
        ZP = sb("ZP", [P, T * 2 * WZ], F16)
        arena = sb("arena", [P, 73728 // 2], F16)
        RAW = arena[:, 0:4 * N].bitcast(F32).rearrange("p (b n) -> p b n", b=2)
        PAIR = arena[:, 4 * N:6 * N].rearrange("p (g k h i) -> p g k h i", g=NG, k=GK, h=2)
        MASK = arena[:, 6 * N:7 * N].rearrange("p (g k i) -> p g k i", g=NG, k=GK)
        junk_abs = arena[:, 7 * N:8 * N].bitcast(BF16)
        junk_count = arena[:, 8 * N:9 * N].bitcast(BF16)
        SLOT = arena[:, 0:SLOTS * K * 2 * P].rearrange("p (s k h i) -> p s k h i", s=SLOTS, k=K, h=2)

        wmob_sb = sb("wmob_sb", [P, D // P, D])
        w1_sb = sb("w1_sb", [P, D // P, H])
        w2_sb = sb("w2_sb", [P, H])
        w3_sb = sb("w3_sb", [P, H2])
        w4_sb = sb("w4_sb", [H2, H])
        w5_sb = sb("w5_sb", [P, H])
        w6_sb = sb("w6_sb", [P, D])
        wnorm_sb = sb("wnorm_sb", [P, D // P, D])
        b_sb = sb("b_sb", [P, D])
        ident = sb("ident", [P, P])
        ones = sb("ones", [1, P])

        abs_sum = sb("abs_sum", [P, T])
        count = sb("count", [P, T])
        root_count = sb("root_count", [P, T])
        row_scale = sb("row_scale", [P, T])
        row_inv = sb("row_inv", [P, T])
        row_sum = sb("row_sum", [P, T])
        x_sq = sb("x_sq", [P, T])
        m_sq = sb("m_sq", [P, T])
        z_bound = sb("z_bound", [P, T])
        unscale = sb("unscale", [P, T])
        z_factor = sb("z_factor", [P, T])
        gamma1 = sb("gamma1", [P, T])
        deg_root = sb("deg_root", [P, T])
        z_max = sb("z_max", [P, 1])
        z_top = sb("z_top", [1, 4])
        z_pair = sb("z_pair", [1, 2])
        z_scale = sb("z_scale", [P, 2])
        stat = sb("stat", [P, 16])
        roots_in = sb("roots_in", [P, 3, T])
        roots = sb("roots", [P, 3, T])
        bt = sb("bt", [P, 10, T])
        gt = sb("gt", [P, 24, SLOTS])
        y4 = sb("y4", [P, SLOTS, D])
        xs4 = sb("xs4", [P, SLOTS, D])
        y = y4[:, 0, :]
        xs = xs4[:, 0, :]
        half = y4[:, 1, 0:H]
        r = y4[:, 2, 0:H]
        z4 = y4[:, 3, 0:H]
        xd = y4[:, 3, :]
        yb = y4[:, 1, :]
        yc = y4[:, 2, :]
        bn6 = sb("bn6", [P, SLOTS, 6])
        mv = sb("mv", [P, SLOTS, 2])
        xT = sb("xT", [P, D])
        zT = sb("zT", [P, D])
        junk_sq = sb("junk_sq", [P, SLOTS, D], BF16)

        x_rows = x.rearrange("(t p) f -> p t f", p=P)
        adj_rows = adj.rearrange("(t p) n -> t p n", p=P)
        out_rows = out.rearrange("(t p) f -> t p f", p=P)

        def zp_view(stage):
            w = WZ if stage == MOB else (D if stage == "inc" else WIDTH[stage])
            return ZP[:, 0:T * 2 * w].rearrange("p (t h f) -> p t h f", h=2, f=w)

        block = ctx.enter_context(nc.Block())

        @block.sync
        def _(sp):
            sp.dma_start(X[:, :, :], x_rows).then_inc(sem("x_in"), 16)

            def load_rows(t, b):
                sp.dma_start(RAW[:, b, :], adj_rows[t]).then_inc(sem(f"raw_in{b}"), 16)

            load_rows(0, 0)
            load_rows(1, 1)
            for dst, src in ((wmob_sb[:, :, :], w_mob.rearrange("(c p) f -> p c f", p=P)),
                             (w1_sb[:, :, :], w1.rearrange("(c p) f -> p c f", p=P)),
                             (w2_sb[:, :], w2), (w3_sb[:, :], w3), (w4_sb[:, :], w4), (w5_sb[:, :], w5),
                             (w6_sb[:, :], w6), (wnorm_sb[:, :, :], w_norm_t.rearrange("(c p) f -> p c f", p=P)),
                             (b_sb[:, :], b_rows)):
                sp.dma_start(dst, src).then_inc(sem("weights_in"), 16)

            def store_tile(t):
                for g in range(NG):
                    sp.wait_ge(sem(f"split_done{g % 2}"), 2 * t + g // 2 + 1)
                    sp.dma_start(pairs_dram[t, :, g * GK * 2 * P:(g + 1) * GK * 2 * P],
                                 PAIR[:, g, :, :, :].rearrange("p k h i -> p (k h i)")).then_inc(
                                     sem(f"pairs_stored{g}"), 16)

            with sp.Fori(0, T // 2 - 1) as i:
                for b in range(2):
                    t = 2 * i + b
                    store_tile(t)
                    load_rows(t + 2, b)
            store_tile(T - 2)
            store_tile(T - 1)

            sp.wait_ge(sem(f"group_used{NG - 1}"), T)
            for g in range(NG):
                sp.wait_ge(sem(f"pairs_stored{g}"), 16 * T)

            def load_pairs(t, s):
                sp.dma_start(SLOT[:, s, :, :, :].rearrange("p k h i -> p (k h i)"), pairs_dram[t]).then_inc(
                    sem(f"slot_in{s}"), 16)

            for stage in range(8):
                for s in range(SLOTS):
                    if stage > 0:
                        sp.wait_ge(*at("agg_done", stage - 1, T - SLOTS + s + 1))
                    load_pairs(s, s)
                with sp.Fori(1, GROUPS) as g:
                    for s in range(SLOTS):
                        sp.wait_ge(*at("agg_done", stage, SLOTS * g + s + 1 - SLOTS))
                        load_pairs(SLOTS * g + s, s)

        @block.tensor
        def _(pe):
            def turn(dst, src):
                return pe.transpose(dst, src, ident[:, :])

            def scale_steps(stage):
                pe.wait_ge(*at("z_max_ready", stage, 1))
                turn(bank[0:1, 3, 0:P], z_max[:, :]).then_inc(sem("z_max_turned"), 1)
                pe.wait_ge(*at("z_pair_ready", stage, 1))
                pe.matmul(bank[:, 3, 256:258], ones[:, :], z_pair[:, :], start=True, stop=True).then_inc(
                    sem("z_pair_sent"), 1)

            pe.wait_ge(sem("ident_ready"), 2)
            scale_steps("inc")
            zp0 = zp_view("inc")

            def turn_group(t, g, b):
                u = g % 2
                if g == 0:
                    pe.wait_ge(sem("scaled"), t + 1)
                pe.wait_ge(sem(f"split_done{u}"), 2 * t + g // 2)
                for kk in range(GK):
                    k = g * GK + kk
                    mm = turn(bank[:, 2 * u + kk // 4, (kk % 4) * P:(kk % 4 + 1) * P], RAW[:, b, k * P:(k + 1) * P])
                mm.then_inc(sem("turned"), 1)

            def multiply_group(t, g, fresh=False):
                pe.wait_ge(sem(f"split_done{g % 2}"), 2 * t + g // 2 + 1)
                if g == 0:
                    pe.wait_ge(*at("acc_read", "inc", t))
                for kk in range(GK):
                    k = g * GK + kk
                    if fresh and k % 4 == 0:
                        pe.wait_ge(*at("z_low_done", "inc", k // 4 + 1))
                    a, z = k == 0, k == K - 1
                    pe.matmul(bank[:, 4, 0:D], PAIR[:, g, kk, 0, :], zp0[:, k, 0, :], start=a, stop=False)
                    pe.matmul(bank[:, 4, 0:D], PAIR[:, g, kk, 0, :], zp0[:, k, 1, :], start=False, stop=False)
                    pe.matmul(bank[:, 4, 0:D], PAIR[:, g, kk, 1, :], zp0[:, k, 0, :], start=False, stop=z)
                    pe.matmul(bank[:, 5, 0:D], MASK[:, g, kk, :], zp0[:, k, 0, :], start=a, stop=False)
                    mm = pe.matmul(bank[:, 5, 0:D], MASK[:, g, kk, :], zp0[:, k, 1, :], start=False, stop=z)
                mm.then_inc(sem(f"group_used{g}"), 1)

            def turn_x(stage, t, src, b=6):
                pe.wait_ge(*at("xs_ready", stage, t + 1))
                pe.wait_ge(*at("xT_ready", stage, t))
                for c in range(D // P):
                    mm = turn(bank[:, b, c * P:(c + 1) * P], src[:, c * P:(c + 1) * P])
                mm.then_inc(sem("xs_turned"), 1)

            def product_x(stage, t, src, w, width, b=7):
                pe.wait_ge(*at("xT_ready", stage, t + 1))
                pe.wait_ge(*at("prod_read", stage, t))
                for c in range(D // P):
                    mm = pe.matmul(bank[:, b, 0:width], src[:, c * P:(c + 1) * P], w[:, c, :],
                                   start=c == 0, stop=c == D // P - 1)
                mm.then_inc(sem("prod_ready"), 1)

            def tile0(t, b, first=False, last=False):
                for g in range(NG):
                    if g < NG - 1:
                        turn_group(t, g + 1, b)
                    elif not last:
                        turn_group(t + 1, 0, 1 - b)
                    multiply_group(t, g, fresh=first)
                    if g == 1 and not first:
                        turn_x("inc", t - 1, xs)
                    if g == 2 and not first:
                        product_x("inc", t - 1, xT, wmob_sb, D)

            turn_group(0, 0, 0)
            tile0(0, 0, first=True)
            pe.wait_ge(sem("weights_in"), 16 * 9)
            tile0(1, 1)
            with pe.Fori(1, T // 2 - 1) as i:
                for b in range(2):
                    tile0(2 * i + b, b)
            tile0(T - 2, 0)
            tile0(T - 1, 1, last=True)
            turn_x("inc", T - 1, xs)
            product_x("inc", T - 1, xT, wmob_sb, D)

            def small_turn(stage, t, w):
                pe.wait_ge(*at("acc_read", stage, t + 1))
                pe.wait_ge(*at("rT_ready", stage, t))
                pe.sem_inc(sem("pe_marks"), 1)
                turn(bank[0:w, 6, 0:P], r[:, 0:w]).then_inc(sem("r_turned"), 1)

            def small_product(stage, t, w, weights, wo):
                pe.wait_ge(*at("rT_ready", stage, t + 1))
                pe.wait_ge(*at("small_read", stage, t))
                pe.matmul(bank[:, 7, 0:wo], xT[0:w, 0:P], weights, start=True, stop=True).then_inc(
                    sem("small_ready"), 1)

            def turn_z4(stage, t):
                pe.wait_ge(*at("small_read", stage, t + 1))
                pe.wait_ge(*at("zT_ready", stage, t))
                turn(bank[:, 4, 0:P], z4[:, :]).then_inc(sem("z_turned"), 1)

            def product_z4(stage, t):
                pe.wait_ge(*at("zT_ready", stage, t + 1))
                pe.wait_ge(*at("prod_read", stage, t))
                pe.matmul(bank[:, 5, 0:H], zT[:, 0:P], w5_sb[:, :], start=True, stop=True).then_inc(
                    sem("prod_ready"), 1)

            def after(stage, t):
                if stage in (G1, G2):
                    weights, wo = (w2_sb[:, :], H) if stage == G1 else (w3_sb[:, :], H2)
                    return [(8, lambda: small_turn(stage, t, H)),
                            (16, lambda: small_product(stage, t, H, weights, wo))]
                if stage == G4:
                    return [(6, lambda: small_turn(stage, t, H2)),
                            (13, lambda: small_product(stage, t, H2, w4_sb[:, :], H)),
                            (20, lambda: turn_z4(stage, t)), (27, lambda: product_z4(stage, t))]
                if stage == G6:
                    return [(6, lambda: small_turn(stage, t, H)),
                            (12, lambda: small_product(stage, t, H, w6_sb[:, :], D)),
                            (25, lambda: turn_x(stage, t, xd, 4)),
                            (30, lambda: product_x(stage, t, zT, wnorm_sb, D, 5))]
                return []

            def after_group(g):
                steps = []
                for s in range(SLOTS):
                    t = SLOTS * g + s
                    steps.append((8 * s + 2, lambda t=t, s=s: turn_x(MOB, t, xs4[:, s, :])))
                    steps.append((8 * s + 6, lambda t=t: product_x(MOB, t, xT, w1_sb, H)))
                return steps

            def aggregate(stage, g, s, steps, fresh=False):
                t = SLOTS * g + s
                w = WIDTH[stage]
                zp = zp_view(stage)
                pe.wait_ge(sem(f"slot_in{s}"), 16 * (GROUPS * stage) + 16 * (g + 1))
                if stage == MOB:
                    acc = bank[:, s, 0:D + 1]
                    if not isinstance(g, int):
                        pe.wait_ge(*at("acc_read", stage, t + 1 - SLOTS))
                else:
                    acc = bank[:, s % 2, :]
                    if not (isinstance(g, int) and s < 2):
                        pe.wait_ge(*at("acc_read", stage, t - 1))
                for k in range(K):
                    for when, step in steps:
                        if when == k:
                            step()
                    if fresh and (stage == MOB or k % 4 == 0):
                        pe.wait_ge(*at("z_low_done", stage, (k if stage == MOB else k // 4) + 1))
                    a, z = k == 0, k == K - 1
                    high, low = SLOT[:, s, k, 0, :], SLOT[:, s, k, 1, :]
                    if stage in (MOB, NORM):
                        n = D + 1 if stage == MOB else D
                        pe.matmul(acc[:, 0:n], high, zp[:, k, 0, 0:n], start=a, stop=False)
                        pe.matmul(acc[:, 0:n], high, zp[:, k, 1, 0:n], start=False, stop=False)
                        mm = pe.matmul(acc[:, 0:n], low, zp[:, k, 0, 0:n], start=False, stop=z)
                    else:
                        pe.matmul(acc[:, 0:2 * w], high, zp[:, k, :, :].rearrange("p h f -> p (h f)"),
                                  start=a, stop=False, skip_group_check=True)
                        mm = pe.matmul(acc[:, w:2 * w], low, zp[:, k, 0, :], start=False, stop=z,
                                       skip_group_check=True)
                mm.then_inc(sem("agg_done"), 1)

            def group(stage, g, first):
                for s in range(SLOTS):
                    if stage == MOB:
                        steps = after_group(g - 1) if s == SLOTS - 1 and not first else []
                    else:
                        steps = after(stage, SLOTS * g + s - 1) if not (first and s == 0) else []
                    aggregate(stage, g, s, steps, fresh=first and s == 0)

            for stage in range(8):
                scale_steps(stage)
                group(stage, 0, True)
                with pe.Fori(1, GROUPS) as g:
                    group(stage, g, False)
                for _, step in (after_group(GROUPS - 1) if stage == MOB else after(stage, T - 1)):
                    step()

        @block.gpsimd
        def _(pool):
            nc.gpsimd.memset(ident[:, :], 0.0).then_inc(sem("ident_zero"), 1)
            nc.gpsimd.memset(ones[:, :], 1.0).then_inc(sem("ident_ready"), 1)
            pool.wait_ge(sem("ident_zero"), 1)
            nc.gpsimd.affine_select(out=ident[:, :], in_=ident[:, :], compare_op=ALU.not_equal, fill=1.0,
                                    base=0, pattern=[[-1, P]], channel_multiplier=1).then_inc(sem("ident_ready"), 1)
            with pool.Fori(0, T) as t:
                pool.wait_ge(*at("xs_ready", "inc", t + 1))
                nc.gpsimd.tensor_copy(X[:, t, :], xs).then_inc(sem("x_kept"), 1)
            with pool.Fori(0, GROUPS) as g:
                pool.wait_ge(*at("xs_ready", MOB, SLOTS * g + SLOTS))
                nc.gpsimd.tensor_copy(X[:, bass.ds(SLOTS * g, SLOTS), :], xs4[:, :, :]).then_inc(
                    sem("x_kept"), 1)
            with pool.Fori(0, T) as t:
                pool.wait_ge(*at("rows_ready", G6, t + 1))
                nc.gpsimd.tensor_copy(X[:, t, :], xs).then_inc(sem("x_kept"), 1)

        @block.scalar
        def _(act):
            def A(*args, **kw):
                return nc.scalar.activation(*args, **kw)

            def A_at(*args, **kw):
                act.sem_inc(sem("act_marks"), 1)
                return A(*args, **kw)

            def split_high(stage, src):
                zp = zp_view(stage)
                w = zp.shape[3]
                act.wait_ge(*at("z_scale_ready", stage, 1))
                for c in range(CHUNKS):
                    A(zp[:, 4 * c:4 * c + 4, 0, :], src[:, 4 * c:4 * c + 4, 0:w], ACT.Copy,
                      scale=z_scale[:, 0:1]).then_inc(sem("z_high_done"), 1)

            def abs_rows(t, i, b):
                act.wait_ge(sem(f"raw_in{b}"), 16 * i + 16)
                A_at(junk_abs, RAW[:, b, :], ACT.Abs, accum_out=abs_sum[:, bass.ds(t, 1)]).then_inc(sem("abs_summed"), 1)

            def scale_rows(t, b):
                act.wait_ge(sem("row_scale_ready"), t + 1)
                A_at(RAW[:, b, :], RAW[:, b, :], ACT.Copy, scale=row_scale[:, bass.ds(t, 1)],
                  accum_out=row_sum[:, bass.ds(t, 1)]).then_inc(sem("scaled"), 1)
                A_at(root_count[:, bass.ds(t, 1)], count[:, bass.ds(t, 1)], ACT.Sqrt).then_inc(sem("count_rooted"), 1)

            def high_group(t, g):
                act.wait_ge(sem("turned"), NG * t + g + 1)
                act.wait_ge(sem(f"group_used{g}"), t)
                act.wait_ge(sem(f"pairs_stored{g}"), 16 * t)
                A(PAIR[:, g, :, 0, :], bank[:, 2 * (g % 2):2 * (g % 2) + 2, :].rearrange("p b (k i) -> p (b k) i", i=P),
                  ACT.Copy).then_inc(sem("high_done"), 1)

            def root_var(stage, t, n=1):
                act.wait_ge(*at("var_ready", stage, t + 1))
                A(stat[:, 1:2], stat[:, 0:1], ACT.Sqrt).then_inc(sem("dev_ready"), 1)

            def keep_xT(stage, t, dst, b):
                act.wait_ge(*at("xs_turned", stage, t + 1))
                act.wait_ge(*at("prod_ready", stage, t))
                A(dst[:, :], bank[:, b, 0:D], ACT.Copy).then_inc(sem("xT_ready"), 1)

            def squares(t):
                act.wait_ge(*at("xs_ready", "inc", t + 1))
                A_at(junk_sq[:, 0, :], xs, ACT.Square, accum_out=x_sq[:, bass.ds(t, 1)]).then_inc(sem("x_squared"), 1)

            def keep_product(t):
                act.wait_ge(*at("prod_ready", "inc", t + 1))
                A_at(junk_sq[:, 1, :], bank[:, 7, 0:D], ACT.Square, accum_out=m_sq[:, bass.ds(t, 1)]).then_inc(sem("m_squared"), 1)
                A_at(Z[:, t, 0:D], bank[:, 7, 0:D], ACT.Copy).then_inc(sem("prod_read"), 1)

            act.wait_ge(sem("x_in"), 16)
            abs_rows(0, 0, 0)
            split_high("inc", X)
            scale_rows(0, 0)

            def tile0(i, b, first=False, last=False):
                t = 2 * i + b
                high_group(t, 0)
                if not last:
                    abs_rows(t + 1, i + b, 1 - b)
                high_group(t, 1)
                if not first:
                    root_var("inc", t - 1)
                high_group(t, 2)
                if not first:
                    squares(t - 1)
                    keep_xT("inc", t - 1, xT, 6)
                if not last:
                    scale_rows(t + 1, 1 - b)
                high_group(t, 3)
                if not first:
                    keep_product(t - 1)

            tile0(0, 0, first=True)
            tile0(0, 1)
            with act.Fori(1, T // 2 - 1) as i:
                for b in range(2):
                    tile0(i, b)
            tile0(T // 2 - 1, 0)
            tile0(T // 2 - 1, 1, last=True)
            root_var("inc", T - 1)
            squares(T - 1)
            keep_xT("inc", T - 1, xT, 6)
            keep_product(T - 1)

            act.wait_ge(sem("factor_in1"), 1)
            A(roots[:, :, :], roots_in[:, :, :], ACT.Sqrt).then_inc(sem("factor_out1"), 1)
            act.wait_ge(sem("factor_in2"), 1)
            A(bt[:, 1, :], bt[:, 0, :], ACT.Ln).then_inc(sem("factor_out2"), 1)
            act.wait_ge(sem("factor_in3"), 1)
            A(bt[:, 1, :], bt[:, 0, :], ACT.Tanh).then_inc(sem("factor_out3"), 1)

            zp = zp_view(MOB)
            act.wait_ge(*at("z_scale_ready", MOB, 1))
            A(zp[:, :, 0, D], gamma1[:, :], ACT.Copy, scale=z_scale[:, 0:1]).then_inc(sem("z_high_done"), 1)
            with act.Fori(0, T) as t:
                A_at(zp[:, t, 0, 0:D], Z[:, t, 0:D], ACT.Copy, scale=z_factor[:, bass.ds(t, 1)]).then_inc(
                    sem("z_high_done"), 1)

            with act.Fori(0, GROUPS) as g:
                act.wait_ge(sem("mob_in1"), g + 1)
                for s in range(SLOTS):
                    last = A_at(junk_sq[:, s, :], Z[:, SLOTS * g + s, 0:D], ACT.Square, scale=gt[:, 0, s:s + 1],
                             accum_out=gt[:, 1, s:s + 1])
                last.then_inc(sem("mob_out1"), 1)
                act.wait_ge(sem("mob_in2"), g + 1)
                A(gt[:, 4:6, :], gt[:, 2:4, :], ACT.Sqrt).then_inc(sem("mob_out2"), 1)
                act.wait_ge(sem("mob_in3"), g + 1)
                A(gt[:, 11, :], gt[:, 10, :], ACT.Ln).then_inc(sem("mob_out3"), 1)
                act.wait_ge(sem("mob_in4"), g + 1)
                A(gt[:, 11, :], gt[:, 10, :], ACT.Tanh).then_inc(sem("mob_out4"), 1)
                act.wait_ge(sem("mob_in5"), g + 1)
                A(gt[:, 11, :], gt[:, 10, :], ACT.Ln).then_inc(sem("mob_out5"), 1)
                act.wait_ge(sem("mob_in6"), g + 1)
                for s in range(SLOTS):
                    last = A_at(Z[:, SLOTS * g + s, 0:D], Z[:, SLOTS * g + s, 0:D], ACT.Relu, scale=gt[:, 12, s:s + 1])
                last.then_inc(sem("mob_relu"), 1)
                act.wait_ge(sem("mob_relu"), g + 1)
                for s in range(SLOTS):
                    last = A_at(junk_sq[:, s, :], Z[:, SLOTS * g + s, 0:D], ACT.Square, accum_out=gt[:, 1, s:s + 1])
                last.then_inc(sem("mob_out6"), 1)
                act.wait_ge(sem("mob_in7"), g + 1)
                A(gt[:, 11, :], gt[:, 10, :], ACT.Sqrt).then_inc(sem("mob_out7"), 1)
                act.wait_ge(sem("mob_out7"), g + 1)
                A(gt[:, 10, :], gt[:, 11, :], ACT.Tanh).then_inc(sem("mob_out8"), 1)
                act.wait_ge(sem("mob_in8"), g + 1)
                A(gt[:, 14, :], gt[:, 13, :], ACT.Sqrt).then_inc(sem("mob_out9"), 1)
                for s in range(SLOTS):
                    keep_xT(MOB, SLOTS * g + s, xT, 6)

            def keep_half(stage, t, b):
                w = WIDTH[stage]
                act.wait_ge(*at("agg_done", stage, t + 1))
                act.wait_ge(*at("acc_read", stage, t))
                A_at(half[:, 0:w], bank[:, b, w:2 * w], ACT.Copy, scale=unscale[:, bass.ds(t, 1)]).then_inc(
                    sem("half_ready"), 1)

            def keep_rT(stage, t, func):
                w = WIDTH[stage]
                act.wait_ge(*at("r_turned", stage, t + 1))
                A(xT[0:w, 0:P], bank[0:w, 6, 0:P], func).then_inc(sem("rT_ready"), 1)

            for stage in (G1, G2, G3, G4, G5, G6):
                split_high(stage, Z)
                with act.Fori(0, T // 2) as i:
                    for b in range(2):
                        t = 2 * i + b
                        keep_half(stage, t, b)
                        if stage in (G1, G2):
                            keep_rT(stage, t, ACT.Relu)
                        if stage in (G4, G6):
                            keep_rT(stage, t, ACT.Copy)
                        if stage == G4:
                            act.wait_ge(*at("z_turned", stage, t + 1))
                            act.wait_ge(*at("prod_ready", stage, t))
                            A(zT[:, 0:P], bank[:, 4, 0:P], ACT.Copy).then_inc(sem("zT_ready"), 1)
                        if stage == G6:
                            root_var(stage, t)
                            keep_xT(stage, t, zT, 4)

            split_high(NORM, Z)
            with act.Fori(0, T // 2) as i:
                for b in range(2):
                    t = 2 * i + b
                    root_var(NORM, t)
                    act.wait_ge(*at("xs_ready", NORM, t + 1))
                    act.dma_start(out_rows[t], xs4[:, b, :]).then_inc(sem(f"out_done{b}"), 16)
            for b in range(2):
                act.wait_ge(sem(f"out_done{b}"), 16 * (T // 2))

        @block.vector
        def _(dve):
            V = nc.vector

            def scales(stage, link, bounds, two_axes=False):
                V.tensor_reduce(z_max[:, :], bounds, AX.XY if two_axes else AX.X, ALU.max,
                                apply_absolute_value=True).then_inc(sem("z_max_ready"), 1)
                dve.wait_ge(*at("z_max_turned", stage, 1))
                link(V.tensor_reduce(z_top[:, 0:1], bank[0:1, 3, 0:P], AX.X, ALU.max))
                link(V.tensor_scalar(z_top[:, 1:2], z_top[:, 0:1], TINY, None, ALU.max))
                link(V.tensor_scalar(z_top[:, 2:3].bitcast(I32), z_top[:, 1:2].bitcast(I32), EXPONENT, None,
                                     ALU.bitwise_and))
                link(V.reciprocal(z_top[:, 3:4], z_top[:, 2:3]))
                V.tensor_scalar(z_pair[:, 0:1], z_top[:, 3:4], TOP, None, ALU.mult)
                V.tensor_scalar(z_pair[:, 1:2], z_top[:, 2:3], 1.0 / TOP, None, ALU.mult).then_inc(
                    sem("z_pair_ready"), 1)
                dve.wait_ge(*at("z_pair_sent", stage, 1))
                V.tensor_copy(z_scale[:, :], bank[:, 3, 256:258]).then_inc(sem("z_scale_ready"), 1)
                if stage != "inc":
                    dve.wait_ge(*at("z_scale_ready", stage, 1))
                    link(V.tensor_scalar(unscale[:, :], row_inv[:, :], z_scale[:, 1:2], None, ALU.mult))

            def split_low(stage, src):
                zp = zp_view(stage)
                w = zp.shape[3]
                for c in range(CHUNKS):
                    for_c = slice(4 * c, 4 * c + 4)
                    dve.wait_ge(*at("z_high_done", stage, c + 1))
                    V.scalar_tensor_tensor(zp[:, for_c, 1, :], src[:, for_c, 0:w], z_scale[:, 0:1],
                                           zp[:, for_c, 0, :], ALU.mult, ALU.subtract).then_inc(
                                               sem("z_low_done"), 1)

            def mean_var(link, src, n=0):
                link(V.bn_stats(bn6[:, n, :], src))
                dve.sem_inc(sem("dve_marks"), 1)
                link(V.bn_aggr(mv[:, n, :], bn6[:, n, :]))

            def norm_ready(stage, link, src):
                mean_var(link, src)
                V.tensor_scalar(stat[:, 0:1], mv[:, 0, 1:2], LN_EPS, None, ALU.add).then_inc(sem("var_ready"), 1)

            def norm_rows(stage, link, t, dst, src, ready):
                dve.wait_ge(*at("dev_ready", stage, t + 1))
                link(V.reciprocal(stat[:, 2:3], stat[:, 1:2]))
                V.tensor_scalar(dst, src, mv[:, 0, 0:1], stat[:, 2:3], ALU.subtract, ALU.mult).then_inc(
                    sem(ready), 1)

            start = Chain(dve, sem("dve_start"))
            dve.wait_ge(sem("x_in"), 16)
            scales("inc", start, X[:, :, :], two_axes=True)

            def count_rows(t, i, b):
                dve.wait_ge(sem(f"raw_in{b}"), 16 * i + 16)
                V.tensor_scalar(junk_count, RAW[:, b, :], 0.0, None, ALU.is_gt, ALU.add,
                                accum_out=count[:, bass.ds(t, 1)])

            def scale_of_rows(t, link):
                dve.wait_ge(sem("abs_summed"), t + 1)
                link(V.tensor_scalar(stat[:, 4:5], abs_sum[:, bass.ds(t, 1)], 1.0, None, ALU.add))
                link(V.tensor_scalar(stat[:, 5:6].bitcast(I32), stat[:, 4:5].bitcast(I32), EXPONENT, None,
                                     ALU.bitwise_and))
                link(V.reciprocal(stat[:, 6:7], stat[:, 5:6]))
                V.tensor_scalar(row_inv[:, bass.ds(t, 1)], stat[:, 5:6], 1.0 / TOP, None, ALU.mult)
                V.tensor_scalar(row_scale[:, bass.ds(t, 1)], stat[:, 6:7], TOP, None, ALU.mult).then_inc(
                    sem("row_scale_ready"), 1)

            def low_group(t, g):
                turned = bank[:, 2 * (g % 2):2 * (g % 2) + 2, :].rearrange("p b (k i) -> p (b k) i", i=P)
                dve.wait_ge(sem("high_done"), NG * t + g + 1)
                V.tensor_scalar(MASK[:, g, :, :], turned, 0.0, None, ALU.is_gt)
                V.tensor_tensor(PAIR[:, g, :, 1, :], turned, PAIR[:, g, :, 0, :], ALU.subtract).then_inc(
                    sem(f"split_done{g % 2}"), 1)

            def edge_factors(t, link):
                one = bass.ds(t, 1)
                dve.wait_ge(sem("count_rooted"), t + 1)
                link(V.tensor_scalar(stat[:, 8:9], root_count[:, one], NORM_EPS, None, ALU.max))
                link(V.reciprocal(stat[:, 9:10], stat[:, 8:9]))
                link(V.tensor_tensor(row_sum[:, one], row_sum[:, one], row_inv[:, one], ALU.mult))
                link(V.scalar_tensor_tensor(stat[:, 10:11], count[:, one], stat[:, 9:10], row_sum[:, one],
                                            ALU.mult, ALU.add))
                link(V.reciprocal(stat[:, 11:12], stat[:, 10:11]))
                V.tensor_scalar(stat[:, 12:13], row_inv[:, one], z_scale[:, 1:2], stat[:, 11:12], ALU.mult, ALU.mult)
                link(V.tensor_scalar(stat[:, 13:14], stat[:, 9:10], z_scale[:, 1:2], stat[:, 11:12], ALU.mult,
                                     ALU.mult))

            def read_sums(t, link):
                dve.wait_ge(sem(f"group_used{NG - 1}"), t + 1)
                link(V.scalar_tensor_tensor(yb, bank[:, 4, 0:D], stat[:, 12:13], X[:, t, :], ALU.mult, ALU.add))
                V.scalar_tensor_tensor(y, bank[:, 5, 0:D], stat[:, 13:14], yb, ALU.mult, ALU.add).then_inc(
                    sem("acc_read"), 1)
                dve.wait_ge(*at("acc_read", "inc", t + 1))
                norm_ready("inc", link, y)

            def finish_rows(t, link):
                dve.wait_ge(*at("xs_turned", "inc", t))
                dve.wait_ge(sem("x_squared"), t)
                dve.wait_ge(*at("x_kept", "inc", t))
                norm_rows("inc", link, t, xs, y, "xs_ready")

            READ, ROWS, EDGE = 4, 3, 6

            def read_chain(t, n=0):
                return Chain(dve, sem("dve_read"), READ * t + n)

            count_rows(0, 0, 0)
            scale_of_rows(0, Chain(dve, sem("dve_rows")))
            split_low("inc", X)

            def tile0(i, b, first=False, last=False):
                t = 2 * i + b
                low_group(t, 0)
                if not first:
                    read_sums(t - 1, read_chain(t - 1))
                low_group(t, 1)
                if not first:
                    finish_rows(t - 1, read_chain(t - 1, READ - 1))
                if not last:
                    count_rows(t + 1, i + b, 1 - b)
                low_group(t, 2)
                if not last:
                    scale_of_rows(t + 1, Chain(dve, sem("dve_rows"), ROWS * t + ROWS))
                low_group(t, 3)
                edge_factors(t, Chain(dve, sem("dve_edge"), EDGE * t))

            tile0(0, 0, first=True)
            tile0(0, 1)
            with dve.Fori(1, T // 2 - 1) as i:
                for b in range(2):
                    tile0(i, b)
            tile0(T // 2 - 1, 0)
            tile0(T // 2 - 1, 1, last=True)
            read_sums(T - 1, read_chain(T - 1))
            finish_rows(T - 1, read_chain(T - 1, READ - 1))

            link = Chain(dve, sem("dve_factors"))

            def magnitude(dst, src):
                return V.scalar_tensor_tensor(dst, src, -1.0, src, ALU.mult, ALU.max)

            def artanh_in(link, w, u, c, t0, t1):
                link(V.tensor_scalar(t0, c, -1.0, 1.0, ALU.mult, ALU.add))
                link(V.reciprocal(t1, t0))
                link(V.scalar_tensor_tensor(u, c, 2.0, t1, ALU.mult, ALU.mult))
                return V.tensor_scalar(w, u, 1.0, None, ALU.add)

            def artanh_out(link, dst, log_w, w, u, c, t0, t1):
                link(V.tensor_scalar(t0, w, -1.0, 1e-30, ALU.add, ALU.max))
                link(V.reciprocal(t1, t0))
                link(V.tensor_tensor(t0, u, t1, ALU.mult))
                link(V.scalar_tensor_tensor(t1, log_w, 0.5, t0, ALU.mult, ALU.mult))
                link(V.tensor_tensor(dst, t1, c, ALU.max))

            dve.wait_ge(sem("x_squared"), T)
            dve.wait_ge(sem("m_squared"), T)
            V.tensor_scalar(roots_in[:, 0, :], x_sq[:, :], EPS * EPS, None, ALU.max)
            V.tensor_scalar(roots_in[:, 1, :], m_sq[:, :], EPS * EPS, None, ALU.max)
            link(V.tensor_scalar(bt[:, 9, :], row_sum[:, :], 1.0, None, ALU.add))
            V.tensor_scalar(roots_in[:, 2, :], bt[:, 9, :], 1e-30, None, ALU.max).then_inc(sem("factor_in1"), 1)
            dve.wait_ge(sem("factor_out1"), 1)
            xn, mn, dn = roots[:, 0, :], roots[:, 1, :], roots[:, 2, :]
            link(V.tensor_scalar(bt[:, 2, :], xn, CLIP, None, ALU.min))
            artanh_in(link, bt[:, 0, :], bt[:, 3, :], bt[:, 2, :], bt[:, 4, :], bt[:, 5, :]).then_inc(
                sem("factor_in2"), 1)
            dve.wait_ge(sem("factor_out2"), 1)
            artanh_out(link, bt[:, 6, :], bt[:, 1, :], bt[:, 0, :], bt[:, 3, :], bt[:, 2, :], bt[:, 4, :], bt[:, 5, :])
            link(V.reciprocal(bt[:, 4, :], xn))
            link(V.tensor_tensor(bt[:, 5, :], mn, bt[:, 4, :], ALU.mult))
            V.tensor_tensor(bt[:, 0, :], bt[:, 5, :], bt[:, 6, :], ALU.mult).then_inc(sem("factor_in3"), 1)
            dve.wait_ge(sem("factor_out3"), 1)
            link(V.reciprocal(bt[:, 4, :], mn))
            link(V.tensor_tensor(bt[:, 5, :], bt[:, 1, :], bt[:, 4, :], ALU.mult))
            link(V.scalar_tensor_tensor(bt[:, 6, :], mn, EPS, bt[:, 5, :], ALU.is_gt, ALU.mult))
            link(V.tensor_tensor(bt[:, 4, :], bt[:, 6, :], bt[:, 6, :], ALU.mult))
            link(V.tensor_tensor(bt[:, 5, :], bt[:, 4, :], m_sq[:, :], ALU.mult))
            link(V.tensor_scalar(bt[:, 4, :], bt[:, 5, :], -1.0, 1.0, ALU.mult, ALU.add))
            link(V.reciprocal(bt[:, 5, :], bt[:, 4, :]))
            link(V.tensor_scalar(bt[:, 7, :], bt[:, 5, :], 2.0, 1e-15, ALU.mult, ALU.max))
            link(V.tensor_scalar(gamma1[:, :], bt[:, 7, :], -1.0, None, ALU.add))
            link(V.tensor_tensor(bt[:, 8, :], bt[:, 7, :], bt[:, 6, :], ALU.mult))
            link(V.tensor_tensor(bt[:, 4, :], bt[:, 8, :], mn, ALU.mult))
            link(magnitude(bt[:, 5, :], bt[:, 4, :]))
            link(magnitude(bt[:, 3, :], gamma1[:, :]))
            link(V.tensor_tensor(z_bound[:, :], bt[:, 5, :], bt[:, 3, :], ALU.max))
            link(V.reciprocal(bt[:, 2, :], dn))
            link(V.scalar_tensor_tensor(deg_root[:, :], bt[:, 9, :], 0.0, bt[:, 2, :], ALU.is_gt, ALU.mult))

            V.tensor_reduce(z_max[:, :], z_bound[:, :], AX.X, ALU.max).then_inc(sem("z_max_ready"), 1)
            dve.wait_ge(*at("z_max_turned", MOB, 1))
            link(V.tensor_reduce(z_top[:, 0:1], bank[0:1, 3, 0:P], AX.X, ALU.max))
            link(V.tensor_scalar(z_top[:, 1:2], z_top[:, 0:1], TINY, None, ALU.max))
            link(V.tensor_scalar(z_top[:, 2:3].bitcast(I32), z_top[:, 1:2].bitcast(I32), EXPONENT, None,
                                 ALU.bitwise_and))
            link(V.reciprocal(z_top[:, 3:4], z_top[:, 2:3]))
            V.tensor_scalar(z_pair[:, 0:1], z_top[:, 3:4], TOP, None, ALU.mult)
            V.tensor_scalar(z_pair[:, 1:2], z_top[:, 2:3], 1.0 / TOP, None, ALU.mult).then_inc(
                sem("z_pair_ready"), 1)
            dve.wait_ge(*at("z_pair_sent", MOB, 1))
            link(V.tensor_copy(z_scale[:, :], bank[:, 3, 256:258]))
            link(V.tensor_scalar(unscale[:, :], row_inv[:, :], z_scale[:, 1:2], None, ALU.mult))
            V.tensor_scalar(z_factor[:, :], bt[:, 8, :], z_scale[:, 0:1], None, ALU.mult).then_inc(
                sem("z_scale_ready"), 1)
            dve.wait_ge(*at("z_scale_ready", MOB, 1))
            zp = zp_view(MOB)
            dve.wait_ge(*at("z_high_done", MOB, 1))
            V.scalar_tensor_tensor(zp[:, :, 1, D], gamma1[:, :], z_scale[:, 0:1], zp[:, :, 0, D], ALU.mult,
                                   ALU.subtract)
            with dve.Fori(0, T) as t:
                dve.wait_ge(*at("z_high_done", MOB, t + 2))
                V.scalar_tensor_tensor(zp[:, t, 1, 0:D], Z[:, t, 0:D], z_factor[:, bass.ds(t, 1)],
                                       zp[:, t, 0, 0:D], ALU.mult, ALU.subtract).then_inc(
                                           sem("z_low_done"), 1)

            MOB_STEPS = 54

            def row(n):
                return gt[:, n, :]

            with dve.Fori(0, GROUPS) as g:
                link = Chain(dve, sem("dve_mob"), MOB_STEPS * g)
                rows = bass.ds(SLOTS * g, SLOTS)
                for s in range(SLOTS):
                    t = SLOTS * g + s
                    dve.wait_ge(*at("agg_done", MOB, t + 1))
                    V.tensor_scalar(Z[:, t, 0:D + 1], bank[:, s, 0:D + 1], 1.0, None, ALU.mult).then_inc(sem("acc_read"), 1)
                dve.wait_ge(*at("acc_read", MOB, SLOTS * g + SLOTS))
                link(V.tensor_tensor(row(15), Z[:, rows, D], unscale[:, rows], ALU.mult))
                link(V.tensor_scalar(row(16), row(15), 0.0, 2.0, ALU.is_ge, ALU.mult))
                link(V.tensor_scalar(row(17), row(16), -1.0, None, ALU.add))
                link(magnitude(row(18), row(15)))
                link(V.tensor_scalar(row(16), row(18), EPS, None, ALU.max))
                link(V.tensor_tensor(row(15), row(16), row(17), ALU.mult))
                link(V.reciprocal(row(16), row(15)))
                V.tensor_tensor(row(0), row(16), unscale[:, rows], ALU.mult).then_inc(sem("mob_in1"), 1)
                dve.wait_ge(sem("mob_out1"), g + 1)
                link(V.tensor_scalar(row(15), row(1), -1.0, 1.0, ALU.mult, ALU.add))
                V.tensor_scalar(row(2), row(15), EPS, None, ALU.max)
                V.tensor_scalar(row(3), row(1), 1.0, None, ALU.mult).then_inc(sem("mob_in2"), 1)
                dve.wait_ge(sem("mob_out2"), g + 1)
                link(V.tensor_scalar(row(15), row(4), 1.0, None, ALU.add))
                link(V.reciprocal(row(6), row(15)))
                link(V.tensor_tensor(row(7), row(5), row(6), ALU.mult))
                link(V.tensor_scalar(row(8), row(7), EPS, None, ALU.max))
                link(V.tensor_scalar(row(9), row(8), CLIP, None, ALU.min))
                artanh_in(link, row(10), row(18), row(9), row(16), row(17)).then_inc(sem("mob_in3"), 1)
                dve.wait_ge(sem("mob_out3"), g + 1)
                artanh_out(link, row(19), row(11), row(10), row(18), row(9), row(16), row(17))
                V.tensor_tensor(row(10), row(19), row_sum[:, rows], ALU.mult).then_inc(sem("mob_in4"), 1)
                dve.wait_ge(sem("mob_out4"), g + 1)
                link(V.reciprocal(row(16), row(8)))
                link(V.tensor_tensor(row(20), row(11), row(16), ALU.mult))
                link(V.tensor_tensor(row(15), row(7), row(20), ALU.mult))
                link(magnitude(row(16), row(15)))
                link(V.tensor_scalar(row(21), row(16), EPS, None, ALU.max))
                link(V.tensor_scalar(row(9), row(21), CLIP, None, ALU.min))
                artanh_in(link, row(10), row(18), row(9), row(16), row(17)).then_inc(sem("mob_in5"), 1)
                dve.wait_ge(sem("mob_out5"), g + 1)
                artanh_out(link, row(19), row(11), row(10), row(18), row(9), row(16), row(17))
                link(V.reciprocal(row(16), row(21)))
                link(V.tensor_tensor(row(17), row(19), row(16), ALU.mult))
                link(V.tensor_tensor(row(16), row(17), row(20), ALU.mult))
                link(V.tensor_tensor(row(17), row(16), row(6), ALU.mult))
                V.tensor_tensor(row(12), row(17), row(0), ALU.mult).then_inc(sem("mob_in6"), 1)
                dve.wait_ge(sem("mob_out6"), g + 1)
                V.tensor_scalar(row(10), row(1), EPS * EPS, None, ALU.max).then_inc(sem("mob_in7"), 1)
                dve.wait_ge(sem("mob_out8"), g + 1)
                link(V.reciprocal(row(16), row(11)))
                link(V.tensor_tensor(row(15), row(10), row(16), ALU.mult))
                for s in range(SLOTS):
                    t = SLOTS * g + s
                    link(V.scalar_tensor_tensor(y4[:, s, :], Z[:, t, 0:D], gt[:, 15, s:s + 1], X[:, t, :],
                                                ALU.mult, ALU.add))
                    mean_var(link, y4[:, s, :], s)
                V.tensor_scalar(row(13), mv[:, :, 1], LN_EPS, None, ALU.add).then_inc(sem("mob_in8"), 1)
                dve.wait_ge(sem("mob_out9"), g + 1)
                link(V.reciprocal(row(15), row(14)))
                dve.wait_ge(*at("xs_turned", MOB, SLOTS * g))
                dve.wait_ge(*at("x_kept", MOB, g))
                for s in range(SLOTS):
                    V.tensor_scalar(xs4[:, s, :], y4[:, s, :], mv[:, s, 0:1], gt[:, 15, s:s + 1], ALU.subtract,
                                    ALU.mult).then_inc(sem("xs_ready"), 1)
                for s in range(SLOTS):
                    t = SLOTS * g + s
                    dve.wait_ge(*at("prod_ready", MOB, t + 1))
                    V.tensor_scalar(Z[:, t, 0:H], bank[:, 7, 0:H], 1.0, None, ALU.mult)
                    V.tensor_reduce(z_bound[:, bass.ds(t, 1)], bank[:, 7, 0:H], AX.X, ALU.max,
                                    apply_absolute_value=True).then_inc(sem("prod_read"), 1)
                assert link.n == MOB_STEPS, link.n

            dve.wait_ge(*at("prod_read", MOB, T))

            for stage in (G1, G2, G3, G4, G5, G6):
                w = WIDTH[stage]
                scales(stage, Chain(dve, *at("dve_scales", stage, 0)), z_bound[:, :])
                split_low(stage, Z)
                steps = {G3: 1, G5: 1, G6: 3}.get(stage, 0)
                with dve.Fori(0, T // 2) as i:
                    for b in range(2):
                        t = 2 * i + b
                        link = Chain(dve, *at("dve_conv", stage, steps * t))
                        dve.wait_ge(*at("half_ready", stage, t + 1))
                        V.scalar_tensor_tensor(r[:, 0:w], bank[:, b, 0:w], unscale[:, bass.ds(t, 1)], half[:, 0:w],
                                               ALU.mult, ALU.add).then_inc(sem("acc_read"), 1)
                        if stage in (G3, G5):
                            dve.wait_ge(*at("acc_read", stage, t + 1))
                            link(V.tensor_scalar(Z[:, t, 0:w], r[:, 0:w], 0.0, None, ALU.max))
                            V.tensor_reduce(z_bound[:, bass.ds(t, 1)], Z[:, t, 0:w], AX.X, ALU.max).then_inc(
                                sem("prod_read"), 1)
                            continue
                        dve.wait_ge(*at("small_ready", stage, t + 1))
                        if stage in (G1, G2):
                            wo, src, done = (H if stage == G1 else H2), bank[:, 7, :], "small_read"
                        elif stage == G4:
                            V.tensor_scalar(z4[:, :], bank[:, 7, 0:H], 0.0, None, ALU.max).then_inc(
                                sem("small_read"), 1)
                            wo, src, done = H, bank[:, 5, :], "prod_read"
                            dve.wait_ge(*at("prod_ready", stage, t + 1))
                        else:
                            V.scalar_tensor_tensor(y, bank[:, 7, 0:D], 0.0, X[:, t, :], ALU.max, ALU.add).then_inc(
                                sem("small_read"), 1)
                            dve.wait_ge(*at("small_read", stage, t + 1))
                            norm_ready(stage, link, y)
                            dve.wait_ge(*at("x_kept", stage, t))
                            norm_rows(stage, link, t, xs, y, "rows_ready")
                            dve.wait_ge(*at("xs_turned", stage, t))
                            dve.wait_ge(*at("rows_ready", stage, t + 1))
                            V.tensor_scalar(xd, xs, deg_root[:, bass.ds(t, 1)], None, ALU.mult).then_inc(
                                sem("xs_ready"), 1)
                            wo, src, done = D, bank[:, 5, :], "prod_read"
                            dve.wait_ge(*at("prod_ready", stage, t + 1))
                        V.tensor_scalar(Z[:, t, 0:wo], src[:, 0:wo], 1.0, None, ALU.mult)
                        V.tensor_reduce(z_bound[:, bass.ds(t, 1)], src[:, 0:wo], AX.X, ALU.max,
                                        apply_absolute_value=True).then_inc(sem(done), 1)
                        assert link.n == steps, link.n
                dve.wait_ge(*at("prod_read" if stage in (G3, G4, G5, G6) else "small_read", stage, T))

            scales(NORM, Chain(dve, *at("dve_scales", NORM, 0)), z_bound[:, :])
            split_low(NORM, Z)
            OUT_STEPS = 5

            def out_pair(i):
                for b in range(2):
                    t = 2 * i + b
                    link = Chain(dve, sem("dve_out"), OUT_STEPS * t)
                    dve.wait_ge(*at("agg_done", NORM, t + 1))
                    V.scalar_tensor_tensor(yb, bank[:, b, 0:D], unscale[:, bass.ds(t, 1)], Z[:, t, 0:D],
                                           ALU.mult, ALU.add).then_inc(sem("acc_read"), 1)
                    dve.wait_ge(*at("acc_read", NORM, t + 1))
                    link(V.scalar_tensor_tensor(yc, yb, deg_root[:, bass.ds(t, 1)], b_sb[:, :], ALU.mult, ALU.add))
                    link(V.scalar_tensor_tensor(y, yc, 0.0, X[:, t, :], ALU.max, ALU.add))
                    norm_ready(NORM, link, y)
                    if not isinstance(i, int):
                        dve.wait_ge(sem(f"out_done{b}"), 16 * i)
                    norm_rows(NORM, link, t, xs4[:, b, :], y, "xs_ready")
                    assert link.n == OUT_STEPS, link.n

            dve.wait_ge(*at("x_kept", G6, T))
            out_pair(0)
            with dve.Fori(1, T // 2) as i:
                out_pair(i)


_INS = ["x", "adj", "L1_gnn_W", "L2_gnn_W1", "L2_gnn_W2", "L2_gnn_W3", "L2_gnn_W4", "L2_gnn_W5", "L2_gnn_W6",
        "L3_gnn_W", "L3_gnn_b"]


def kernel(**inputs):
    import numpy as np
    import concourse.bacc as bacc
    from concourse.bass_utils import run_bass_kernel_spmd

    laid = {name: np.ascontiguousarray(inputs[name]) for name in _INS}
    laid["L3_gnn_W"] = np.ascontiguousarray(laid["L3_gnn_W"].T)
    laid["L3_gnn_b"] = np.ascontiguousarray(np.broadcast_to(laid["L3_gnn_b"], (P, laid["L3_gnn_b"].shape[0])))

    nc = bacc.Bacc("TRN2", target_bir_lowering=False, num_devices=1)
    arrays = {f"in_{n}": a for n, a in laid.items()}
    args = [nc.dram_tensor(f"in_{n}", a.shape, mybir.dt.from_np(a.dtype), kind="ExternalInput").ap()
            for n, a in laid.items()]
    out = nc.dram_tensor("out", laid["x"].shape, F32, kind="ExternalOutput").ap()
    build(nc, *args, out)
    result = run_bass_kernel_spmd(nc, [arrays], core_ids=[0])
    return result.results[0]["out"]
```

```python
from contextlib import ExitStack

import concourse.bass as bass
from concourse import mybir

ALU = mybir.AluOpType
ACT = mybir.ActivationFunctionType
AX = mybir.AxisListType
F32 = mybir.dt.float32
F16 = mybir.dt.float16
BF16 = mybir.dt.bfloat16
I32 = mybir.dt.int32

P = 128
LN_EPS = 1e-5
NORM_EPS = 1e-12
EPS = 1e-10
CLIP = 1.0 - 1e-7
TOP = 2.0 ** 14
TINY = 2.0 ** -100
EXPONENT = 0x7F800000

SLOTS = 4
KEPT = 3
GK = 8
MOB, G1, G2, G3, G4, G5, G6, NORM = range(8)
NAMES = ["mob", "g1", "g2", "g3", "g4", "g5", "g6", "norm"]


class Chain:

    def __init__(self, eng, sem, base=0):
        self.eng, self.sem, self.base, self.n = eng, sem, base, 0

    def __call__(self, ins):
        ins.then_inc(self.sem, 1)
        self.n += 1
        self.eng.wait_ge(self.sem, self.base + self.n)


def build(nc, x, adj, w_mob, w1, w2, w3, w4, w5, w6, w_norm_t, b_rows, out):
    N, D = x.shape
    T = N // P
    K = N // P
    NG = K // GK
    GROUPS = T // SLOTS
    H = w1.shape[1]
    H2 = w3.shape[1]
    WZ = D + 2
    WIDTH = {MOB: D, G1: H, G2: H, G3: H2, G4: H2, G5: H, G6: H, NORM: D}
    CHUNKS = T // 4

    ctx = ExitStack()
    with ctx:
        def sb(name, shape, dt=F32):
            return ctx.enter_context(nc.sbuf_tensor(name, shape, dt))

        made = {}

        def sem(name):
            if name not in made:
                made[name] = ctx.enter_context(nc.semaphore(name))
            return made[name]

        def total(name, stage):
            turning = ("inc", MOB, NORM)
            if name in ("z_max_ready", "z_max_turned", "z_pair_ready", "z_pair_sent", "z_scale_ready"):
                return 1
            if name == "z_high_done":
                return T + 1 if stage == MOB else CHUNKS
            if name == "z_low_done":
                return T if stage == MOB else CHUNKS
            if name == "x_kept" and stage == MOB:
                return GROUPS
            if name == "dve_scales":
                return 0 if stage in ("inc", MOB) else 5
            if name == "dve_conv":
                return {G3: T, G5: T, G6: 3 * T}.get(stage, 0)
            given = {
                "acc_read": ("inc", *range(8)), "agg_done": tuple(range(8)), "half_used": tuple(range(8)),
                "xs_ready": ("inc", MOB), "rows_ready": (G6, NORM),
                "xT_ready": turning, "xs_turned": turning, "x_kept": ("inc", MOB, G6),
                "prod_ready": (*turning, G4), "prod_read": (*turning, G3, G4, G5, G6),
                "var_ready": ("inc", G6, NORM), "dev_ready": ("inc", G6, NORM),
                "half_ready": (G1, G2, G3, G4, G5, G6), "rT_ready": (G1, G2, G4, G6),
                "r_turned": (G1, G2, G4, G6), "small_ready": (G1, G2, G4, G6), "small_read": (G1, G2, G4, G6),
                "z_turned": (G4,), "zT_ready": (G4,),
            }[name]
            return T if stage in given else 0

        def at(name, stage, value):
            before = ["inc", *range(8)]
            return sem(name), sum(total(name, s) for s in before[:before.index(stage)]) + value

        pairs_dram = nc.dram_tensor("adj_pairs", [T, P, K * 2 * P], F16, kind="Internal").ap()

        bank = ctx.enter_context(nc.psum_tensor("bank", [P, 8, 512], F32))

        X = sb("X", [P, T, D])
        Z = sb("Z", [P, T, WZ])
        ZP = sb("ZP", [P, T * 2 * WZ], F16)
        TILE = K * 2 * P
        ARENA = 5 * TILE
        arena = sb("arena", [P, ARENA], F16)
        RAW = arena[:, 0:4 * N].bitcast(F32).rearrange("p (b n) -> p b n", b=2)
        ROWS = arena[:, 4 * N:7 * N].rearrange("p (c n) -> p c n", c=3)
        PAIR = arena[:, 7 * N:9 * N].rearrange("p (g k h i) -> p g k h i", g=NG, k=GK, h=2)
        MASK = arena[:, 9 * N:10 * N].rearrange("p (g k i) -> p g k i", g=NG, k=GK)

        STAY = arena[:, 0:T * KEPT * 2 * P].rearrange("p (t k h i) -> p t k h i", k=KEPT, h=2, i=P)
        RING = arena[:, T * KEPT * 2 * P:(T * KEPT + 2 * (K - KEPT)) * 2 * P].rearrange(
            "p (s k h i) -> p s k h i", s=2, h=2, i=P)
        SPARE = ZP[:, T * 2 * H:T * 2 * H + T * 2 * P].rearrange("p (t h i) -> p t h i", h=2, i=P)

        def kept(stage):
            return KEPT if stage in (MOB, NORM) else KEPT + 1

        def streamed(stage, half):
            return (kept(stage), K // 2 + 1) if half == 0 else (K // 2 + 1, K)

        wmob_sb = sb("wmob_sb", [P, D // P, D])
        w1_sb = sb("w1_sb", [P, D // P, H])
        w2_sb = sb("w2_sb", [P, H])
        w3_sb = sb("w3_sb", [P, H2])
        w4_sb = sb("w4_sb", [H2, H])
        w5_sb = sb("w5_sb", [P, H])
        w6_sb = sb("w6_sb", [P, D])
        wnorm_sb = sb("wnorm_sb", [P, D // P, D])
        b_sb = sb("b_sb", [P, D])
        ident = sb("ident", [P, P])
        ident16 = sb("ident16", [P, P], F16)
        ones = sb("ones", [1, P])

        abs_parts = sb("abs_parts", [P, T, NG])
        sum_parts = sb("sum_parts", [P, T, NG])
        count_parts = sb("count_parts", [P, T, NG])
        count = sb("count", [P, T])
        root_count = sb("root_count", [P, T])
        row_scale = sb("row_scale", [P, T])
        row_inv = sb("row_inv", [P, T])
        row_sum = sb("row_sum", [P, T])
        x_sq = sb("x_sq", [P, T])
        m_sq = sb("m_sq", [P, T])
        z_bound = sb("z_bound", [P, T])
        unscale = sb("unscale", [P, T])
        z_factor = sb("z_factor", [P, T])
        gamma1 = sb("gamma1", [P, T])
        deg_root = sb("deg_root", [P, T])
        norm_bound = sb("norm_bound", [P, T])
        z_max = sb("z_max", [P, 1])
        x_max = sb("x_max", [P, 4])
        z_top = sb("z_top", [1, 4])
        z_pair = sb("z_pair", [1, 2])
        z_scale = sb("z_scale", [P, 2])
        stat = sb("stat", [P, 16])
        roots_in = sb("roots_in", [P, 3, T])
        roots = sb("roots", [P, 3, T])
        bt = sb("bt", [P, 10, T])
        gt = sb("gt", [P, 24, SLOTS])
        y4 = sb("y4", [P, SLOTS, D])
        xs4 = sb("xs4", [P, SLOTS, D])
        y = y4[:, 0, :]
        xs = xs4[:, 0, :]
        half = y4[:, 1, 0:H]
        r = y4[:, 2, 0:H]
        z4 = y4[:, 3, 0:H]
        xd = y4[:, 3, :]
        yb = y4[:, 1, :]
        yc = y4[:, 2, :]
        junk_abs = [y4[:, 2:4, :].rearrange("p s f -> p (s f)").bitcast(BF16),
                    xs4[:, 2:4, :].rearrange("p s f -> p (s f)").bitcast(BF16)]
        bn6 = sb("bn6", [P, SLOTS, 6])
        mv = sb("mv", [P, SLOTS, 2])
        xT = sb("xT", [P, D])
        zT = sb("zT", [P, D])
        junk_sq = sb("junk_sq", [P, SLOTS, D], BF16)

        TURNED = [[bank[:, 3 * u + c, :].bitcast(F16) for c in range(3)] for u in range(2)]

        x_rows = x.rearrange("(t p) f -> p t f", p=P)
        adj_rows = adj.rearrange("(t p) n -> t p n", p=P)
        out_rows = out.rearrange("(t p) f -> t p f", p=P)

        def zp_view(stage):
            w = WZ if stage == MOB else (D if stage == "inc" else WIDTH[stage])
            return ZP[:, 0:T * 2 * w].rearrange("p (t h f) -> p t h f", h=2, f=w)

        block = ctx.enter_context(nc.Block())

        @block.sync
        def _(sp):
            def load_rows(t, b, g):
                sp.dma_start(RAW[:, b, g * GK * P:(g + 1) * GK * P],
                             adj_rows[t, :, g * GK * P:(g + 1) * GK * P]).then_inc(sem(f"raw_in{b}{g}"), 16)

            for g in range(NG):
                load_rows(0, 0, g)
            for c in range(4):
                part = slice(c * T // 4, (c + 1) * T // 4)
                sp.dma_start(X[:, part, :], x_rows[:, part, :]).then_inc(sem(f"x_in{c}"), 16)
            for g in range(NG):
                load_rows(1, 1, g)
            for dst, src in ((wmob_sb[:, :, :], w_mob.rearrange("(c p) f -> p c f", p=P)),
                             (w1_sb[:, :, :], w1.rearrange("(c p) f -> p c f", p=P)),
                             (w2_sb[:, :], w2), (w3_sb[:, :], w3), (w4_sb[:, :], w4), (w5_sb[:, :], w5),
                             (w6_sb[:, :], w6), (wnorm_sb[:, :, :], w_norm_t.rearrange("(c p) f -> p c f", p=P)),
                             (b_sb[:, :], b_rows)):
                sp.dma_start(dst, src).then_inc(sem("weights_in"), 16)
            for g in range(NG):
                sp.wait_ge(sem("rows_split"), g + 1)
                load_rows(2, 0, g)

            def pair_of_tiles(i):
                for b in range(2):
                    t = 2 * i + b
                    for g in range(NG):
                        n = NG * t + g
                        sp.wait_ge(sem("pairs_done"), n + 1)
                        sp.dma_start(pairs_dram[t, :, g * GK * 2 * P:(g + 1) * GK * 2 * P],
                                     PAIR[:, g, :, :, :].rearrange("p k h i -> p (k h i)")).then_inc(
                                         sem(f"pairs_stored{g}"), 16)
                        if not (isinstance(t, int) and t + 3 >= T):
                            sp.wait_ge(sem("rows_split"), n + NG + 1)
                            load_rows(t + 3, 1 - b, g)

            pair_of_tiles(0)
            with sp.Fori(1, T // 2 - 2) as i:
                pair_of_tiles(i)
            pair_of_tiles(T // 2 - 2)
            pair_of_tiles(T // 2 - 1)

            sp.wait_ge(sem("group_used"), NG * T)
            for g in range(NG):
                sp.wait_ge(sem(f"pairs_stored{g}"), 16 * T)

            def load_half(stage, t, s, half):
                a, z = streamed(stage, half)
                sp.dma_start(RING[:, s % 2, a - KEPT:z - KEPT, :, :].rearrange("p k h i -> p (k h i)"),
                             pairs_dram[t, :, a * 2 * P:z * 2 * P]).then_inc(sem(f"ring_in{s % 2}{half}"), 16)

            def load_kept(c):
                tiles = slice(c * T // 4, (c + 1) * T // 4)
                sp.dma_start(STAY[:, tiles, :, :, :].rearrange("p t k h i -> p t (k h i)"),
                             pairs_dram[tiles, :, 0:KEPT * 2 * P].rearrange("t p f -> p t f")).then_inc(
                                 sem("kept_in"), 16)

            load_kept(0)
            for stage in range(8):
                if stage == G1:
                    sp.wait_ge(*at("agg_done", MOB, T))
                    sp.dma_start(SPARE.rearrange("p t h i -> p t (h i)"),
                                 pairs_dram[:, :, KEPT * 2 * P:(KEPT + 1) * 2 * P].rearrange(
                                     "t p f -> p t f")).then_inc(sem("spare_in"), 16)

                def load_group(g):
                    for s in range(SLOTS):
                        t = SLOTS * g + s
                        for half in range(2):
                            used = ("half_used", "agg_done")[half]
                            if not (isinstance(g, int) and s < 2):
                                sp.wait_ge(*at(used, stage, t - 1))
                            elif stage > 0:
                                sp.wait_ge(*at(used, stage - 1, T - 1 + s))
                            load_half(stage, t, s, half)
                        if stage == MOB and isinstance(g, int) and s == 1:
                            for c in range(1, 4):
                                load_kept(c)

                load_group(0)
                with sp.Fori(1, GROUPS) as g:
                    load_group(g)

        @block.tensor
        def _(pe):
            def turn(dst, src):
                return pe.transpose(dst, src, ident[:, :])

            def scale_steps(stage):
                pe.wait_ge(*at("z_max_ready", stage, 1))
                turn(bank[0:1, 7, 0:P], z_max[:, :]).then_inc(sem("z_max_turned"), 1)
                pe.wait_ge(*at("z_pair_ready", stage, 1))
                pe.matmul(bank[:, 7, 256:258], ones[:, :], z_pair[:, :], start=True, stop=True).then_inc(
                    sem("z_pair_sent"), 1)

            zp0 = zp_view("inc")

            def turn_group(n, g):
                pe.wait_ge(sem("rows_split"), n + 1)
                if not (isinstance(n, int) and n < 2):
                    pe.wait_ge(sem("pairs_done"), n - 1)
                    pe.wait_ge(sem("mask_done"), n - 1)
                for c in range(3):
                    for kk in range(GK):
                        mm = pe.transpose(TURNED[g % 2][c][:, kk * P:(kk + 1) * P],
                                          ROWS[:, c, (g * GK + kk) * P:(g * GK + kk + 1) * P], ident16[:, :])
                mm.then_inc(sem("turned"), 1)

            def multiply_group(t, g):
                n = NG * t + g
                pe.wait_ge(sem("pairs_done"), n + 1)
                pe.wait_ge(sem("mask_done"), n + 1)
                if g == 0 and not (isinstance(t, int) and t == 0):
                    pe.wait_ge(*at("acc_read", "inc", t))
                for kk in range(GK):
                    k = g * GK + kk
                    if isinstance(t, int) and t == 0 and k % 4 == 0:
                        pe.wait_ge(*at("z_low_done", "inc", k // 4 + 1))
                    a, z = k == 0, k == K - 1

                    def mm(side, lhs, rhs, start=False, stop=False):
                        return pe.matmul(bank[:, 6, side * D:(side + 1) * D], lhs, rhs, start=start, stop=stop,
                                         skip_group_check=True)

                    mm(0, PAIR[:, g, kk, 0, :], zp0[:, k, 0, :], start=a)
                    mm(0, PAIR[:, g, kk, 0, :], zp0[:, k, 1, :])
                    mm(0, PAIR[:, g, kk, 1, :], zp0[:, k, 0, :], stop=z)
                    mm(1, MASK[:, g, kk, :], zp0[:, k, 0, :])
                    last = mm(1, MASK[:, g, kk, :], zp0[:, k, 1, :], stop=z)
                last.then_inc(sem("group_used"), 1)

            def turn_x(stage, t, src, b):
                pe.wait_ge(*at("acc_read" if stage == NORM else "xs_ready", stage, t + 1))
                pe.wait_ge(*at("xT_ready", stage, t))
                for c in range(D // P):
                    mm = turn(b[:, c * P:(c + 1) * P], src[:, c * P:(c + 1) * P])
                mm.then_inc(sem("xs_turned"), 1)

            def product_x(stage, t, src, w, width, b):
                pe.wait_ge(*at("xT_ready", stage, t + 1))
                pe.wait_ge(*at("prod_read", stage, t))
                for c in range(D // P):
                    mm = pe.matmul(b[:, 0:width], src[:, c * P:(c + 1) * P], w[:, c, :],
                                   start=c == 0, stop=c == D // P - 1)
                mm.then_inc(sem("prod_ready"), 1)

            def pair_of_tiles(i):
                for b in range(2):
                    t = 2 * i + b
                    for g in range(NG):
                        n = NG * t + g
                        if not (isinstance(n, int) and n + 2 >= NG * T):
                            turn_group(n + 2, (g + 2) % NG)
                        multiply_group(t, g)
                        if isinstance(t, int) and t == 0:
                            continue
                        if g == 1:
                            turn_x("inc", t - 1, xs, bank[:, 7, 0:D])
                        if g == 2:
                            product_x("inc", t - 1, xT, wmob_sb, D, bank[:, 7, D:2 * D])

            pe.wait_ge(sem("ident_ready"), 3)
            turn_group(0, 0)
            turn_group(1, 1)
            scale_steps("inc")
            pe.wait_ge(sem("weights_in"), 16 * 9)
            pair_of_tiles(0)
            with pe.Fori(1, T // 2 - 1) as i:
                pair_of_tiles(i)
            pair_of_tiles(T // 2 - 1)
            turn_x("inc", T - 1, xs, bank[:, 7, 0:D])
            product_x("inc", T - 1, xT, wmob_sb, D, bank[:, 7, D:2 * D])

            def small_turn(stage, t, w):
                pe.wait_ge(*at("acc_read", stage, t + 1))
                pe.wait_ge(*at("rT_ready", stage, t))
                pe.sem_inc(sem("pe_marks"), 1)
                turn(bank[0:w, 6, 0:P], r[:, 0:w]).then_inc(sem("r_turned"), 1)

            def small_product(stage, t, w, weights, wo):
                pe.wait_ge(*at("rT_ready", stage, t + 1))
                pe.wait_ge(*at("small_read", stage, t))
                pe.matmul(bank[:, 7, 0:wo], xT[0:w, 0:P], weights, start=True, stop=True).then_inc(
                    sem("small_ready"), 1)

            def turn_z4(stage, t):
                pe.wait_ge(*at("small_read", stage, t + 1))
                pe.wait_ge(*at("zT_ready", stage, t))
                turn(bank[:, 4, 0:P], z4[:, :]).then_inc(sem("z_turned"), 1)

            def product_z4(stage, t):
                pe.wait_ge(*at("zT_ready", stage, t + 1))
                pe.wait_ge(*at("prod_read", stage, t))
                pe.matmul(bank[:, 5, 0:H], zT[:, 0:P], w5_sb[:, :], start=True, stop=True).then_inc(
                    sem("prod_ready"), 1)

            def after(stage, t):
                if stage in (G1, G2):
                    weights, wo = (w2_sb[:, :], H) if stage == G1 else (w3_sb[:, :], H2)
                    return [(8, lambda: small_turn(stage, t, H)),
                            (16, lambda: small_product(stage, t, H, weights, wo))]
                if stage == G4:
                    return [(6, lambda: small_turn(stage, t, H2)),
                            (13, lambda: small_product(stage, t, H2, w4_sb[:, :], H)),
                            (20, lambda: turn_z4(stage, t)), (27, lambda: product_z4(stage, t))]
                if stage == G6:
                    return [(8, lambda: small_turn(stage, t, H)),
                            (16, lambda: small_product(stage, t, H, w6_sb[:, :], D))]
                if stage == NORM:
                    return [(8, lambda: turn_x(stage, t, yb, bank[:, 4, :])),
                            (16, lambda: product_x(stage, t, zT, wnorm_sb, D, bank[:, 5, :]))]
                return []

            def after_group(g):
                steps = []
                for s in range(SLOTS):
                    t = SLOTS * g + s
                    steps.append((8 * s + 2, lambda t=t, s=s: turn_x(MOB, t, xs4[:, s, :], bank[:, 6, :])))
                    steps.append((8 * s + 6, lambda t=t: product_x(MOB, t, xT, w1_sb, H, bank[:, 7, :])))
                return steps

            def aggregate(stage, g, s, steps, fresh=False):
                t = SLOTS * g + s
                w = WIDTH[stage]
                zp = zp_view(stage)
                if stage == MOB:
                    acc = bank[:, s, 0:D + 1]
                    if not isinstance(g, int):
                        pe.wait_ge(*at("acc_read", stage, t + 1 - SLOTS))
                else:
                    acc = bank[:, s % 2, :]
                    if not (isinstance(g, int) and s < 2):
                        pe.wait_ge(*at("acc_read", stage, t - 1))
                halves = [streamed(stage, half)[0] for half in range(2)]
                for k in range(K):
                    if fresh and k == 0 and stage == MOB:
                        pe.wait_ge(sem("kept_in"), 16 * 4)
                    if fresh and k == KEPT and stage == G1:
                        pe.wait_ge(sem("spare_in"), 16)
                    if k in halves:
                        pe.wait_ge(sem(f"ring_in{s % 2}{halves.index(k)}"),
                                   16 * (T // 2 * stage + 1) + 16 * (2 * g + s // 2))
                    for when, step in steps:
                        if when == k:
                            step()
                    if fresh and (stage == MOB or k % 4 == 0):
                        pe.wait_ge(*at("z_low_done", stage, (k if stage == MOB else k // 4) + 1))
                    a, z = k == 0, k == K - 1
                    if k < KEPT:
                        high, low = STAY[:, t, k, 0, :], STAY[:, t, k, 1, :]
                    elif k < kept(stage):
                        high, low = SPARE[:, t, 0, :], SPARE[:, t, 1, :]
                    else:
                        high, low = RING[:, s % 2, k - KEPT, 0, :], RING[:, s % 2, k - KEPT, 1, :]
                    if stage in (MOB, NORM):
                        n = D + 1 if stage == MOB else D
                        pe.matmul(acc[:, 0:n], high, zp[:, k, 0, 0:n], start=a, stop=False)
                        pe.matmul(acc[:, 0:n], high, zp[:, k, 1, 0:n], start=False, stop=False)
                        mm = pe.matmul(acc[:, 0:n], low, zp[:, k, 0, 0:n], start=False, stop=z)
                    else:
                        pe.matmul(acc[:, 0:2 * w], high, zp[:, k, :, :].rearrange("p h f -> p (h f)"),
                                  start=a, stop=False, skip_group_check=True)
                        mm = pe.matmul(acc[:, w:2 * w], low, zp[:, k, 0, :], start=False, stop=z,
                                       skip_group_check=True)
                    if k == K // 2:
                        mm.then_inc(sem("half_used"), 1)
                mm.then_inc(sem("agg_done"), 1)

            def group(stage, g, first):
                for s in range(SLOTS):
                    if stage == MOB:
                        steps = after_group(g - 1) if s == SLOTS - 1 and not first else []
                    else:
                        steps = after(stage, SLOTS * g + s - 1) if not (first and s == 0) else []
                    aggregate(stage, g, s, steps, fresh=first and s == 0)

            for stage in range(8):
                scale_steps(stage)
                group(stage, 0, True)
                with pe.Fori(1, GROUPS) as g:
                    group(stage, g, False)
                for _, step in (after_group(GROUPS - 1) if stage == MOB else after(stage, T - 1)):
                    step()

        @block.gpsimd
        def _(pool):
            nc.gpsimd.memset(ident[:, :], 0.0).then_inc(sem("ident_zero"), 1)
            nc.gpsimd.memset(ones[:, :], 1.0).then_inc(sem("ident_ready"), 1)
            pool.wait_ge(sem("ident_zero"), 1)
            nc.gpsimd.affine_select(out=ident[:, :], in_=ident[:, :], compare_op=ALU.not_equal, fill=1.0,
                                    base=0, pattern=[[-1, P]], channel_multiplier=1).then_inc(sem("ident_ready"), 1)
            pool.wait_ge(sem("ident_ready"), 2)
            nc.gpsimd.tensor_copy(ident16[:, :], ident[:, :]).then_inc(sem("ident_ready"), 1)
            with pool.Fori(0, T) as t:
                pool.wait_ge(*at("xs_ready", "inc", t + 1))
                nc.gpsimd.tensor_copy(X[:, t, :], xs).then_inc(sem("x_kept"), 1)
            with pool.Fori(0, GROUPS) as g:
                pool.wait_ge(*at("xs_ready", MOB, SLOTS * g + SLOTS))
                nc.gpsimd.tensor_copy(X[:, bass.ds(SLOTS * g, SLOTS), :], xs4[:, :, :]).then_inc(
                    sem("x_kept"), 1)
            with pool.Fori(0, T) as t:
                pool.wait_ge(*at("rows_ready", G6, t + 1))
                nc.gpsimd.tensor_copy(X[:, t, :], xs).then_inc(sem("x_kept"), 1)

        @block.scalar
        def _(act):
            def A(*args, **kw):
                return nc.scalar.activation(*args, **kw)

            def A_at(*args, **kw):
                act.sem_inc(sem("act_marks"), 1)
                return A(*args, **kw)

            def split_high(stage, src):
                zp = zp_view(stage)
                w = zp.shape[3]
                act.wait_ge(*at("z_scale_ready", stage, 1))
                for c in range(CHUNKS):
                    A(zp[:, 4 * c:4 * c + 4, 0, :], src[:, 4 * c:4 * c + 4, 0:w], ACT.Copy,
                      scale=z_scale[:, 0:1]).then_inc(sem("z_high_done"), 1)

            def sum_magnitudes(t, i, b, g):
                act.wait_ge(sem(f"raw_in{b}{g}"), 16 * i + 16)
                if not (isinstance(t, int) and NG * t + g < 2):
                    act.wait_ge(sem("magnitudes"), NG * t + g - 1)
                A_at(junk_abs[g % 2], RAW[:, b, g * GK * P:(g + 1) * GK * P], ACT.Abs,
                     accum_out=abs_parts[:, t, g:g + 1]).then_inc(sem("magnitudes"), 1)

            def high_rows(t, b, g):
                act.wait_ge(sem("row_scale_ready"), t + 1)
                if not (isinstance(t, int) and t == 0):
                    act.wait_ge(sem("turned"), NG * t + g + 1 - NG)
                A_at(ROWS[:, 0, g * GK * P:(g + 1) * GK * P], RAW[:, b, g * GK * P:(g + 1) * GK * P], ACT.Copy,
                     scale=row_scale[:, bass.ds(t, 1)], accum_out=sum_parts[:, t, g:g + 1]).then_inc(
                         sem("high_rows_done"), 1)

            def copy_mask(n, g):
                act.wait_ge(sem("turned"), n + 1)
                if not (isinstance(n, int) and n < NG):
                    act.wait_ge(sem("group_used"), n + 1 - NG)
                A(MASK[:, g, :, :].rearrange("p k i -> p (k i)"), TURNED[g % 2][2], ACT.Copy).then_inc(
                    sem("mask_done"), 1)

            def root_count_of(t):
                act.wait_ge(sem("counted"), t + 1)
                A_at(root_count[:, bass.ds(t, 1)], count[:, bass.ds(t, 1)], ACT.Sqrt).then_inc(sem("count_rooted"), 1)

            def root_var(stage, t, n=1):
                act.wait_ge(*at("var_ready", stage, t + 1))
                A(stat[:, 1:2], stat[:, 0:1], ACT.Sqrt).then_inc(sem("dev_ready"), 1)

            def keep_xT(stage, t, dst, b):
                act.wait_ge(*at("xs_turned", stage, t + 1))
                act.wait_ge(*at("prod_ready", stage, t))
                A(dst[:, :], b[:, 0:D], ACT.Copy).then_inc(sem("xT_ready"), 1)

            def squares(t):
                act.wait_ge(*at("xs_ready", "inc", t + 1))
                A_at(junk_sq[:, 0, :], xs, ACT.Square, accum_out=x_sq[:, bass.ds(t, 1)]).then_inc(sem("x_squared"), 1)

            def keep_product(t):
                act.wait_ge(*at("prod_ready", "inc", t + 1))
                A_at(junk_sq[:, 1, :], bank[:, 7, D:2 * D], ACT.Square, accum_out=m_sq[:, bass.ds(t, 1)]).then_inc(sem("m_squared"), 1)
                A_at(Z[:, t, 0:D], bank[:, 7, D:2 * D], ACT.Copy).then_inc(sem("prod_read"), 1)

            for b in range(2):
                for g in range(NG):
                    sum_magnitudes(b, 0, b, g)
                if b == 0:
                    for g in range(NG):
                        high_rows(0, 0, g)
                    copy_mask(0, 0)
                    copy_mask(1, 1)
                    split_high("inc", X)

            def pair_of_tiles(i):
                for b in range(2):
                    t = 2 * i + b
                    fixed = isinstance(t, int)
                    for g in range(NG):
                        n = NG * t + g
                        if not (fixed and t + 1 >= T):
                            high_rows(t + 1, 1 - b, g)
                        if not (fixed and n + 2 >= NG * T):
                            copy_mask(n + 2, (g + 2) % NG)
                        if not (fixed and t + 2 >= T):
                            sum_magnitudes(t + 2, i + 1, b, g)
                        if g == 1:
                            root_count_of(t)
                        if fixed and t == 0:
                            continue
                        if g == 0:
                            root_var("inc", t - 1)
                        if g == 1:
                            squares(t - 1)
                        if g == 2:
                            keep_xT("inc", t - 1, xT, bank[:, 7, :])
                        if g == 3:
                            keep_product(t - 1)

            pair_of_tiles(0)
            with act.Fori(1, T // 2 - 1) as i:
                pair_of_tiles(i)
            pair_of_tiles(T // 2 - 1)
            root_var("inc", T - 1)
            squares(T - 1)
            keep_xT("inc", T - 1, xT, bank[:, 7, :])
            keep_product(T - 1)

            act.wait_ge(sem("factor_in1"), 1)
            A(roots[:, :, :], roots_in[:, :, :], ACT.Sqrt).then_inc(sem("factor_out1"), 1)
            act.wait_ge(sem("factor_in2"), 1)
            A(bt[:, 1, :], bt[:, 0, :], ACT.Ln).then_inc(sem("factor_out2"), 1)
            act.wait_ge(sem("factor_in3"), 1)
            A(bt[:, 1, :], bt[:, 0, :], ACT.Tanh).then_inc(sem("factor_out3"), 1)

            zp = zp_view(MOB)
            act.wait_ge(*at("z_scale_ready", MOB, 1))
            A(zp[:, :, 0, D], gamma1[:, :], ACT.Copy, scale=z_scale[:, 0:1]).then_inc(sem("z_high_done"), 1)
            with act.Fori(0, T) as t:
                A_at(zp[:, t, 0, 0:D], Z[:, t, 0:D], ACT.Copy, scale=z_factor[:, bass.ds(t, 1)]).then_inc(
                    sem("z_high_done"), 1)

            with act.Fori(0, GROUPS) as g:
                act.wait_ge(sem("mob_in1"), g + 1)
                for s in range(SLOTS):
                    last = A_at(junk_sq[:, s, :], Z[:, SLOTS * g + s, 0:D], ACT.Square, scale=gt[:, 0, s:s + 1],
                             accum_out=gt[:, 1, s:s + 1])
                last.then_inc(sem("mob_out1"), 1)
                act.wait_ge(sem("mob_in2"), g + 1)
                A(gt[:, 4:6, :], gt[:, 2:4, :], ACT.Sqrt).then_inc(sem("mob_out2"), 1)
                act.wait_ge(sem("mob_in3"), g + 1)
                A(gt[:, 11, :], gt[:, 10, :], ACT.Ln).then_inc(sem("mob_out3"), 1)
                act.wait_ge(sem("mob_in4"), g + 1)
                A(gt[:, 11, :], gt[:, 10, :], ACT.Tanh).then_inc(sem("mob_out4"), 1)
                act.wait_ge(sem("mob_in5"), g + 1)
                A(gt[:, 11, :], gt[:, 10, :], ACT.Ln).then_inc(sem("mob_out5"), 1)
                act.wait_ge(sem("mob_in6"), g + 1)
                for s in range(SLOTS):
                    last = A_at(Z[:, SLOTS * g + s, 0:D], Z[:, SLOTS * g + s, 0:D], ACT.Relu, scale=gt[:, 12, s:s + 1])
                last.then_inc(sem("mob_relu"), 1)
                act.wait_ge(sem("mob_relu"), g + 1)
                for s in range(SLOTS):
                    last = A_at(junk_sq[:, s, :], Z[:, SLOTS * g + s, 0:D], ACT.Square, accum_out=gt[:, 1, s:s + 1])
                last.then_inc(sem("mob_out6"), 1)
                act.wait_ge(sem("mob_in7"), g + 1)
                A(gt[:, 11, :], gt[:, 10, :], ACT.Sqrt).then_inc(sem("mob_out7"), 1)
                act.wait_ge(sem("mob_out7"), g + 1)
                A(gt[:, 10, :], gt[:, 11, :], ACT.Tanh).then_inc(sem("mob_out8"), 1)
                act.wait_ge(sem("mob_in8"), g + 1)
                A(gt[:, 14, :], gt[:, 13, :], ACT.Sqrt).then_inc(sem("mob_out9"), 1)
                for s in range(SLOTS):
                    keep_xT(MOB, SLOTS * g + s, xT, bank[:, 6, :])

            def keep_half(stage, t, b):
                w = WIDTH[stage]
                act.wait_ge(*at("agg_done", stage, t + 1))
                act.wait_ge(*at("acc_read", stage, t))
                A_at(half[:, 0:w], bank[:, b, w:2 * w], ACT.Copy, scale=unscale[:, bass.ds(t, 1)]).then_inc(
                    sem("half_ready"), 1)

            def keep_rT(stage, t, func):
                w = WIDTH[stage]
                act.wait_ge(*at("r_turned", stage, t + 1))
                A(xT[0:w, 0:P], bank[0:w, 6, 0:P], func).then_inc(sem("rT_ready"), 1)

            for stage in (G1, G2, G3, G4, G5, G6):
                split_high(stage, Z)
                with act.Fori(0, T // 2) as i:
                    for b in range(2):
                        t = 2 * i + b
                        keep_half(stage, t, b)
                        if stage in (G1, G2):
                            keep_rT(stage, t, ACT.Relu)
                        if stage in (G4, G6):
                            keep_rT(stage, t, ACT.Copy)
                        if stage == G4:
                            act.wait_ge(*at("z_turned", stage, t + 1))
                            act.wait_ge(*at("prod_ready", stage, t))
                            A(zT[:, 0:P], bank[:, 4, 0:P], ACT.Copy).then_inc(sem("zT_ready"), 1)
                        if stage == G6:
                            root_var(stage, t)

            split_high(NORM, Z)
            with act.Fori(0, T // 2) as i:
                for b in range(2):
                    t = 2 * i + b
                    keep_xT(NORM, t, zT, bank[:, 4, :])
                    root_var(NORM, t)
                    act.wait_ge(*at("rows_ready", NORM, t + 1))
                    act.dma_start(out_rows[t], xs4[:, b, :]).then_inc(sem(f"out_done{b}"), 16)
            for b in range(2):
                act.wait_ge(sem(f"out_done{b}"), 16 * (T // 2))

        @block.vector
        def _(dve):
            V = nc.vector

            def scales(stage, link, bounds, two_axes=False):
                V.tensor_reduce(z_max[:, :], bounds, AX.XY if two_axes else AX.X, ALU.max,
                                apply_absolute_value=True).then_inc(sem("z_max_ready"), 1)
                dve.wait_ge(*at("z_max_turned", stage, 1))
                link(V.tensor_reduce(z_top[:, 0:1], bank[0:1, 7, 0:P], AX.X, ALU.max))
                link(V.tensor_scalar(z_top[:, 1:2], z_top[:, 0:1], TINY, None, ALU.max))
                link(V.tensor_scalar(z_top[:, 2:3].bitcast(I32), z_top[:, 1:2].bitcast(I32), EXPONENT, None,
                                     ALU.bitwise_and))
                link(V.reciprocal(z_top[:, 3:4], z_top[:, 2:3]))
                V.tensor_scalar(z_pair[:, 0:1], z_top[:, 3:4], TOP, None, ALU.mult)
                V.tensor_scalar(z_pair[:, 1:2], z_top[:, 2:3], 1.0 / TOP, None, ALU.mult).then_inc(
                    sem("z_pair_ready"), 1)
                dve.wait_ge(*at("z_pair_sent", stage, 1))
                V.tensor_copy(z_scale[:, :], bank[:, 7, 256:258]).then_inc(sem("z_scale_ready"), 1)
                if stage != "inc":
                    dve.wait_ge(*at("z_scale_ready", stage, 1))
                    link(V.tensor_scalar(unscale[:, :], row_inv[:, :], z_scale[:, 1:2], None, ALU.mult))

            def split_low(stage, src):
                zp = zp_view(stage)
                w = zp.shape[3]
                for c in range(CHUNKS):
                    for_c = slice(4 * c, 4 * c + 4)
                    dve.wait_ge(*at("z_high_done", stage, c + 1))
                    V.scalar_tensor_tensor(zp[:, for_c, 1, :], src[:, for_c, 0:w], z_scale[:, 0:1],
                                           zp[:, for_c, 0, :], ALU.mult, ALU.subtract).then_inc(
                                               sem("z_low_done"), 1)

            def mean_var(link, src, n=0):
                link(V.bn_stats(bn6[:, n, :], src))
                dve.sem_inc(sem("dve_marks"), 1)
                link(V.bn_aggr(mv[:, n, :], bn6[:, n, :]))

            def norm_ready(stage, link, src):
                mean_var(link, src)
                V.tensor_scalar(stat[:, 0:1], mv[:, 0, 1:2], LN_EPS, None, ALU.add).then_inc(sem("var_ready"), 1)

            def norm_rows(stage, link, t, dst, src, ready):
                dve.wait_ge(*at("dev_ready", stage, t + 1))
                link(V.reciprocal(stat[:, 2:3], stat[:, 1:2]))
                V.tensor_scalar(dst, src, mv[:, 0, 0:1], stat[:, 2:3], ALU.subtract, ALU.mult).then_inc(
                    sem(ready), 1)

            READ, SCALE, EDGE = 4, 4, 6

            def scale_of_rows(t):
                link = Chain(dve, sem("dve_scale_of"), SCALE * t)
                dve.wait_ge(sem("magnitudes"), NG * t + NG)
                link(V.tensor_reduce(stat[:, 3:4], abs_parts[:, t, :], AX.X, ALU.add))
                link(V.tensor_scalar(stat[:, 4:5], stat[:, 3:4], 1.0, None, ALU.add))
                link(V.tensor_scalar(stat[:, 5:6].bitcast(I32), stat[:, 4:5].bitcast(I32), EXPONENT, None,
                                     ALU.bitwise_and))
                link(V.reciprocal(stat[:, 6:7], stat[:, 5:6]))
                V.tensor_scalar(row_inv[:, bass.ds(t, 1)], stat[:, 5:6], 1.0 / TOP, None, ALU.mult)
                V.tensor_scalar(row_scale[:, bass.ds(t, 1)], stat[:, 6:7], TOP, None, ALU.mult).then_inc(
                    sem("row_scale_ready"), 1)

            def split_rows(t, b, g):
                n = NG * t + g
                quarter = slice(g * GK * P, (g + 1) * GK * P)
                dve.wait_ge(sem("high_rows_done"), n + 1)
                if not (isinstance(t, int) and t == 0):
                    dve.wait_ge(sem("turned"), n + 1 - NG)
                V.tensor_scalar(ROWS[:, 2, quarter], RAW[:, b, quarter], 0.0, None, ALU.is_gt, ALU.add,
                                accum_out=count_parts[:, t, g:g + 1])
                V.scalar_tensor_tensor(ROWS[:, 1, quarter], RAW[:, b, quarter], row_scale[:, bass.ds(t, 1)],
                                       ROWS[:, 0, quarter], ALU.mult, ALU.subtract).then_inc(sem("rows_split"), 1)

            def copy_pairs(n, t, g):
                dve.wait_ge(sem("turned"), n + 1)
                if not (isinstance(n, int) and n < NG):
                    dve.wait_ge(sem("group_used"), n + 1 - NG)
                    dve.wait_ge(sem(f"pairs_stored{g}"), 16 * t)
                for c in range(2):
                    last = V.tensor_copy(PAIR[:, g, :, c, :], TURNED[g % 2][c].rearrange("p (k i) -> p k i", i=P))
                last.then_inc(sem("pairs_done"), 1)

            def total_rows(t):
                V.tensor_reduce(row_sum[:, bass.ds(t, 1)], sum_parts[:, t, :], AX.X, ALU.add)
                V.tensor_reduce(count[:, bass.ds(t, 1)], count_parts[:, t, :], AX.X, ALU.add).then_inc(
                    sem("counted"), 1)

            def edge_factors(t):
                link = Chain(dve, sem("dve_edge"), EDGE * t)
                one = bass.ds(t, 1)
                dve.wait_ge(sem("count_rooted"), t + 1)
                link(V.tensor_scalar(stat[:, 8:9], root_count[:, one], NORM_EPS, None, ALU.max))
                link(V.reciprocal(stat[:, 9:10], stat[:, 8:9]))
                link(V.tensor_tensor(row_sum[:, one], row_sum[:, one], row_inv[:, one], ALU.mult))
                link(V.scalar_tensor_tensor(stat[:, 10:11], count[:, one], stat[:, 9:10], row_sum[:, one],
                                            ALU.mult, ALU.add))
                link(V.reciprocal(stat[:, 11:12], stat[:, 10:11]))
                V.tensor_scalar(stat[:, 12:13], row_inv[:, one], z_scale[:, 1:2], stat[:, 11:12], ALU.mult, ALU.mult)
                link(V.tensor_scalar(stat[:, 13:14], stat[:, 9:10], z_scale[:, 1:2], stat[:, 11:12], ALU.mult,
                                     ALU.mult))

            def read_sums(t):
                link = Chain(dve, sem("dve_read"), READ * t)
                dve.wait_ge(sem("group_used"), NG * t + NG)
                link(V.scalar_tensor_tensor(yb, bank[:, 6, 0:D], stat[:, 12:13], X[:, t, :], ALU.mult, ALU.add))
                V.scalar_tensor_tensor(y, bank[:, 6, D:2 * D], stat[:, 13:14], yb, ALU.mult, ALU.add).then_inc(
                    sem("acc_read"), 1)
                dve.wait_ge(*at("acc_read", "inc", t + 1))
                norm_ready("inc", link, y)

            def finish_rows(t):
                if not (isinstance(t, int) and t == 0):
                    dve.wait_ge(*at("xs_turned", "inc", t))
                    dve.wait_ge(sem("x_squared"), t)
                    dve.wait_ge(*at("x_kept", "inc", t))
                norm_rows("inc", Chain(dve, sem("dve_read"), READ * t + READ - 1), t, xs, y, "xs_ready")

            scale_of_rows(0)
            for g in range(NG):
                split_rows(0, 0, g)
            for c in range(4):
                dve.wait_ge(sem(f"x_in{c}"), 16)
                part = slice(c * T // 4, (c + 1) * T // 4)
                V.tensor_reduce(x_max[:, c:c + 1], X[:, part, :], AX.XY, ALU.max,
                                apply_absolute_value=True).then_inc(sem("x_topped"), 1)
            dve.wait_ge(sem("x_topped"), 4)
            scales("inc", Chain(dve, sem("dve_start")), x_max[:, :])
            copy_pairs(0, 0, 0)
            copy_pairs(1, 0, 1)
            split_low("inc", X)
            scale_of_rows(1)

            def pair_of_tiles(i):
                for b in range(2):
                    t = 2 * i + b
                    fixed = isinstance(t, int)
                    for g in range(NG):
                        n = NG * t + g
                        if g == 0 and not (fixed and t == 0):
                            read_sums(t - 1)
                        if not (fixed and n + 2 >= NG * T):
                            copy_pairs(n + 2, t + (g + 2) // NG, (g + 2) % NG)
                        if not (fixed and t + 1 >= T):
                            split_rows(t + 1, 1 - b, g)
                        if g == 0:
                            total_rows(t)
                        if g == 1 and not (fixed and t == 0):
                            finish_rows(t - 1)
                        if g == 2:
                            edge_factors(t)
                        if g == 3 and not (fixed and t + 2 >= T):
                            scale_of_rows(t + 2)

            pair_of_tiles(0)
            with dve.Fori(1, T // 2 - 1) as i:
                pair_of_tiles(i)
            pair_of_tiles(T // 2 - 1)
            read_sums(T - 1)
            finish_rows(T - 1)

            link = Chain(dve, sem("dve_factors"))

            def magnitude(dst, src):
                return V.scalar_tensor_tensor(dst, src, -1.0, src, ALU.mult, ALU.max)

            def artanh_in(link, w, u, c, t0, t1):
                link(V.tensor_scalar(t0, c, -1.0, 1.0, ALU.mult, ALU.add))
                link(V.reciprocal(t1, t0))
                link(V.scalar_tensor_tensor(u, c, 2.0, t1, ALU.mult, ALU.mult))
                return V.tensor_scalar(w, u, 1.0, None, ALU.add)

            def artanh_out(link, dst, log_w, w, u, c, t0, t1):
                link(V.tensor_scalar(t0, w, -1.0, 1e-30, ALU.add, ALU.max))
                link(V.reciprocal(t1, t0))
                link(V.tensor_tensor(t0, u, t1, ALU.mult))
                link(V.scalar_tensor_tensor(t1, log_w, 0.5, t0, ALU.mult, ALU.mult))
                link(V.tensor_tensor(dst, t1, c, ALU.max))

            dve.wait_ge(sem("x_squared"), T)
            dve.wait_ge(sem("m_squared"), T)
            V.tensor_scalar(roots_in[:, 0, :], x_sq[:, :], EPS * EPS, None, ALU.max)
            V.tensor_scalar(roots_in[:, 1, :], m_sq[:, :], EPS * EPS, None, ALU.max)
            link(V.tensor_scalar(bt[:, 9, :], row_sum[:, :], 1.0, None, ALU.add))
            V.tensor_scalar(roots_in[:, 2, :], bt[:, 9, :], 1e-30, None, ALU.max).then_inc(sem("factor_in1"), 1)
            dve.wait_ge(sem("factor_out1"), 1)
            xn, mn, dn = roots[:, 0, :], roots[:, 1, :], roots[:, 2, :]
            link(V.tensor_scalar(bt[:, 2, :], xn, CLIP, None, ALU.min))
            artanh_in(link, bt[:, 0, :], bt[:, 3, :], bt[:, 2, :], bt[:, 4, :], bt[:, 5, :]).then_inc(
                sem("factor_in2"), 1)
            dve.wait_ge(sem("factor_out2"), 1)
            artanh_out(link, bt[:, 6, :], bt[:, 1, :], bt[:, 0, :], bt[:, 3, :], bt[:, 2, :], bt[:, 4, :], bt[:, 5, :])
            link(V.reciprocal(bt[:, 4, :], xn))
            link(V.tensor_tensor(bt[:, 5, :], mn, bt[:, 4, :], ALU.mult))
            V.tensor_tensor(bt[:, 0, :], bt[:, 5, :], bt[:, 6, :], ALU.mult).then_inc(sem("factor_in3"), 1)
            dve.wait_ge(sem("factor_out3"), 1)
            link(V.reciprocal(bt[:, 4, :], mn))
            link(V.tensor_tensor(bt[:, 5, :], bt[:, 1, :], bt[:, 4, :], ALU.mult))
            link(V.scalar_tensor_tensor(bt[:, 6, :], mn, EPS, bt[:, 5, :], ALU.is_gt, ALU.mult))
            link(V.tensor_tensor(bt[:, 4, :], bt[:, 6, :], bt[:, 6, :], ALU.mult))
            link(V.tensor_tensor(bt[:, 5, :], bt[:, 4, :], m_sq[:, :], ALU.mult))
            link(V.tensor_scalar(bt[:, 4, :], bt[:, 5, :], -1.0, 1.0, ALU.mult, ALU.add))
            link(V.reciprocal(bt[:, 5, :], bt[:, 4, :]))
            link(V.tensor_scalar(bt[:, 7, :], bt[:, 5, :], 2.0, 1e-15, ALU.mult, ALU.max))
            link(V.tensor_scalar(gamma1[:, :], bt[:, 7, :], -1.0, None, ALU.add))
            link(V.tensor_tensor(bt[:, 8, :], bt[:, 7, :], bt[:, 6, :], ALU.mult))
            link(V.tensor_tensor(bt[:, 4, :], bt[:, 8, :], mn, ALU.mult))
            link(magnitude(bt[:, 5, :], bt[:, 4, :]))
            link(magnitude(bt[:, 3, :], gamma1[:, :]))
            link(V.tensor_tensor(z_bound[:, :], bt[:, 5, :], bt[:, 3, :], ALU.max))
            link(V.reciprocal(bt[:, 2, :], dn))
            link(V.scalar_tensor_tensor(deg_root[:, :], bt[:, 9, :], 0.0, bt[:, 2, :], ALU.is_gt, ALU.mult))
            link(V.tensor_scalar(norm_bound[:, :], deg_root[:, :], float(D) ** 0.5, None, ALU.mult))

            V.tensor_reduce(z_max[:, :], z_bound[:, :], AX.X, ALU.max).then_inc(sem("z_max_ready"), 1)
            dve.wait_ge(*at("z_max_turned", MOB, 1))
            link(V.tensor_reduce(z_top[:, 0:1], bank[0:1, 7, 0:P], AX.X, ALU.max))
            link(V.tensor_scalar(z_top[:, 1:2], z_top[:, 0:1], TINY, None, ALU.max))
            link(V.tensor_scalar(z_top[:, 2:3].bitcast(I32), z_top[:, 1:2].bitcast(I32), EXPONENT, None,
                                 ALU.bitwise_and))
            link(V.reciprocal(z_top[:, 3:4], z_top[:, 2:3]))
            V.tensor_scalar(z_pair[:, 0:1], z_top[:, 3:4], TOP, None, ALU.mult)
            V.tensor_scalar(z_pair[:, 1:2], z_top[:, 2:3], 1.0 / TOP, None, ALU.mult).then_inc(
                sem("z_pair_ready"), 1)
            dve.wait_ge(*at("z_pair_sent", MOB, 1))
            link(V.tensor_copy(z_scale[:, :], bank[:, 7, 256:258]))
            link(V.tensor_scalar(unscale[:, :], row_inv[:, :], z_scale[:, 1:2], None, ALU.mult))
            V.tensor_scalar(z_factor[:, :], bt[:, 8, :], z_scale[:, 0:1], None, ALU.mult).then_inc(
                sem("z_scale_ready"), 1)
            dve.wait_ge(*at("z_scale_ready", MOB, 1))
            zp = zp_view(MOB)
            dve.wait_ge(*at("z_high_done", MOB, 1))
            V.scalar_tensor_tensor(zp[:, :, 1, D], gamma1[:, :], z_scale[:, 0:1], zp[:, :, 0, D], ALU.mult,
                                   ALU.subtract)
            with dve.Fori(0, T) as t:
                dve.wait_ge(*at("z_high_done", MOB, t + 2))
                V.scalar_tensor_tensor(zp[:, t, 1, 0:D], Z[:, t, 0:D], z_factor[:, bass.ds(t, 1)],
                                       zp[:, t, 0, 0:D], ALU.mult, ALU.subtract).then_inc(
                                           sem("z_low_done"), 1)

            MOB_STEPS = 54

            def row(n):
                return gt[:, n, :]

            with dve.Fori(0, GROUPS) as g:
                link = Chain(dve, sem("dve_mob"), MOB_STEPS * g)
                rows = bass.ds(SLOTS * g, SLOTS)
                for s in range(SLOTS):
                    t = SLOTS * g + s
                    dve.wait_ge(*at("agg_done", MOB, t + 1))
                    V.tensor_scalar(Z[:, t, 0:D + 1], bank[:, s, 0:D + 1], 1.0, None, ALU.mult).then_inc(sem("acc_read"), 1)
                dve.wait_ge(*at("acc_read", MOB, SLOTS * g + SLOTS))
                link(V.tensor_tensor(row(15), Z[:, rows, D], unscale[:, rows], ALU.mult))
                link(V.tensor_scalar(row(16), row(15), 0.0, 2.0, ALU.is_ge, ALU.mult))
                link(V.tensor_scalar(row(17), row(16), -1.0, None, ALU.add))
                link(magnitude(row(18), row(15)))
                link(V.tensor_scalar(row(16), row(18), EPS, None, ALU.max))
                link(V.tensor_tensor(row(15), row(16), row(17), ALU.mult))
                link(V.reciprocal(row(16), row(15)))
                V.tensor_tensor(row(0), row(16), unscale[:, rows], ALU.mult).then_inc(sem("mob_in1"), 1)
                dve.wait_ge(sem("mob_out1"), g + 1)
                link(V.tensor_scalar(row(15), row(1), -1.0, 1.0, ALU.mult, ALU.add))
                V.tensor_scalar(row(2), row(15), EPS, None, ALU.max)
                V.tensor_scalar(row(3), row(1), 1.0, None, ALU.mult).then_inc(sem("mob_in2"), 1)
                dve.wait_ge(sem("mob_out2"), g + 1)
                link(V.tensor_scalar(row(15), row(4), 1.0, None, ALU.add))
                link(V.reciprocal(row(6), row(15)))
                link(V.tensor_tensor(row(7), row(5), row(6), ALU.mult))
                link(V.tensor_scalar(row(8), row(7), EPS, None, ALU.max))
                link(V.tensor_scalar(row(9), row(8), CLIP, None, ALU.min))
                artanh_in(link, row(10), row(18), row(9), row(16), row(17)).then_inc(sem("mob_in3"), 1)
                dve.wait_ge(sem("mob_out3"), g + 1)
                artanh_out(link, row(19), row(11), row(10), row(18), row(9), row(16), row(17))
                V.tensor_tensor(row(10), row(19), row_sum[:, rows], ALU.mult).then_inc(sem("mob_in4"), 1)
                dve.wait_ge(sem("mob_out4"), g + 1)
                link(V.reciprocal(row(16), row(8)))
                link(V.tensor_tensor(row(20), row(11), row(16), ALU.mult))
                link(V.tensor_tensor(row(15), row(7), row(20), ALU.mult))
                link(magnitude(row(16), row(15)))
                link(V.tensor_scalar(row(21), row(16), EPS, None, ALU.max))
                link(V.tensor_scalar(row(9), row(21), CLIP, None, ALU.min))
                artanh_in(link, row(10), row(18), row(9), row(16), row(17)).then_inc(sem("mob_in5"), 1)
                dve.wait_ge(sem("mob_out5"), g + 1)
                artanh_out(link, row(19), row(11), row(10), row(18), row(9), row(16), row(17))
                link(V.reciprocal(row(16), row(21)))
                link(V.tensor_tensor(row(17), row(19), row(16), ALU.mult))
                link(V.tensor_tensor(row(16), row(17), row(20), ALU.mult))
                link(V.tensor_tensor(row(17), row(16), row(6), ALU.mult))
                V.tensor_tensor(row(12), row(17), row(0), ALU.mult).then_inc(sem("mob_in6"), 1)
                dve.wait_ge(sem("mob_out6"), g + 1)
                V.tensor_scalar(row(10), row(1), EPS * EPS, None, ALU.max).then_inc(sem("mob_in7"), 1)
                dve.wait_ge(sem("mob_out8"), g + 1)
                link(V.reciprocal(row(16), row(11)))
                link(V.tensor_tensor(row(15), row(10), row(16), ALU.mult))
                for s in range(SLOTS):
                    t = SLOTS * g + s
                    link(V.scalar_tensor_tensor(y4[:, s, :], Z[:, t, 0:D], gt[:, 15, s:s + 1], X[:, t, :],
                                                ALU.mult, ALU.add))
                    mean_var(link, y4[:, s, :], s)
                V.tensor_scalar(row(13), mv[:, :, 1], LN_EPS, None, ALU.add).then_inc(sem("mob_in8"), 1)
                dve.wait_ge(sem("mob_out9"), g + 1)
                link(V.reciprocal(row(15), row(14)))
                dve.wait_ge(*at("xs_turned", MOB, SLOTS * g))
                dve.wait_ge(*at("x_kept", MOB, g))
                for s in range(SLOTS):
                    V.tensor_scalar(xs4[:, s, :], y4[:, s, :], mv[:, s, 0:1], gt[:, 15, s:s + 1], ALU.subtract,
                                    ALU.mult).then_inc(sem("xs_ready"), 1)
                for s in range(SLOTS):
                    t = SLOTS * g + s
                    dve.wait_ge(*at("prod_ready", MOB, t + 1))
                    V.tensor_scalar(Z[:, t, 0:H], bank[:, 7, 0:H], 1.0, None, ALU.mult)
                    V.tensor_reduce(z_bound[:, bass.ds(t, 1)], bank[:, 7, 0:H], AX.X, ALU.max,
                                    apply_absolute_value=True).then_inc(sem("prod_read"), 1)
                assert link.n == MOB_STEPS, link.n

            dve.wait_ge(*at("prod_read", MOB, T))

            for stage in (G1, G2, G3, G4, G5, G6):
                w = WIDTH[stage]
                scales(stage, Chain(dve, *at("dve_scales", stage, 0)), z_bound[:, :])
                split_low(stage, Z)
                steps = {G3: 1, G5: 1, G6: 3}.get(stage, 0)
                with dve.Fori(0, T // 2) as i:
                    for b in range(2):
                        t = 2 * i + b
                        link = Chain(dve, *at("dve_conv", stage, steps * t))
                        dve.wait_ge(*at("half_ready", stage, t + 1))
                        V.scalar_tensor_tensor(r[:, 0:w], bank[:, b, 0:w], unscale[:, bass.ds(t, 1)], half[:, 0:w],
                                               ALU.mult, ALU.add).then_inc(sem("acc_read"), 1)
                        if stage in (G3, G5):
                            dve.wait_ge(*at("acc_read", stage, t + 1))
                            link(V.tensor_scalar(Z[:, t, 0:w], r[:, 0:w], 0.0, None, ALU.max))
                            V.tensor_reduce(z_bound[:, bass.ds(t, 1)], Z[:, t, 0:w], AX.X, ALU.max).then_inc(
                                sem("prod_read"), 1)
                            continue
                        dve.wait_ge(*at("small_ready", stage, t + 1))
                        if stage in (G1, G2):
                            wo, src, done = (H if stage == G1 else H2), bank[:, 7, :], "small_read"
                        elif stage == G4:
                            V.tensor_scalar(z4[:, :], bank[:, 7, 0:H], 0.0, None, ALU.max).then_inc(
                                sem("small_read"), 1)
                            wo, src, done = H, bank[:, 5, :], "prod_read"
                            dve.wait_ge(*at("prod_ready", stage, t + 1))
                        else:
                            V.scalar_tensor_tensor(y, bank[:, 7, 0:D], 0.0, X[:, t, :], ALU.max, ALU.add).then_inc(
                                sem("small_read"), 1)
                            dve.wait_ge(*at("small_read", stage, t + 1))
                            norm_ready(stage, link, y)
                            dve.wait_ge(*at("x_kept", stage, t))
                            norm_rows(stage, link, t, xs, y, "rows_ready")
                            dve.wait_ge(*at("rows_ready", stage, t + 1))
                            V.tensor_scalar(Z[:, t, 0:D], xs, deg_root[:, bass.ds(t, 1)], None, ALU.mult).then_inc(
                                sem("prod_read"), 1)
                            continue
                        V.tensor_scalar(Z[:, t, 0:wo], src[:, 0:wo], 1.0, None, ALU.mult)
                        V.tensor_reduce(z_bound[:, bass.ds(t, 1)], src[:, 0:wo], AX.X, ALU.max,
                                        apply_absolute_value=True).then_inc(sem(done), 1)
                        assert link.n == steps, link.n
                dve.wait_ge(*at("prod_read" if stage in (G3, G4, G5, G6) else "small_read", stage, T))

            dve.wait_ge(*at("x_kept", G6, T))
            scales(NORM, Chain(dve, *at("dve_scales", NORM, 0)), norm_bound[:, :])
            split_low(NORM, Z)
            OUT_STEPS = 4

            def out_pair(i):
                for b in range(2):
                    t = 2 * i + b
                    link = Chain(dve, sem("dve_out"), OUT_STEPS * t)
                    dve.wait_ge(*at("agg_done", NORM, t + 1))
                    V.scalar_tensor_tensor(yb, bank[:, b, 0:D], unscale[:, bass.ds(t, 1)], Z[:, t, 0:D],
                                           ALU.mult, ALU.add).then_inc(sem("acc_read"), 1)
                    dve.wait_ge(*at("prod_ready", NORM, t + 1))
                    V.scalar_tensor_tensor(yc, bank[:, 5, 0:D], deg_root[:, bass.ds(t, 1)], b_sb[:, :],
                                           ALU.mult, ALU.add).then_inc(sem("prod_read"), 1)
                    dve.wait_ge(*at("prod_read", NORM, t + 1))
                    link(V.scalar_tensor_tensor(y, yc, 0.0, X[:, t, :], ALU.max, ALU.add))
                    norm_ready(NORM, link, y)
                    if not isinstance(i, int):
                        dve.wait_ge(sem(f"out_done{b}"), 16 * i)
                    norm_rows(NORM, link, t, xs4[:, b, :], y, "rows_ready")
                    assert link.n == OUT_STEPS, link.n

            out_pair(0)
            with dve.Fori(1, T // 2) as i:
                out_pair(i)


_INS = ["x", "adj", "L1_gnn_W", "L2_gnn_W1", "L2_gnn_W2", "L2_gnn_W3", "L2_gnn_W4", "L2_gnn_W5", "L2_gnn_W6",
        "L3_gnn_W", "L3_gnn_b"]


def kernel(**inputs):
    import numpy as np
    import concourse.bacc as bacc
    from concourse.bass_utils import run_bass_kernel_spmd

    laid = {name: np.ascontiguousarray(inputs[name]) for name in _INS}
    laid["L3_gnn_W"] = np.ascontiguousarray(laid["L3_gnn_W"].T)
    laid["L3_gnn_b"] = np.ascontiguousarray(np.broadcast_to(laid["L3_gnn_b"], (P, laid["L3_gnn_b"].shape[0])))

    nc = bacc.Bacc("TRN2", target_bir_lowering=False, num_devices=1)
    arrays = {f"in_{n}": a for n, a in laid.items()}
    args = [nc.dram_tensor(f"in_{n}", a.shape, mybir.dt.from_np(a.dtype), kind="ExternalInput").ap()
            for n, a in laid.items()]
    out = nc.dram_tensor("out", laid["x"].shape, F32, kind="ExternalOutput").ap()
    build(nc, *args, out)
    result = run_bass_kernel_spmd(nc, [arrays], core_ids=[0])
    return result.results[0]["out"]
```

```python
from contextlib import ExitStack

import concourse.bass as bass
from concourse import mybir

ALU = mybir.AluOpType
ACT = mybir.ActivationFunctionType
AX = mybir.AxisListType
F32 = mybir.dt.float32
F16 = mybir.dt.float16
BF16 = mybir.dt.bfloat16
I32 = mybir.dt.int32

P = 128
LN_EPS = 1e-5
NORM_EPS = 1e-12
EPS = 1e-10
CLIP = 1.0 - 1e-7
TOP = 2.0 ** 14
TINY = 2.0 ** -100
LEAST = 2.0 ** -14
EXPONENT = 0x7F800000

NORMED = 2.0 ** 10

SLOTS = 4
KEPT = 3
GK = 8
MOB, G1, G2, G3, G4, G5, G6, NORM = range(8)
NAMES = ["mob", "g1", "g2", "g3", "g4", "g5", "g6", "norm"]


class Chain:

    def __init__(self, eng, sem, base=0):
        self.eng, self.sem, self.base, self.n = eng, sem, base, 0

    def __call__(self, ins):
        ins.then_inc(self.sem, 1)
        self.n += 1
        self.eng.wait_ge(self.sem, self.base + self.n)


def build(nc, x, adj, w_mob, w1, w2, w3, w4, w5, w6, w_norm_t, b_rows, out):
    N, D = x.shape
    T = N // P
    K = N // P
    NG = K // GK
    GROUPS = T // SLOTS
    H = w1.shape[1]
    H2 = w3.shape[1]
    WZ = D + 2
    WIDTH = {MOB: D, G1: H, G2: H, G3: H2, G4: H2, G5: H, G6: H, NORM: D}
    CHUNKS = T // 4

    ctx = ExitStack()
    with ctx:
        def sb(name, shape, dt=F32):
            return ctx.enter_context(nc.sbuf_tensor(name, shape, dt))

        made = {}

        def sem(name):
            if name not in made:
                made[name] = ctx.enter_context(nc.semaphore(name))
            return made[name]

        def total(name, stage):
            turning = ("inc", MOB, NORM)
            if name in ("z_max_ready", "z_max_turned"):
                return 0 if stage == G1 else 1
            if name in ("z_pair_ready", "z_pair_sent", "z_scale_ready"):
                return 1
            if name == "z_high_done":
                return {"inc": CHUNKS, MOB: CHUNKS + 1}.get(stage, 0)
            if name == "z_low_done":
                return {"inc": CHUNKS, MOB: CHUNKS}.get(stage, 0)
            if name == "z_split":
                return 0 if stage in ("inc", MOB) else T
            if name == "x_kept" and stage == MOB:
                return GROUPS
            if name == "dve_scales":
                return {"inc": 0, MOB: 0, G1: 4}.get(stage, 5)
            if name == "dve_conv":
                return CONV_STEPS.get(stage, 0) * T
            given = {
                "acc_read": ("inc", *range(8)), "agg_done": tuple(range(8)), "half_used": tuple(range(8)),
                "xs_ready": ("inc", MOB), "xp_ready": turning, "rows_ready": (G6, NORM),
                "xT_ready": turning, "xs_turned": turning, "x_kept": ("inc", MOB, G6),
                "prod_ready": (*turning, G4), "prod_read": (*turning, G3, G4, G5),
                "var_ready": ("inc", G6, NORM), "dev_ready": ("inc", G6, NORM),
                "half_ready": (G1, G2, G3, G4, G5, G6), "rT_ready": (G1, G2, G4, G6),
                "r_turned": (G1, G2, G4, G6), "small_ready": (G1, G2, G4, G6), "small_read": (G1, G2, G4, G6),
                "z_turned": (G4,), "zT_ready": (G4,),
            }[name]
            return T if stage in given else 0

        def at(name, stage, value):
            early = name[:2] == "z_" and name != "z_split" or name == "dve_scales"
            before = ["inc", MOB, G1, NORM, G2, G3, G4, G5, G6] if early else ["inc", *range(8)]
            return sem(name), sum(total(name, s) for s in before[:before.index(stage)]) + value

        CONV_STEPS = {G1: 1, G2: 1, G3: 2, G4: 1, G5: 2, G6: 4}
        pairs_dram = nc.dram_tensor("adj_pairs", [T, P, K * 2 * P], F16, kind="Internal").ap()

        x_dram = nc.dram_tensor("x_rows_out", [GROUPS, P, SLOTS * D], F32, kind="Internal").ap()

        bank = ctx.enter_context(nc.psum_tensor("bank", [P, 8, 512], F32))

        X = sb("X", [P, T, D])
        Z = sb("Z", [P, T, WZ])
        ZP = sb("ZP", [P, T * 2 * WZ], F16)
        TILE = K * 2 * P
        ARENA = 5 * TILE
        arena = sb("arena", [P, ARENA], F16)
        RAW = arena[:, 0:4 * N].bitcast(F32).rearrange("p (b n) -> p b n", b=2)
        ROWS = arena[:, 4 * N:7 * N].rearrange("p (c n) -> p c n", c=3)
        PAIR = arena[:, 7 * N:9 * N].rearrange("p (g k h i) -> p g k h i", g=NG, k=GK, h=2)
        MASK = arena[:, 9 * N:10 * N].rearrange("p (g k i) -> p g k i", g=NG, k=GK)

        STAY = arena[:, 0:T * KEPT * 2 * P].rearrange("p (t k h i) -> p t k h i", k=KEPT, h=2, i=P)
        RING = arena[:, T * KEPT * 2 * P:(T * KEPT + 2 * (K - KEPT)) * 2 * P].rearrange(
            "p (s k h i) -> p s k h i", s=2, h=2, i=P)
        ZB = Z[:, :, :].rearrange("p t f -> p (t f)").bitcast(F16)
        SPARES = [place[:, T * 2 * H:T * 2 * H + T * 2 * P].rearrange("p (t h i) -> p t h i", h=2, i=P)
                  for place in (ZP, ZB)]
        XH = X[:, :, :].rearrange("p t f -> p (t f)").bitcast(F16)
        SPARES += [XH[:, n * T * 2 * P:(n + 1) * T * 2 * P].rearrange("p (t h i) -> p t h i", h=2, i=P)
                   for n in range(2)]

        def kept(stage):
            return KEPT + {MOB: 0, G1: 1, G2: 3, G3: 4, G4: 4, G5: 4, G6: 1, NORM: 1}[stage]

        def streamed(stage, half):
            return (kept(stage), K // 2 + 1) if half == 0 else (K // 2 + 1, K)

        LATE = Z[:, :, :].rearrange("p t f -> p (t f)")[:, T * WZ - (2 * D + H) * (D // P):]
        wmob_sb, wnorm_sb, w1_sb = (LATE[:, a * (D // P):z * (D // P)].rearrange("p (c f) -> p c f", c=D // P)
                                    for a, z in ((0, D), (D, 2 * D), (2 * D, 2 * D + H)))
        w2_sb = sb("w2_sb", [P, H])
        w3_sb = sb("w3_sb", [P, H2])
        w4_sb = sb("w4_sb", [H2, H])
        w5_sb = sb("w5_sb", [P, H])
        w6_sb = sb("w6_sb", [P, D])
        b_sb = sb("b_sb", [P, D])
        ident = sb("ident", [P, P])
        ident16 = sb("ident16", [P, P], F16)
        ones = sb("ones", [3, P])
        wp_mob = sb("wp_mob", [P, D // P, 2, D], F16)
        wp1 = sb("wp1", [P, D // P, 2, H], F16)
        wp_norm = sb("wp_norm", [P, D // P, 2, D], F16)
        w_top = sb("w_top", [3, 4])
        w_diag = sb("w_diag", [3, 6])
        w_scales = sb("w_scales", [P, 6])
        w_back = sb("w_back", [P, 2])
        row_factor = sb("row_factor", [P, T])
        out_factor = sb("out_factor", [P, T])
        xp4 = sb("xp4", [P, 4, 2, D], F16)

        abs_parts = sb("abs_parts", [P, T, NG])
        sum_parts = sb("sum_parts", [P, T, NG])
        count_parts = sb("count_parts", [P, T, NG])
        count = sb("count", [P, T])
        root_count = sb("root_count", [P, T])
        row_scale = sb("row_scale", [P, T])
        row_inv = sb("row_inv", [P, T])
        row_sum = sb("row_sum", [P, T])
        x_sq = sb("x_sq", [P, T])
        m_sq = sb("m_sq", [P, T])
        z_bound = sb("z_bound", [P, T])
        unscales = sb("unscales", [P, 2, T])
        unscale_norm = sb("unscale_norm", [P, T])
        norm_factor = sb("norm_factor", [P, T])
        inv_degree = sb("inv_degree", [P, T])
        w_tops = sb("w_tops", [P, 11])
        row_top = sb("row_top", [P, 1])
        least = sb("least", [P, 1], F16)
        ones_col = sb("ones_col", [P, 1])
        w_sums = sb("w_sums", [1, 8])
        gains = sb("gains", [1, 8])
        z_factor = sb("z_factor", [P, T])
        gamma1 = sb("gamma1", [P, T])
        deg_root = sb("deg_root", [P, T])
        norm_bound = sb("norm_bound", [P, T])
        z_max = sb("z_max", [P, 1])
        x_max = sb("x_max", [P, 8])
        z_top = sb("z_top", [1, 4])
        z_pair = sb("z_pair", [1, 2])
        z_scale = sb("z_scale", [P, 2])
        z_keep = sb("z_keep", [P, 1])
        stat = sb("stat", [P, 16])
        roots_in = sb("roots_in", [P, 3, T])
        roots = sb("roots", [P, 3, T])
        bt = sb("bt", [P, 10, T])
        gt = sb("gt", [P, 24, SLOTS])
        y4 = sb("y4", [P, SLOTS, D])
        xs4 = sb("xs4", [P, SLOTS, D])
        y = y4[:, 0, :]
        xs = xs4[:, 0, :]
        half = y4[:, 1, 0:H]
        r = y4[:, 2, 0:H]
        z4 = y4[:, 3, 0:H]
        xd = y4[:, 3, :]
        yb = y4[:, 1, :]
        yc = y4[:, 2, :]
        junk_abs = [y4[:, 2:4, :].rearrange("p s f -> p (s f)").bitcast(BF16),
                    xs4[:, 2:4, :].rearrange("p s f -> p (s f)").bitcast(BF16)]
        bn6 = sb("bn6", [P, SLOTS, 6])
        mv = sb("mv", [P, SLOTS, 2])
        xT = sb("xT", [P, D])
        junk_sq = sb("junk_sq", [P, 2, D], BF16)
        USED = (T * KEPT + 2 * (K - KEPT)) * 2 * P
        junk_mob = arena[:, USED:USED + SLOTS * D].bitcast(BF16).rearrange("p (s f) -> p s f", f=D)
        zT = arena[:, USED + SLOTS * D:USED + SLOTS * D + 2 * D].bitcast(F32)

        TURNED = [[bank[:, 3 * u + c, :].bitcast(F16) for c in range(2)] for u in range(2)]
        SUMS = [bank[:, 6, :], bank[:, 5, :]]

        def turned_pairs(place):
            return place[:, 0:D].bitcast(F16).rearrange("p (h c i) -> p h c i", h=2, i=P)

        x_rows = x.rearrange("(t p) f -> p t f", p=P)
        adj_rows = adj.rearrange("(t p) n -> t p n", p=P)
        out_rows = out.rearrange("(t p) f -> t p f", p=P)

        def zp_view(stage):
            w = WZ if stage == MOB else (D if stage == "inc" else WIDTH[stage])
            place = ZB if stage in (G1, G3, G5, NORM) else ZP
            return place[:, 0:T * 2 * w].rearrange("p (t h f) -> p t h f", h=2, f=w)

        def unscale_of(stage):
            return unscale_norm if stage == NORM else unscales[:, stage % 2, :]

        block = ctx.enter_context(nc.Block())

        @block.sync
        def _(sp):
            def load_rows(t, b, g):
                sp.dma_start(RAW[:, b, g * GK * P:(g + 1) * GK * P],
                             adj_rows[t, :, g * GK * P:(g + 1) * GK * P]).then_inc(sem(f"raw_in{b}{g}"), 16)

            for g in range(NG):
                load_rows(0, 0, g)
            for c in range(4):
                part = slice(c * T // 4, (c + 1) * T // 4)
                sp.dma_start(X[:, part, :], x_rows[:, part, :]).then_inc(sem(f"x_in{c}"), 16)
            for g in range(NG):
                load_rows(1, 1, g)
            for dst, src in ((wmob_sb[:, :, :], w_mob.rearrange("(c p) f -> p c f", p=P)),
                             (w1_sb[:, :, :], w1.rearrange("(c p) f -> p c f", p=P)),
                             (w2_sb[:, :], w2), (w3_sb[:, :], w3), (w4_sb[:, :], w4), (w5_sb[:, :], w5),
                             (w6_sb[:, :], w6), (wnorm_sb[:, :, :], w_norm_t.rearrange("(c p) f -> p c f", p=P)),
                             (b_sb[:, :], b_rows)):
                sp.dma_start(dst, src).then_inc(sem("weights_in"), 16)
            for g in range(NG):
                sp.wait_ge(sem("rows_split"), g + 1)
                sp.wait_ge(sem("row_sums_done"), g + 1)
                load_rows(2, 0, g)

            def pair_of_tiles(i):
                for b in range(2):
                    t = 2 * i + b
                    for g in range(NG):
                        n = NG * t + g
                        sp.wait_ge(sem("pairs_done"), n + 1)
                        sp.dma_start(pairs_dram[t, :, g * GK * 2 * P:(g + 1) * GK * 2 * P],
                                     PAIR[:, g, :, :, :].rearrange("p k h i -> p (k h i)")).then_inc(
                                         sem(f"pairs_stored{g}"), 16)
                        if not (isinstance(t, int) and t + 3 >= T):
                            sp.wait_ge(sem("rows_split"), n + NG + 1)
                            sp.wait_ge(sem("row_sums_done"), n + NG + 1)
                            load_rows(t + 3, 1 - b, g)

            pair_of_tiles(0)
            with sp.Fori(1, T // 2 - 2) as i:
                pair_of_tiles(i)
            pair_of_tiles(T // 2 - 2)
            pair_of_tiles(T // 2 - 1)

            sp.wait_ge(sem("group_used"), NG * T)
            for g in range(NG):
                sp.wait_ge(sem(f"pairs_stored{g}"), 16 * T)

            def load_half(stage, t, s, half):
                a, z = streamed(stage, half)
                sp.dma_start(RING[:, s % 2, a - KEPT:z - KEPT, :, :].rearrange("p k h i -> p (k h i)"),
                             pairs_dram[t, :, a * 2 * P:z * 2 * P]).then_inc(sem(f"ring_in{s % 2}{half}"), 16)

            def load_kept(c):
                tiles = slice(c * T // 4, (c + 1) * T // 4)
                sp.dma_start(STAY[:, tiles, :, :, :].rearrange("p t k h i -> p t (k h i)"),
                             pairs_dram[tiles, :, 0:KEPT * 2 * P].rearrange("t p f -> p t f")).then_inc(
                                 sem("kept_in"), 16)

            load_kept(0)
            for stage in range(8):
                def load_spare(n):
                    sp.dma_start(SPARES[n].rearrange("p t h i -> p t (h i)"),
                                 pairs_dram[:, :, (KEPT + n) * 2 * P:(KEPT + n + 1) * 2 * P].rearrange(
                                     "t p f -> p t f")).then_inc(sem(f"spare_in{n}"), 16)

                def load_x(c):
                    groups = slice(c * GROUPS // 4, (c + 1) * GROUPS // 4)
                    sp.dma_start(X[:, c * T // 4:(c + 1) * T // 4, :].rearrange("p (g s) f -> p g (s f)", s=SLOTS),
                                 x_dram[groups].rearrange("g p f -> p g f")).then_inc(sem(f"x_back{c}"), 16)

                if stage == G1:
                    sp.wait_ge(*at("agg_done", MOB, T))
                    load_spare(0)

                def load_group(g):
                    for s in range(SLOTS):
                        t = SLOTS * g + s
                        for half in range(2):
                            used = ("half_used", "agg_done")[half]
                            if not (isinstance(g, int) and s < 2):
                                sp.wait_ge(*at(used, stage, t - 1))
                            elif stage > 0:
                                sp.wait_ge(*at(used, stage - 1, T - 1 + s))
                            load_half(stage, t, s, half)
                        if stage == MOB and isinstance(g, int) and s == 1:
                            for c in range(1, 4):
                                load_kept(c)
                        if stage == G6 and isinstance(g, int):
                            if s == 0:
                                sp.wait_ge(sem("x_stored"), 16 * GROUPS)
                                sp.wait_ge(*at("agg_done", G5, T))
                            load_x(s)

                def load_spare_group(n, g):
                    tiles = bass.ds(SLOTS * g, SLOTS)
                    sp.dma_start(SPARES[n][:, tiles, :, :].rearrange("p t h i -> p t (h i)"),
                                 pairs_dram[tiles, :, (KEPT + n) * 2 * P:(KEPT + n + 1) * 2 * P].rearrange(
                                     "t p f -> p t f")).then_inc(sem(f"spare_in{n}"), 16)

                filled = {G1: (1, 2), G2: (3,)}.get(stage, ())
                load_group(0)
                if stage == G1:
                    sp.wait_ge(*at("z_split", G1, T))
                for n in filled:
                    load_spare_group(n, 0)
                with sp.Fori(1, GROUPS) as g:
                    load_group(g)
                    for n in filled:
                        load_spare_group(n, g)

        @block.tensor
        def _(pe):
            def turn(dst, src):
                return pe.transpose(dst, src, ident[:, :])

            def turn_max(stage):
                pe.wait_ge(*at("z_max_ready", stage, 1))
                turn(bank[0:1, 7, 0:P], z_max[:, :]).then_inc(sem("z_max_turned"), 1)

            def send_scale(stage):
                pe.wait_ge(*at("z_pair_ready", stage, 1))
                pe.matmul(bank[:, 7, 256:258], ones[0:1, :], z_pair[:, :], start=True, stop=True).then_inc(
                    sem("z_pair_sent"), 1)

            def scale_read(stage):
                pe.wait_ge(*at("z_scale_ready", stage, 1))

            zp0 = zp_view("inc")

            def turn_group(n, g):
                pe.wait_ge(sem("rows_split"), n + 1)
                if not (isinstance(n, int) and n < 2):
                    pe.wait_ge(sem("pairs_done"), n - 1)
                for c in range(2):
                    for kk in range(GK):
                        mm = pe.transpose(TURNED[g % 2][c][:, kk * P:(kk + 1) * P],
                                          ROWS[:, c, (g * GK + kk) * P:(g * GK + kk + 1) * P], ident16[:, :])
                mm.then_inc(sem("turned"), 1)

            def multiply_group(t, b, g):
                n = NG * t + g
                pe.wait_ge(sem("pairs_done"), n + 1)
                pe.wait_ge(sem("mask_done"), n + 1)
                if g == 0 and not (isinstance(t, int) and t < 2):
                    pe.wait_ge(*at("acc_read", "inc", t - 1))
                for kk in range(GK):
                    k = g * GK + kk
                    if isinstance(t, int) and t == 0 and k % 4 == 0:
                        pe.wait_ge(*at("z_low_done", "inc", k // 4 + 1))
                    a, z = k == 0, k == K - 1

                    def mm(side, lhs, rhs, start=False, stop=False):
                        return pe.matmul(SUMS[b][:, side * D:(side + 1) * D], lhs, rhs, start=start, stop=stop,
                                         skip_group_check=True)

                    mm(0, PAIR[:, g, kk, 0, :], zp0[:, k, 0, :], start=a)
                    mm(0, PAIR[:, g, kk, 0, :], zp0[:, k, 1, :])
                    mm(0, PAIR[:, g, kk, 1, :], zp0[:, k, 0, :], stop=z)
                    mm(1, MASK[:, g, kk, :], zp0[:, k, 0, :])
                    last = mm(1, MASK[:, g, kk, :], zp0[:, k, 1, :], stop=z)
                last.then_inc(sem("group_used"), 1)

            def turn_x(stage, t, src, b):
                pe.wait_ge(*at("xp_ready", stage, t + 1))
                pe.wait_ge(*at("xT_ready", stage, t))
                pe.sem_inc(sem("pe_marks"), 1)
                for h in range(2):
                    for c in range(D // P):
                        mm = pe.transpose(turned_pairs(b)[:, h, c, :], src[:, h, c * P:(c + 1) * P], ident16[:, :])
                mm.then_inc(sem("xs_turned"), 1)

            def product_x(stage, t, src, w, width, b):
                pe.wait_ge(*at("xT_ready", stage, t + 1))
                pe.wait_ge(*at("prod_read", stage, t))
                pairs = turned_pairs(src)
                for c in range(D // P):
                    for h, hw in ((0, 0), (0, 1), (1, 0)):
                        mm = pe.matmul(b[:, 0:width], pairs[:, h, c, :], w[:, c, hw, :], start=c + h + hw == 0,
                                       stop=c == D // P - 1 and h == 1)
                mm.then_inc(sem("prod_ready"), 1)

            def pair_of_tiles(i):
                for b in range(2):
                    t = 2 * i + b
                    for g in range(NG):
                        n = NG * t + g
                        if not (isinstance(n, int) and n + 2 >= NG * T):
                            turn_group(n + 2, (g + 2) % NG)
                        if g == 2 and not (isinstance(t, int) and t == 0):
                            turn_x("inc", t - 1, xp4[:, 0, :, :], bank[:, 7, 0:D])
                        multiply_group(t, b, g)
                        if isinstance(t, int) and t == 0:
                            if g == 3:
                                pe.wait_ge(sem("w_max_ready"), 1)
                                turn(bank[0:3, 2, 0:P], w_tops[:, 8:11]).then_inc(sem("w_turned"), 1)
                            continue
                        if isinstance(t, int) and t == 1 and g == 1:
                            pe.wait_ge(sem("w_diag_ready"), 1)
                            pe.matmul(bank[:, 2, 264:270], ones[:, :], w_diag[:, :], start=True,
                                      stop=True).then_inc(sem("w_sent"), 1)
                        late = isinstance(t, int) and t == 1
                        if late and g == 3:
                            pe.wait_ge(sem("w_pairs_ready"), 1)
                        if g == (3 if late else 2):
                            product_x("inc", t - 1, xT, wp_mob, D, bank[:, 7, D:2 * D])

            pe.wait_ge(sem("ident_ready"), 3)
            turn_group(0, 0)
            turn_group(1, 1)
            turn_max("inc")
            send_scale("inc")
            pe.wait_ge(sem("weights_in"), 16 * 9)
            pair_of_tiles(0)
            with pe.Fori(1, T // 2 - 1) as i:
                pair_of_tiles(i)
            pair_of_tiles(T // 2 - 1)
            turn_x("inc", T - 1, xp4[:, 0, :, :], bank[:, 7, 0:D])
            product_x("inc", T - 1, xT, wp_mob, D, bank[:, 7, D:2 * D])

            def small_turn(stage, t, w):
                pe.wait_ge(*at("acc_read", stage, t + 1))
                pe.wait_ge(*at("rT_ready", stage, t))
                pe.sem_inc(sem("pe_marks"), 1)
                turn(bank[0:w, 6, 0:P], r[:, 0:w]).then_inc(sem("r_turned"), 1)

            def small_product(stage, t, w, weights, wo):
                pe.wait_ge(*at("rT_ready", stage, t + 1))
                pe.wait_ge(*at("small_read", stage, t))
                pe.matmul(bank[:, 7, 0:wo], xT[0:w, 0:P], weights, start=True, stop=True).then_inc(
                    sem("small_ready"), 1)

            def turn_z4(stage, t):
                pe.wait_ge(*at("small_read", stage, t + 1))
                pe.wait_ge(*at("zT_ready", stage, t))
                turn(bank[:, 4, 0:P], z4[:, :]).then_inc(sem("z_turned"), 1)

            def product_z4(stage, t):
                pe.wait_ge(*at("zT_ready", stage, t + 1))
                pe.wait_ge(*at("prod_read", stage, t))
                pe.matmul(bank[:, 5, 0:H], zT[:, 0:P], w5_sb[:, :], start=True, stop=True).then_inc(
                    sem("prod_ready"), 1)

            def after(stage, t):
                if stage in (G1, G2):
                    weights, wo = (w2_sb[:, :], H) if stage == G1 else (w3_sb[:, :], H2)
                    return [(12, lambda: small_turn(stage, t, H)),
                            (19, lambda: small_product(stage, t, H, weights, wo))]
                if stage == G4:
                    return [(10, lambda: small_turn(stage, t, H2)),
                            (17, lambda: small_product(stage, t, H2, w4_sb[:, :], H)),
                            (24, lambda: turn_z4(stage, t)), (31, lambda: product_z4(stage, t))]
                if stage == G6:
                    return [(12, lambda: small_turn(stage, t, H)),
                            (19, lambda: small_product(stage, t, H, w6_sb[:, :], D))]
                if stage == NORM:
                    return [(8, lambda: turn_x(stage, t, xp4[:, 0, :, :], bank[:, 4, :])),
                            (16, lambda: product_x(stage, t, zT, wp_norm, D, bank[:, 5, :]))]
                return []

            def after_group(g):
                steps = []
                for s in range(SLOTS):
                    t = SLOTS * g + s
                    steps.append((8 * s + 2, lambda t=t, s=s: turn_x(MOB, t, xp4[:, s, :, :], bank[:, 6, :])))
                    steps.append((8 * s + 6, lambda t=t: product_x(MOB, t, xT, wp1, H, bank[:, 7, :])))
                return steps

            def sum_tops():
                pe.wait_ge(sem("tops_ready"), 1)
                turn(bank[0:1, 7, 0:P], row_top[:, :])
                pe.matmul(bank[0:1, 7, 384:392], ones_col[:, :], w_tops[:, 0:8], start=True, stop=True).then_inc(
                    sem("tops_sent"), 1)

            def aggregate(stage, g, s, steps, fresh=False, ks=(0, K)):
                t = SLOTS * g + s
                w = WIDTH[stage]
                zp = zp_view(stage)
                if stage == MOB:
                    acc = bank[:, s, 0:D + 1]
                    if not isinstance(g, int):
                        pe.wait_ge(*at("acc_read", stage, t + 1 - SLOTS))
                else:
                    acc = bank[:, s % 2, :]
                    if ks[0] == 0:
                        pe.wait_ge(*at("acc_read", stage, t - 1))
                halves = [streamed(stage, half)[0] for half in range(2)]
                for k in range(*ks):
                    if fresh and k == 0 and stage == MOB:
                        pe.wait_ge(sem("kept_in"), 16 * 4)
                    if fresh and k == KEPT and stage == G1:
                        pe.wait_ge(sem("spare_in0"), 16)
                    if fresh and k == KEPT + 1 and stage == G2:
                        pe.wait_ge(sem("spare_in1"), 16 * GROUPS)
                        pe.wait_ge(sem("spare_in2"), 16 * GROUPS)
                    if fresh and k == KEPT + 3 and stage == G3:
                        pe.wait_ge(sem("spare_in3"), 16 * GROUPS)
                    if k in halves:
                        pe.wait_ge(sem(f"ring_in{s % 2}{halves.index(k)}"),
                                   16 * (T // 2 * stage + 1) + 16 * (2 * g + s // 2))
                    for when, step in steps:
                        if when == k:
                            step()
                    if fresh and stage == MOB and k % 4 == 0:
                        pe.wait_ge(*at("z_low_done", stage, k // 4 + 1))
                    if fresh and stage != MOB:
                        pe.wait_ge(*at("z_split", stage, k + 1))
                    a, z = k == 0, k == K - 1
                    if k < KEPT:
                        high, low = STAY[:, t, k, 0, :], STAY[:, t, k, 1, :]
                    elif k < kept(stage):
                        high, low = SPARES[k - KEPT][:, t, 0, :], SPARES[k - KEPT][:, t, 1, :]
                    else:
                        high, low = RING[:, s % 2, k - KEPT, 0, :], RING[:, s % 2, k - KEPT, 1, :]
                    if stage in (MOB, NORM):
                        n = D + 1 if stage == MOB else D
                        pe.matmul(acc[:, 0:n], high, zp[:, k, 0, 0:n], start=a, stop=False)
                        pe.matmul(acc[:, 0:n], high, zp[:, k, 1, 0:n], start=False, stop=False)
                        mm = pe.matmul(acc[:, 0:n], low, zp[:, k, 0, 0:n], start=False, stop=z)
                    else:
                        pe.matmul(acc[:, 0:2 * w], high, zp[:, k, :, :].rearrange("p h f -> p (h f)"),
                                  start=a, stop=False, skip_group_check=True)
                        mm = pe.matmul(acc[:, w:2 * w], low, zp[:, k, 0, :], start=False, stop=z,
                                       skip_group_check=True)
                    if k == K // 2:
                        mm.then_inc(sem("half_used"), 1)
                if ks[1] == K:
                    mm.then_inc(sem("agg_done"), 1)

            def first_group(stage):
                if stage == MOB:
                    extra = {2: [(4, sum_tops), (16, lambda: send_scale(G1)), (24, lambda: scale_read(G1))],
                             3: [(4, lambda: turn_max(NORM)), (16, lambda: send_scale(NORM)), (24, lambda: scale_read(NORM))]}
                    for k in range(K):
                        aggregate(stage, 0, 0, [], fresh=True, ks=(k, k + 1))
                        aggregate(stage, 0, 1, [], ks=(k, k + 1))
                    for s in range(2, SLOTS):
                        aggregate(stage, 0, s, extra[s])
                    return
                if stage == G1:
                    ready = K - SLOTS
                    aggregate(stage, 0, 0, [], fresh=True, ks=(0, ready))
                    aggregate(stage, 0, 1, [], ks=(0, ready))
                    steps = [step for _, step in after_group(GROUPS - 1)]
                    for n in (0, 2, 1, 4, 3, 6, 5, 7):
                        steps[n]()
                    aggregate(stage, 0, 0, [], fresh=True, ks=(ready, K))
                    aggregate(stage, 0, 1, [], ks=(ready, K))
                    turned, product = (step for _, step in after(stage, 0))
                    turned1, product1 = (step for _, step in after(stage, 1))
                    aggregate(stage, 0, 2, [(4, lambda: turn_max(G2)), (7, turned), (10, lambda: send_scale(G2)),
                                            (13, lambda: scale_read(G2)), (13, product), (19, turned1), (25, product1)])
                    aggregate(stage, 0, 3, after(stage, 2))
                    return
                for s in range(SLOTS):
                    steps = list(after(stage - 1, T - 1) if s == 0 else after(stage, s - 1))
                    if s == 1 and stage < G6:
                        steps += [(3, lambda: turn_max(stage + 1)), (10, lambda: send_scale(stage + 1)),
                                  (12, lambda: scale_read(stage + 1))]
                    aggregate(stage, 0, s, steps, fresh=s == 0)

            pe.wait_ge(sem("w_pairs_ready"), 3)
            turn_max(MOB)
            send_scale(MOB)
            for stage in range(8):
                first_group(stage)
                with pe.Fori(1, GROUPS) as g:
                    for s in range(SLOTS):
                        if stage == MOB:
                            steps = after_group(g - 1) if s == SLOTS - 1 else []
                        else:
                            steps = after(stage, SLOTS * g + s - 1)
                        aggregate(stage, g, s, steps)
            for _, step in after(NORM, T - 1):
                step()

        @block.gpsimd
        def _(pool):
            nc.gpsimd.memset(ident[:, :], 0.0).then_inc(sem("ident_zero"), 1)
            nc.gpsimd.memset(ones_col[:, :], 1.0)
            nc.gpsimd.memset(least[:, :], LEAST)
            nc.gpsimd.memset(ones[:, :], 1.0).then_inc(sem("ident_ready"), 1)
            pool.wait_ge(sem("ident_zero"), 1)
            nc.gpsimd.affine_select(out=ident[:, :], in_=ident[:, :], compare_op=ALU.not_equal, fill=1.0,
                                    base=0, pattern=[[-1, P]], channel_multiplier=1).then_inc(sem("ident_ready"), 1)
            pool.wait_ge(sem("ident_ready"), 2)
            nc.gpsimd.tensor_copy(ident16[:, :], ident[:, :]).then_inc(sem("ident_ready"), 1)
            def write_mask(n, g):
                pool.wait_ge(sem("high_turned"), n + 1)
                if not (isinstance(n, int) and n < NG):
                    pool.wait_ge(sem("group_used"), n + 1 - NG)
                pool.sem_inc(sem("pool_marks"), 1)
                nc.gpsimd.tensor_scalar(MASK[:, g, :, :], PAIR[:, g, :, 0, :], 0.0, None, ALU.is_gt).then_inc(
                    sem("mask_done"), 1)

            write_mask(0, 0)
            write_mask(1, 1)

            def split_weights(n):
                w_sb, wp = ((wmob_sb, wp_mob), (w1_sb, wp1), (wnorm_sb, wp_norm))[n]
                pool.wait_ge(sem("w_scale_ready"), 1)
                nc.gpsimd.tensor_scalar(w_sb[:, :, :], w_sb[:, :, :], w_scales[:, n:n + 1], None,
                                        ALU.mult).then_inc(sem("w_scaled"), 1)
                pool.wait_ge(sem("w_scaled"), n + 1)
                nc.gpsimd.tensor_copy(wp[:, :, 0, :], w_sb[:, :, :]).then_inc(sem("w_high_done"), 1)
                pool.wait_ge(sem("w_high_done"), n + 1)
                nc.gpsimd.tensor_tensor(wp[:, :, 1, :], w_sb[:, :, :], wp[:, :, 0, :], ALU.subtract).then_inc(
                    sem("w_pairs_ready"), 1)

            def keep_rows(t):
                pool.wait_ge(*at("xs_ready", "inc", t + 1))
                nc.gpsimd.tensor_copy(X[:, t, :], xs).then_inc(sem("x_kept"), 1)

            def pair_of_tiles(i):
                for b in range(2):
                    t = 2 * i + b
                    fixed = isinstance(t, int)
                    for g in range(NG):
                        if not (fixed and NG * t + g + 2 >= NG * T):
                            write_mask(NG * t + g + 2, (g + 2) % NG)
                        if fixed and (t, g) == (1, 2):
                            split_weights(0)
                        if g == 2 and not (fixed and t == 0):
                            keep_rows(t - 1)

            pair_of_tiles(0)
            split_weights(1)
            pair_of_tiles(1)
            split_weights(2)
            with pool.Fori(2, T // 2 - 1) as i:
                pair_of_tiles(i)
            pair_of_tiles(T // 2 - 1)
            keep_rows(T - 1)
            with pool.Fori(0, GROUPS) as g:
                pool.wait_ge(sem("x_stored"), 16 * g + 16)
                pool.sem_inc(sem("x_kept"), 1)
            with pool.Fori(0, T) as t:
                pool.wait_ge(*at("rows_ready", G6, t + 1))
                nc.gpsimd.tensor_copy(X[:, t, :], xs).then_inc(sem("x_kept"), 1)

        @block.scalar
        def _(act):
            def A(*args, **kw):
                return nc.scalar.activation(*args, **kw)

            def A_at(*args, **kw):
                act.sem_inc(sem("act_marks"), 1)
                return A(*args, **kw)

            def split_high(stage, src):
                zp = zp_view(stage)
                w = zp.shape[3]
                act.wait_ge(*at("z_scale_ready", stage, 1))
                for c in range(CHUNKS):
                    A(zp[:, 4 * c:4 * c + 4, 0, :], src[:, 4 * c:4 * c + 4, 0:w], ACT.Copy,
                      scale=z_scale[:, 0:1]).then_inc(sem("z_high_done"), 1)

            def sum_magnitudes(t, i, b, g):
                act.wait_ge(sem(f"raw_in{b}{g}"), 16 * i + 16)
                if not (isinstance(t, int) and NG * t + g == 0):
                    act.wait_ge(sem("magnitudes"), NG * t + g)
                A_at(junk_abs[0], RAW[:, b, g * GK * P:(g + 1) * GK * P], ACT.Abs,
                     accum_out=abs_parts[:, t, g:g + 1]).then_inc(sem("magnitudes"), 1)

            def sum_rows(t, b, g):
                act.wait_ge(sem("row_scale_ready"), t + 1)
                if not (isinstance(t, int) and NG * t + g == 0):
                    act.wait_ge(sem("row_sums_done"), NG * t + g)
                A_at(junk_abs[1], RAW[:, b, g * GK * P:(g + 1) * GK * P], ACT.Copy,
                     scale=row_scale[:, bass.ds(t, 1)], accum_out=sum_parts[:, t, g:g + 1]).then_inc(
                         sem("row_sums_done"), 1)

            def copy_pairs(n, t, g):
                act.wait_ge(sem("turned"), n + 1)
                if not (isinstance(n, int) and n < NG):
                    act.wait_ge(sem("group_used"), n + 1 - NG)
                    act.wait_ge(sem(f"pairs_stored{g}"), 16 * t)
                for c, done in enumerate(("high_turned", "pairs_done")):
                    A(PAIR[:, g, :, c, :], TURNED[g % 2][c].rearrange("p (k i) -> p k i", i=P),
                      ACT.Copy).then_inc(sem(done), 1)

            def root_count_of(t):
                act.wait_ge(sem("counted"), t + 1)
                A_at(root_count[:, bass.ds(t, 1)], count[:, bass.ds(t, 1)], ACT.Sqrt, scale=1.0 / LEAST).then_inc(sem("count_rooted"), 1)

            def root_var(stage, t, n=1):
                act.wait_ge(*at("var_ready", stage, t + 1))
                A(stat[:, 1:2], stat[:, 0:1], ACT.Sqrt).then_inc(sem("dev_ready"), 1)

            def keep_xT(stage, t, dst, b):
                act.wait_ge(*at("xs_turned", stage, t + 1))
                act.wait_ge(*at("prod_ready", stage, t))
                A(dst[:, :].bitcast(F16), b[:, 0:D].bitcast(F16), ACT.Copy).then_inc(sem("xT_ready"), 1)

            def squares(t):
                act.wait_ge(*at("xs_ready", "inc", t + 1))
                A_at(junk_sq[:, 0, :], xs, ACT.Square, accum_out=x_sq[:, bass.ds(t, 1)]).then_inc(sem("x_squared"), 1)

            def keep_product(t):
                act.wait_ge(*at("prod_ready", "inc", t + 1))
                A_at(junk_sq[:, 1, :], bank[:, 7, D:2 * D], ACT.Square,
                     scale=w_back[:, 0:1], accum_out=m_sq[:, bass.ds(t, 1)]).then_inc(sem("m_squared"), 1)
                A_at(Z[:, t, 0:D], bank[:, 7, D:2 * D], ACT.Copy, scale=w_back[:, 0:1]).then_inc(
                    sem("prod_read"), 1)

            def bound_x(n):
                tiles = slice(n * T // 8, (n + 1) * T // 8)
                act.wait_ge(sem(f"x_in{n // 2}"), 16)
                if n > 0:
                    act.wait_ge(sem("x_bounded"), n)
                else:
                    act.wait_ge(sem("magnitudes"), NG)
                A(junk_abs[0], X[:, tiles, :].rearrange("p t f -> p (t f)"), ACT.Abs,
                  accum_out=x_max[:, n:n + 1]).then_inc(sem("x_bounded"), 1)

            for g in range(NG):
                sum_magnitudes(0, 0, 0, g)
            for g in range(NG):
                sum_rows(0, 0, g)
            bound_x(0)
            copy_pairs(0, 0, 0)
            bound_x(1)
            copy_pairs(1, 0, 1)
            for n in range(2, 8):
                bound_x(n)
            act.wait_ge(sem("x_bounded"), 8)
            for g in range(2):
                sum_magnitudes(1, 0, 1, g)
            split_high("inc", X)
            for g in range(2, NG):
                sum_magnitudes(1, 0, 1, g)

            def pair_of_tiles(i):
                for b in range(2):
                    t = 2 * i + b
                    fixed = isinstance(t, int)
                    for g in range(NG):
                        n = NG * t + g
                        if g == 2 and not (fixed and t == 0):
                            keep_xT("inc", t - 1, xT, bank[:, 7, :])
                        if not (fixed and t + 1 >= T):
                            sum_rows(t + 1, 1 - b, g)
                        if not (fixed and n + 2 >= NG * T):
                            copy_pairs(n + 2, t + (g + 2) // NG, (g + 2) % NG)
                        if not (fixed and t + 2 >= T):
                            sum_magnitudes(t + 2, i + 1, b, g)
                        if g == 1:
                            root_count_of(t)
                        if fixed and t == 0:
                            continue
                        if g == 0:
                            root_var("inc", t - 1)
                        if g == 1:
                            squares(t - 1)
                        if g == 3:
                            keep_product(t - 1)

            pair_of_tiles(0)
            with act.Fori(1, T // 2 - 1) as i:
                pair_of_tiles(i)
            pair_of_tiles(T // 2 - 1)
            root_var("inc", T - 1)
            squares(T - 1)
            keep_xT("inc", T - 1, xT, bank[:, 7, :])
            keep_product(T - 1)

            act.wait_ge(sem("factor_in1"), 1)
            A(roots[:, :, :], roots_in[:, :, :], ACT.Sqrt).then_inc(sem("factor_out1"), 1)
            act.wait_ge(sem("factor_in2"), 1)
            A(bt[:, 1, :], bt[:, 0, :], ACT.Ln).then_inc(sem("factor_out2"), 1)
            act.wait_ge(sem("factor_in3"), 1)
            A(bt[:, 1, :], bt[:, 0, :], ACT.Tanh).then_inc(sem("factor_out3"), 1)

            zp = zp_view(MOB)
            act.wait_ge(*at("z_scale_ready", MOB, 1))
            A(zp[:, :, 0, D], gamma1[:, :], ACT.Copy, scale=z_scale[:, 0:1]).then_inc(sem("z_high_done"), 1)
            with act.Fori(0, CHUNKS) as c:
                for s in range(4):
                    last = A_at(zp[:, 4 * c + s, 0, 0:D], Z[:, 4 * c + s, 0:D], ACT.Copy,
                                scale=z_factor[:, bass.ds(4 * c + s, 1)])
                last.then_inc(sem("z_high_done"), 1)

            with act.Fori(0, GROUPS) as g:
                act.wait_ge(sem("mob_in1"), g + 1)
                for s in range(SLOTS):
                    last = A_at(junk_mob[:, s, :], Z[:, SLOTS * g + s, 0:D], ACT.Square, scale=gt[:, 0, s:s + 1],
                             accum_out=gt[:, 1, s:s + 1])
                last.then_inc(sem("mob_out1"), 1)
                act.wait_ge(sem("mob_in2"), g + 1)
                A(gt[:, 4:6, :], gt[:, 2:4, :], ACT.Sqrt).then_inc(sem("mob_out2"), 1)
                act.wait_ge(sem("mob_in3"), g + 1)
                A(gt[:, 11, :], gt[:, 10, :], ACT.Ln).then_inc(sem("mob_out3"), 1)
                act.wait_ge(sem("mob_in4"), g + 1)
                A(gt[:, 11, :], gt[:, 10, :], ACT.Tanh).then_inc(sem("mob_out4"), 1)
                act.wait_ge(sem("mob_in5"), g + 1)
                A(gt[:, 11, :], gt[:, 10, :], ACT.Ln).then_inc(sem("mob_out5"), 1)
                act.wait_ge(sem("mob_in6"), g + 1)
                for s in range(SLOTS):
                    last = A_at(Z[:, SLOTS * g + s, 0:D], Z[:, SLOTS * g + s, 0:D], ACT.Relu, scale=gt[:, 12, s:s + 1])
                last.then_inc(sem("mob_relu"), 1)
                act.wait_ge(sem("mob_relu"), g + 1)
                for s in range(SLOTS):
                    last = A_at(junk_mob[:, s, :], Z[:, SLOTS * g + s, 0:D], ACT.Square, accum_out=gt[:, 1, s:s + 1])
                last.then_inc(sem("mob_out6"), 1)
                act.wait_ge(sem("mob_in7"), g + 1)
                A(gt[:, 11, :], gt[:, 10, :], ACT.Sqrt).then_inc(sem("mob_out7"), 1)
                act.wait_ge(sem("mob_out7"), g + 1)
                A(gt[:, 10, :], gt[:, 11, :], ACT.Tanh).then_inc(sem("mob_out8"), 1)
                act.wait_ge(sem("mob_in8"), g + 1)
                A(gt[:, 14, :], gt[:, 13, :], ACT.Sqrt).then_inc(sem("mob_out9"), 1)
                act.wait_ge(*at("xs_ready", MOB, SLOTS * g + SLOTS))
                act.dma_start(x_dram[g], xs4[:, :, :].rearrange("p s f -> p (s f)")).then_inc(
                    sem("x_stored"), 16)
                for s in range(SLOTS):
                    keep_xT(MOB, SLOTS * g + s, xT, bank[:, 6, :])

            def keep_half(stage, t, b):
                w = WIDTH[stage]
                act.wait_ge(*at("agg_done", stage, t + 1))
                act.wait_ge(*at("acc_read", stage, t))
                A_at(half[:, 0:w], bank[:, b, w:2 * w], ACT.Copy, scale=unscale_of(stage)[:, bass.ds(t, 1)]).then_inc(
                    sem("half_ready"), 1)

            def keep_rT(stage, t, func):
                w = WIDTH[stage]
                act.wait_ge(*at("r_turned", stage, t + 1))
                A(xT[0:w, 0:P], bank[0:w, 6, 0:P], func).then_inc(sem("rT_ready"), 1)

            for stage in (G1, G2, G3, G4, G5, G6):
                act.wait_ge(*at("z_scale_ready", stage, 1))
                with act.Fori(0, T // 2) as i:
                    for b in range(2):
                        t = 2 * i + b
                        keep_half(stage, t, b)
                        if stage in (G1, G2):
                            keep_rT(stage, t, ACT.Relu)
                        if stage in (G4, G6):
                            keep_rT(stage, t, ACT.Copy)
                        if stage == G4:
                            act.wait_ge(*at("z_turned", stage, t + 1))
                            act.wait_ge(*at("prod_ready", stage, t))
                            A(zT[:, 0:P], bank[:, 4, 0:P], ACT.Copy).then_inc(sem("zT_ready"), 1)
                        if stage == G6:
                            root_var(stage, t)

            with act.Fori(0, T // 2) as i:
                for b in range(2):
                    t = 2 * i + b
                    keep_xT(NORM, t, zT, bank[:, 4, :])
                    root_var(NORM, t)
                    act.wait_ge(*at("rows_ready", NORM, t + 1))
                    act.dma_start(out_rows[t], xs4[:, b, :]).then_inc(sem(f"out_done{b}"), 16)
            for b in range(2):
                act.wait_ge(sem(f"out_done{b}"), 16 * (T // 2))

        @block.vector
        def _(dve):
            V = nc.vector

            def find_max(stage, bounds, two_axes=False):
                V.tensor_reduce(z_max[:, :], bounds, AX.XY if two_axes else AX.X, ALU.max,
                                apply_absolute_value=True).then_inc(sem("z_max_ready"), 1)

            def scales(stage, link):
                gain, top = gains[:, stage:stage + 1] if stage in range(G1, NORM) else 1.0, gains[:, G1:G1 + 1]
                if stage == G1:
                    gain = 1.0
                else:
                    dve.wait_ge(*at("z_max_turned", stage, 1))
                    top = z_top[:, 0:1]
                    link(V.tensor_reduce(top, bank[0:1, 7, 0:P], AX.X, ALU.max))
                link(V.tensor_scalar(z_top[:, 1:2], top, gain, TINY, ALU.mult, ALU.max))
                link(V.tensor_scalar(z_top[:, 2:3].bitcast(I32), z_top[:, 1:2].bitcast(I32), EXPONENT, None,
                                     ALU.bitwise_and))
                link(V.reciprocal(z_top[:, 3:4], z_top[:, 2:3]))
                V.tensor_scalar(z_pair[:, 0:1], z_top[:, 3:4], TOP, None, ALU.mult)
                V.tensor_scalar(z_pair[:, 1:2], z_top[:, 2:3], 1.0 / TOP, None, ALU.mult).then_inc(
                    sem("z_pair_ready"), 1)
                dve.wait_ge(*at("z_pair_sent", stage, 1))
                if stage == "inc":
                    V.tensor_copy(z_scale[:, :], bank[:, 7, 256:258]).then_inc(sem("z_scale_ready"), 1)
                    return
                link(V.tensor_copy(z_scale[:, :], bank[:, 7, 256:258]))
                if stage == MOB:
                    V.tensor_scalar(z_factor[:, :], bt[:, 8, :], z_scale[:, 0:1], None, ALU.mult)
                if stage == NORM:
                    V.tensor_scalar(norm_factor[:, :], deg_root[:, :], z_scale[:, 0:1], None, ALU.mult)
                    V.scalar_tensor_tensor(unscale_norm[:, :], row_inv[:, :], z_scale[:, 1:2], roots[:, 2, :],
                                           ALU.mult, ALU.mult).then_inc(sem("z_scale_ready"), 1)
                else:
                    V.tensor_scalar(unscale_of(stage)[:, :], row_inv[:, :], z_scale[:, 1:2], None,
                                    ALU.mult).then_inc(sem("z_scale_ready"), 1)
                dve.wait_ge(*at("z_scale_ready", stage, 1))

            def write_z(link, stage, t, src, factor):
                zp = zp_view(stage)
                link(V.tensor_scalar(zp[:, t, 0, :], src, factor, None, ALU.mult))
                V.scalar_tensor_tensor(zp[:, t, 1, :], src, factor, zp[:, t, 0, :], ALU.mult,
                                       ALU.subtract).then_inc(sem("z_split"), 1)

            def bound_z(t, src, done):
                V.tensor_reduce(z_bound[:, bass.ds(t, 1)], src, AX.X, ALU.max,
                                apply_absolute_value=True).then_inc(sem(done), 1)

            def split_low(stage, src):
                zp = zp_view(stage)
                w = zp.shape[3]
                for c in range(CHUNKS):
                    for_c = slice(4 * c, 4 * c + 4)
                    dve.wait_ge(*at("z_high_done", stage, c + 1))
                    V.scalar_tensor_tensor(zp[:, for_c, 1, :], src[:, for_c, 0:w], z_scale[:, 0:1],
                                           zp[:, for_c, 0, :], ALU.mult, ALU.subtract).then_inc(
                                               sem("z_low_done"), 1)

            def mean_var(link, src, n=0):
                link(V.bn_stats(bn6[:, n, :], src))
                dve.sem_inc(sem("dve_marks"), 1)
                link(V.bn_aggr(mv[:, n, :], bn6[:, n, :]))

            def norm_ready(stage, link, src):
                mean_var(link, src)
                V.tensor_scalar(stat[:, 0:1], mv[:, 0, 1:2], LN_EPS, None, ALU.add).then_inc(sem("var_ready"), 1)

            def norm_rows(stage, link, t, dst, src, ready):
                dve.wait_ge(*at("dev_ready", stage, t + 1))
                link(V.reciprocal(stat[:, 2:3], stat[:, 1:2]))
                V.tensor_scalar(dst, src, mv[:, 0, 0:1], stat[:, 2:3], ALU.subtract, ALU.mult).then_inc(
                    sem(ready), 1)

            def split_x(link, n, src, factor):
                link(V.tensor_scalar(xp4[:, n, 0, :], src, factor, None, ALU.mult))
                V.scalar_tensor_tensor(xp4[:, n, 1, :], src, factor, xp4[:, n, 0, :], ALU.mult,
                                       ALU.subtract).then_inc(sem("xp_ready"), 1)

            READ, SCALE, EDGE = 5, 4, 6

            def scale_of_rows(t):
                link = Chain(dve, sem("dve_scale_of"), SCALE * t)
                dve.wait_ge(sem("magnitudes"), NG * t + NG)
                link(V.tensor_reduce(stat[:, 3:4], abs_parts[:, t, :], AX.X, ALU.add))
                link(V.tensor_scalar(stat[:, 4:5], stat[:, 3:4], 1.0, None, ALU.add))
                link(V.tensor_scalar(stat[:, 5:6].bitcast(I32), stat[:, 4:5].bitcast(I32), EXPONENT, None,
                                     ALU.bitwise_and))
                link(V.reciprocal(stat[:, 6:7], stat[:, 5:6]))
                V.tensor_scalar(row_inv[:, bass.ds(t, 1)], stat[:, 5:6], 1.0 / TOP, None, ALU.mult)
                V.tensor_scalar(row_scale[:, bass.ds(t, 1)], stat[:, 6:7], TOP, None, ALU.mult).then_inc(
                    sem("row_scale_ready"), 1)

            def split_rows(t, b, g):
                n = NG * t + g
                quarter = slice(g * GK * P, (g + 1) * GK * P)
                dve.wait_ge(sem("row_scale_ready"), t + 1)
                if not (isinstance(t, int) and t == 0):
                    dve.wait_ge(sem("turned"), n + 1 - NG)
                V.scalar_tensor_tensor(ROWS[:, 2, quarter], RAW[:, b, quarter], 0.0,
                                       least[:, :].to_broadcast([P, GK * P]), ALU.is_gt, ALU.mult,
                                       accum_out=count_parts[:, t, g:g + 1]).then_inc(sem("positives_done"), 1)
                dve.wait_ge(sem("positives_done"), n + 1)
                V.scalar_tensor_tensor(ROWS[:, 0, quarter], RAW[:, b, quarter], row_scale[:, bass.ds(t, 1)],
                                       ROWS[:, 2, quarter], ALU.mult, ALU.add).then_inc(sem("high_rows_done"), 1)
                dve.wait_ge(sem("high_rows_done"), n + 1)
                V.scalar_tensor_tensor(ROWS[:, 1, quarter], RAW[:, b, quarter], row_scale[:, bass.ds(t, 1)],
                                       ROWS[:, 0, quarter], ALU.mult, ALU.subtract).then_inc(sem("rows_split"), 1)

            def total_rows(t):
                dve.wait_ge(sem("row_sums_done"), NG * t + NG)
                V.tensor_reduce(row_sum[:, bass.ds(t, 1)], sum_parts[:, t, :], AX.X, ALU.add)
                V.tensor_reduce(count[:, bass.ds(t, 1)], count_parts[:, t, :], AX.X, ALU.add).then_inc(
                    sem("counted"), 1)

            def edge_factors(t):
                link = Chain(dve, sem("dve_edge"), EDGE * t)
                one = bass.ds(t, 1)
                dve.wait_ge(sem("count_rooted"), t + 1)
                link(V.tensor_scalar(stat[:, 8:9], root_count[:, one], NORM_EPS, None, ALU.max))
                link(V.reciprocal(stat[:, 9:10], stat[:, 8:9]))
                V.tensor_scalar(stat[:, 14:15], stat[:, 9:10], 1.0 / LEAST, None, ALU.mult)
                link(V.tensor_tensor(row_sum[:, one], row_sum[:, one], row_inv[:, one], ALU.mult))
                link(V.scalar_tensor_tensor(stat[:, 10:11], count[:, one], stat[:, 14:15], row_sum[:, one],
                                            ALU.mult, ALU.add))
                link(V.reciprocal(stat[:, 11:12], stat[:, 10:11]))
                V.tensor_scalar(stat[:, 12:13], row_inv[:, one], z_scale[:, 1:2], stat[:, 11:12], ALU.mult, ALU.mult)
                link(V.tensor_scalar(stat[:, 13:14], stat[:, 9:10], z_scale[:, 1:2], stat[:, 11:12], ALU.mult,
                                     ALU.mult))

            def read_sums(t, b):
                link = Chain(dve, sem("dve_read"), READ * t)
                dve.wait_ge(sem("group_used"), NG * t + NG)
                link(V.scalar_tensor_tensor(yb, SUMS[b][:, 0:D], stat[:, 12:13], X[:, t, :], ALU.mult, ALU.add))
                V.scalar_tensor_tensor(y, SUMS[b][:, D:2 * D], stat[:, 13:14], yb, ALU.mult, ALU.add).then_inc(
                    sem("acc_read"), 1)
                if not (isinstance(t, int) and t + 2 >= T):
                    scale_of_rows(t + 2)
                dve.wait_ge(*at("acc_read", "inc", t + 1))
                norm_ready("inc", link, y)

            def finish_rows(t):
                if not (isinstance(t, int) and t == 0):
                    dve.wait_ge(*at("xs_turned", "inc", t))
                    dve.wait_ge(sem("x_squared"), t)
                    dve.wait_ge(*at("x_kept", "inc", t))
                link = Chain(dve, sem("dve_read"), READ * t + READ - 2)
                norm_rows("inc", link, t, xs, y, "xs_ready")
                dve.wait_ge(*at("xs_ready", "inc", t + 1))
                split_x(link, 0, xs, NORMED)

            def top_weights():
                V.memset(w_tops[:, :], 0.0).then_inc(sem("w_tops_empty"), 1)
                dve.wait_ge(sem("w_tops_empty"), 1)
                dve.wait_ge(sem("weights_in"), 16 * 9)
                V.tensor_reduce(w_tops[:, 0:2], w1_sb[:, :, :], AX.X, ALU.max, apply_absolute_value=True)
                for n, (w_sb, rows_in) in enumerate(((w2_sb, P), (w3_sb, P), (w4_sb, H2), (w5_sb, P))):
                    V.tensor_reduce(w_tops[0:rows_in, G2 + n:G2 + n + 1], w_sb[:, :], AX.X, ALU.max,
                                    apply_absolute_value=True)
                for n, w_sb in enumerate((wmob_sb, w1_sb, wnorm_sb)):
                    last = V.tensor_reduce(w_tops[:, 8 + n:9 + n], w_sb[:, :, :], AX.XY, ALU.max,
                                           apply_absolute_value=True)
                last.then_inc(sem("w_max_ready"), 1)

            def scale_weights():
                link = Chain(dve, sem("dve_w"))
                dve.wait_ge(sem("w_turned"), 1)
                link(V.tensor_reduce(w_top[:, 0:1], bank[0:3, 2, 0:P], AX.X, ALU.max))
                link(V.tensor_scalar(w_top[:, 1:2], w_top[:, 0:1], TINY, None, ALU.max))
                link(V.tensor_scalar(w_top[:, 2:3].bitcast(I32), w_top[:, 1:2].bitcast(I32), EXPONENT, None,
                                     ALU.bitwise_and))
                link(V.reciprocal(w_top[:, 3:4], w_top[:, 2:3]))
                V.tensor_scalar(w_diag[:, 0:3], ident[0:3, 0:3], w_top[:, 3:4], TOP, ALU.mult, ALU.mult)
                V.tensor_scalar(w_diag[:, 3:6], ident[0:3, 0:3], w_top[:, 2:3], 1.0 / TOP, ALU.mult,
                                ALU.mult).then_inc(sem("w_diag_ready"), 1)

            def keep_weight_scales():
                dve.wait_ge(sem("w_sent"), 1)
                V.tensor_copy(w_scales[:, :], bank[:, 2, 264:270])
                V.tensor_scalar(w_back[:, :], bank[:, 2, 267:269], 1.0 / NORMED, None, ALU.mult).then_inc(
                    sem("w_scale_ready"), 1)

            dve.wait_ge(sem("ident_ready"), 3)
            scale_of_rows(0)
            for g in range(NG):
                split_rows(0, 0, g)
            dve.wait_ge(sem("x_bounded"), 8)
            find_max("inc", x_max[:, :])
            scales("inc", Chain(dve, sem("dve_start")))
            for c in range(4):
                dve.wait_ge(sem(f"x_in{c}"), 16)
            split_low("inc", X)
            scale_of_rows(1)

            def pair_of_tiles(i):
                for b in range(2):
                    t = 2 * i + b
                    fixed = isinstance(t, int)
                    for g in range(NG):
                        n = NG * t + g
                        if g == 0 and not (fixed and t == 0):
                            read_sums(t - 1, 1 - b)
                        if fixed and (t, g) == (1, 2):
                            keep_weight_scales()
                        if g == 1 and not (fixed and t == 0):
                            finish_rows(t - 1)
                        if not (fixed and t + 1 >= T):
                            split_rows(t + 1, 1 - b, g)
                        if g == 0:
                            total_rows(t)
                        if g == 2:
                            edge_factors(t)
                        if fixed and (t, g) == (0, 1):
                            top_weights()
                        if fixed and (t, g) == (1, 0):
                            scale_weights()

            pair_of_tiles(0)
            with dve.Fori(1, T // 2 - 1) as i:
                pair_of_tiles(i)
            pair_of_tiles(T // 2 - 1)
            read_sums(T - 1, 1)
            finish_rows(T - 1)

            link = Chain(dve, sem("dve_factors"))

            def magnitude(dst, src):
                return V.scalar_tensor_tensor(dst, src, -1.0, src, ALU.mult, ALU.max)

            def artanh_in(link, w, u, c, t0, t1):
                link(V.tensor_scalar(t0, c, -1.0, 1.0, ALU.mult, ALU.add))
                link(V.reciprocal(t1, t0))
                link(V.scalar_tensor_tensor(u, c, 2.0, t1, ALU.mult, ALU.mult))
                return V.tensor_scalar(w, u, 1.0, None, ALU.add)

            def artanh_out(link, dst, log_w, w, u, c, t0, t1):
                link(V.tensor_scalar(t0, w, -1.0, 1e-30, ALU.add, ALU.max))
                link(V.reciprocal(t1, t0))
                link(V.tensor_tensor(t0, u, t1, ALU.mult))
                link(V.scalar_tensor_tensor(t1, log_w, 0.5, t0, ALU.mult, ALU.mult))
                link(V.tensor_tensor(dst, t1, c, ALU.max))

            dve.wait_ge(sem("x_squared"), T)
            dve.wait_ge(sem("m_squared"), T)
            V.tensor_scalar(roots_in[:, 0, :], x_sq[:, :], EPS * EPS, None, ALU.max)
            V.tensor_scalar(roots_in[:, 1, :], m_sq[:, :], EPS * EPS, None, ALU.max)
            link(V.tensor_scalar(bt[:, 9, :], row_sum[:, :], 1.0, None, ALU.add))
            V.tensor_scalar(roots_in[:, 2, :], bt[:, 9, :], 1e-30, None, ALU.max).then_inc(sem("factor_in1"), 1)
            dve.wait_ge(sem("factor_out1"), 1)
            xn, mn, dn = roots[:, 0, :], roots[:, 1, :], roots[:, 2, :]
            link(V.tensor_scalar(bt[:, 2, :], xn, CLIP, None, ALU.min))
            artanh_in(link, bt[:, 0, :], bt[:, 3, :], bt[:, 2, :], bt[:, 4, :], bt[:, 5, :]).then_inc(
                sem("factor_in2"), 1)
            dve.wait_ge(sem("factor_out2"), 1)
            artanh_out(link, bt[:, 6, :], bt[:, 1, :], bt[:, 0, :], bt[:, 3, :], bt[:, 2, :], bt[:, 4, :], bt[:, 5, :])
            link(V.reciprocal(bt[:, 4, :], xn))
            link(V.tensor_tensor(bt[:, 5, :], mn, bt[:, 4, :], ALU.mult))
            V.tensor_tensor(bt[:, 0, :], bt[:, 5, :], bt[:, 6, :], ALU.mult).then_inc(sem("factor_in3"), 1)
            dve.wait_ge(sem("factor_out3"), 1)
            link(V.reciprocal(bt[:, 4, :], mn))
            link(V.tensor_tensor(bt[:, 5, :], bt[:, 1, :], bt[:, 4, :], ALU.mult))
            link(V.scalar_tensor_tensor(bt[:, 6, :], mn, EPS, bt[:, 5, :], ALU.is_gt, ALU.mult))
            link(V.tensor_tensor(bt[:, 4, :], bt[:, 6, :], bt[:, 6, :], ALU.mult))
            link(V.tensor_tensor(bt[:, 5, :], bt[:, 4, :], m_sq[:, :], ALU.mult))
            link(V.tensor_scalar(bt[:, 4, :], bt[:, 5, :], -1.0, 1.0, ALU.mult, ALU.add))
            link(V.reciprocal(bt[:, 5, :], bt[:, 4, :]))
            link(V.tensor_scalar(bt[:, 7, :], bt[:, 5, :], 2.0, 1e-15, ALU.mult, ALU.max))
            link(V.tensor_scalar(gamma1[:, :], bt[:, 7, :], -1.0, None, ALU.add))
            link(V.tensor_tensor(bt[:, 8, :], bt[:, 7, :], bt[:, 6, :], ALU.mult))
            link(V.tensor_tensor(bt[:, 4, :], bt[:, 8, :], mn, ALU.mult))
            link(magnitude(bt[:, 5, :], bt[:, 4, :]))
            link(magnitude(bt[:, 3, :], gamma1[:, :]))
            link(V.tensor_tensor(z_bound[:, :], bt[:, 5, :], bt[:, 3, :], ALU.max))

            find_max(MOB, z_bound[:, :])
            scales(MOB, link)
            zp = zp_view(MOB)
            dve.wait_ge(*at("z_high_done", MOB, 1))
            V.scalar_tensor_tensor(zp[:, :, 1, D], gamma1[:, :], z_scale[:, 0:1], zp[:, :, 0, D], ALU.mult,
                                   ALU.subtract)
            with dve.Fori(0, CHUNKS) as c:
                dve.wait_ge(*at("z_high_done", MOB, c + 2))
                for s in range(4):
                    last = V.scalar_tensor_tensor(zp[:, 4 * c + s, 1, 0:D], Z[:, 4 * c + s, 0:D],
                                                  z_factor[:, bass.ds(4 * c + s, 1)], zp[:, 4 * c + s, 0, 0:D],
                                                  ALU.mult, ALU.subtract)
                last.then_inc(sem("z_low_done"), 1)

            link(V.reciprocal(bt[:, 2, :], roots[:, 2, :]))
            link(V.scalar_tensor_tensor(deg_root[:, :], bt[:, 9, :], 0.0, bt[:, 2, :], ALU.is_gt, ALU.mult))
            V.tensor_tensor(inv_degree[:, :], deg_root[:, :], deg_root[:, :], ALU.mult)
            link(V.tensor_scalar(norm_bound[:, :], deg_root[:, :], float(D) ** 0.5, None, ALU.mult))

            V.tensor_reduce(row_top[:, :], row_inv[:, :], AX.X, ALU.max).then_inc(sem("tops_ready"), 1)
            dve.wait_ge(sem("tops_sent"), 1)
            link = Chain(dve, sem("dve_gains"))
            link(V.tensor_reduce(z_top[:, 0:1], bank[0:1, 7, 0:P], AX.X, ALU.max))
            link(V.tensor_copy(w_sums[:, :], bank[0:1, 7, 384:392]))
            link(V.tensor_scalar(gains[:, G4:G4 + 1], z_top[:, 0:1], 2.0 * TOP, None, ALU.mult))
            V.tensor_scalar(gains[:, G6:G6 + 1], gains[:, G4:G4 + 1], 1.0, None, ALU.mult)
            V.tensor_scalar(gains[:, G2:G2 + 1], w_sums[:, G2:G2 + 1], gains[:, G4:G4 + 1], w_back[0:1, 1:2],
                            ALU.mult, ALU.mult)
            V.tensor_scalar(gains[:, G3:G3 + 1], w_sums[:, G3:G3 + 1], gains[:, G4:G4 + 1], None, ALU.mult)
            V.tensor_scalar(gains[:, G5:G5 + 1], w_sums[:, G4:G4 + 1], w_sums[:, G5:G5 + 1], gains[:, G4:G4 + 1],
                            ALU.mult, ALU.mult)
            link(V.tensor_scalar(gains[:, G1:G1 + 1], w_sums[:, 0:1], w_sums[:, 1:2], float(D) ** 0.5,
                                 ALU.add, ALU.mult))
            find_max(NORM, norm_bound[:, :])
            scales(G1, Chain(dve, *at("dve_scales", G1, 0)))
            V.tensor_scalar(z_keep[:, :], z_scale[:, 0:1], w_back[:, 1:2], None, ALU.mult).then_inc(
                sem("z_kept"), 1)
            dve.wait_ge(sem("z_kept"), 1)
            scales(NORM, Chain(dve, *at("dve_scales", NORM, 0)))
            link = Chain(dve, sem("dve_row_factors"))
            link(V.tensor_scalar(bt[:, 0, :], unscale_norm[:, :], 4.0 * TOP * TOP, float(D) ** 0.5, ALU.mult,
                                 ALU.add))
            link(V.tensor_scalar(bt[:, 1, :].bitcast(I32), bt[:, 0, :].bitcast(I32), EXPONENT, None,
                                 ALU.bitwise_and))
            link(V.reciprocal(bt[:, 2, :], bt[:, 1, :]))
            link(V.tensor_scalar(row_factor[:, :], bt[:, 2, :], TOP, None, ALU.mult))
            link(V.tensor_scalar(bt[:, 3, :], bt[:, 1, :], w_scales[:, 5:6], 1.0 / TOP, ALU.mult, ALU.mult))
            link(V.tensor_tensor(out_factor[:, :], bt[:, 3, :], inv_degree[:, :], ALU.mult))

            MOB_STEPS = 62

            def row(n):
                return gt[:, n, :]

            with dve.Fori(0, GROUPS) as g:
                link = Chain(dve, sem("dve_mob"), MOB_STEPS * g)
                rows = bass.ds(SLOTS * g, SLOTS)
                for s in range(SLOTS):
                    t = SLOTS * g + s
                    dve.wait_ge(*at("agg_done", MOB, t + 1))
                    V.tensor_scalar(Z[:, t, 0:D + 1], bank[:, s, 0:D + 1], 1.0, None, ALU.mult).then_inc(sem("acc_read"), 1)
                dve.wait_ge(*at("acc_read", MOB, SLOTS * g + SLOTS))
                link(V.tensor_tensor(row(15), Z[:, rows, D], unscales[:, 0, rows], ALU.mult))
                link(V.tensor_scalar(row(16), row(15), 0.0, 2.0, ALU.is_ge, ALU.mult))
                link(V.tensor_scalar(row(17), row(16), -1.0, None, ALU.add))
                link(magnitude(row(18), row(15)))
                link(V.tensor_scalar(row(16), row(18), EPS, None, ALU.max))
                link(V.tensor_tensor(row(15), row(16), row(17), ALU.mult))
                link(V.reciprocal(row(16), row(15)))
                V.tensor_tensor(row(0), row(16), unscales[:, 0, rows], ALU.mult).then_inc(sem("mob_in1"), 1)
                dve.wait_ge(sem("mob_out1"), g + 1)
                link(V.tensor_scalar(row(15), row(1), -1.0, 1.0, ALU.mult, ALU.add))
                V.tensor_scalar(row(2), row(15), EPS, None, ALU.max)
                V.tensor_scalar(row(3), row(1), 1.0, None, ALU.mult).then_inc(sem("mob_in2"), 1)
                dve.wait_ge(sem("mob_out2"), g + 1)
                link(V.tensor_scalar(row(15), row(4), 1.0, None, ALU.add))
                link(V.reciprocal(row(6), row(15)))
                link(V.tensor_tensor(row(7), row(5), row(6), ALU.mult))
                link(V.tensor_scalar(row(8), row(7), EPS, None, ALU.max))
                link(V.tensor_scalar(row(9), row(8), CLIP, None, ALU.min))
                artanh_in(link, row(10), row(18), row(9), row(16), row(17)).then_inc(sem("mob_in3"), 1)
                dve.wait_ge(sem("mob_out3"), g + 1)
                artanh_out(link, row(19), row(11), row(10), row(18), row(9), row(16), row(17))
                V.tensor_tensor(row(10), row(19), row_sum[:, rows], ALU.mult).then_inc(sem("mob_in4"), 1)
                dve.wait_ge(sem("mob_out4"), g + 1)
                link(V.reciprocal(row(16), row(8)))
                link(V.tensor_tensor(row(20), row(11), row(16), ALU.mult))
                link(V.tensor_tensor(row(15), row(7), row(20), ALU.mult))
                link(magnitude(row(16), row(15)))
                link(V.tensor_scalar(row(21), row(16), EPS, None, ALU.max))
                link(V.tensor_scalar(row(9), row(21), CLIP, None, ALU.min))
                artanh_in(link, row(10), row(18), row(9), row(16), row(17)).then_inc(sem("mob_in5"), 1)
                dve.wait_ge(sem("mob_out5"), g + 1)
                artanh_out(link, row(19), row(11), row(10), row(18), row(9), row(16), row(17))
                link(V.reciprocal(row(16), row(21)))
                link(V.tensor_tensor(row(17), row(19), row(16), ALU.mult))
                link(V.tensor_tensor(row(16), row(17), row(20), ALU.mult))
                link(V.tensor_tensor(row(17), row(16), row(6), ALU.mult))
                V.tensor_tensor(row(12), row(17), row(0), ALU.mult).then_inc(sem("mob_in6"), 1)
                dve.wait_ge(sem("mob_out6"), g + 1)
                V.tensor_scalar(row(10), row(1), EPS * EPS, None, ALU.max).then_inc(sem("mob_in7"), 1)
                dve.wait_ge(sem("mob_out8"), g + 1)
                link(V.reciprocal(row(16), row(11)))
                link(V.tensor_tensor(row(15), row(10), row(16), ALU.mult))
                for s in range(SLOTS):
                    t = SLOTS * g + s
                    link(V.scalar_tensor_tensor(y4[:, s, :], Z[:, t, 0:D], gt[:, 15, s:s + 1], X[:, t, :],
                                                ALU.mult, ALU.add))
                    mean_var(link, y4[:, s, :], s)
                V.tensor_scalar(row(13), mv[:, :, 1], LN_EPS, None, ALU.add).then_inc(sem("mob_in8"), 1)
                dve.wait_ge(sem("mob_out9"), g + 1)
                link(V.reciprocal(row(15), row(14)))
                dve.wait_ge(*at("xs_turned", MOB, SLOTS * g))
                dve.wait_ge(*at("x_kept", MOB, g))
                for s in range(SLOTS):
                    V.tensor_scalar(xs4[:, s, :], y4[:, s, :], mv[:, s, 0:1], gt[:, 15, s:s + 1], ALU.subtract,
                                    ALU.mult).then_inc(sem("xs_ready"), 1)
                for s in range(SLOTS):
                    dve.wait_ge(*at("xs_ready", MOB, SLOTS * g + s + 1))
                    split_x(link, s, xs4[:, s, :], NORMED)
                for s in range(SLOTS):
                    t = SLOTS * g + s
                    dve.wait_ge(*at("prod_ready", MOB, t + 1))
                    write_z(link, G1, t, bank[:, 7, 0:H], z_keep[:, 0:1])
                    bound_z(t, bank[:, 7, 0:H], "prod_read")
                assert link.n == MOB_STEPS, link.n

            def finish_conv(stage, i, b):
                w = WIDTH[stage]
                t = 2 * i + b
                first = isinstance(t, int) and t == 0
                link = Chain(dve, *at("dve_conv", stage, CONV_STEPS[stage] * t))
                scale = z_scale[:, 0:1]
                if first and stage < G6:
                    dve.wait_ge(*at("small_read" if stage in (G2, G3) else "prod_read", stage - 1, T))
                    find_max(stage + 1, z_bound[:, :])
                dve.wait_ge(*at("half_ready", stage, t + 1))
                V.scalar_tensor_tensor(r[:, 0:w], bank[:, b, 0:w], unscale_of(stage)[:, bass.ds(t, 1)],
                                       half[:, 0:w], ALU.mult, ALU.add).then_inc(sem("acc_read"), 1)
                if first and stage < G6:
                    scales(stage + 1, Chain(dve, *at("dve_scales", stage + 1, 0)))
                if stage in (G3, G5):
                    dve.wait_ge(*at("acc_read", stage, t + 1))
                    link(V.tensor_scalar(y[:, 0:w], r[:, 0:w], 0.0, None, ALU.max))
                    write_z(link, stage + 1, t, y[:, 0:w], scale)
                    bound_z(t, y[:, 0:w], "prod_read")
                    return
                dve.wait_ge(*at("small_ready", stage, t + 1))
                if stage in (G1, G2):
                    wo = WIDTH[stage + 1]
                    write_z(link, stage + 1, t, bank[:, 7, 0:wo], scale)
                    bound_z(t, bank[:, 7, 0:wo], "small_read")
                elif stage == G4:
                    V.tensor_scalar(z4[:, :], bank[:, 7, 0:H], 0.0, None, ALU.max).then_inc(sem("small_read"), 1)
                    dve.wait_ge(*at("prod_ready", stage, t + 1))
                    write_z(link, stage + 1, t, bank[:, 5, 0:H], scale)
                    bound_z(t, bank[:, 5, 0:H], "prod_read")
                else:
                    V.scalar_tensor_tensor(y, bank[:, 7, 0:D], 0.0, X[:, t, :], ALU.max, ALU.add).then_inc(
                        sem("small_read"), 1)
                    dve.wait_ge(*at("small_read", stage, t + 1))
                    norm_ready(stage, link, y)
                    dve.wait_ge(*at("x_kept", stage, t))
                    norm_rows(stage, link, t, xs, y, "rows_ready")
                    dve.wait_ge(*at("rows_ready", stage, t + 1))
                    write_z(link, NORM, t, xs, norm_factor[:, bass.ds(t, 1)])
                assert link.n == CONV_STEPS[stage], link.n

            for stage in (G1, G2, G3, G4, G5, G6):
                quarters = 4 if stage == G6 else 1
                for q in range(quarters):
                    if stage == G6:
                        dve.wait_ge(sem(f"x_back{q}"), 16)
                    if q == 0:
                        for b in range(2):
                            finish_conv(stage, 0, b)
                    with dve.Fori(max(1, q * T // 2 // quarters), (q + 1) * T // 2 // quarters) as i:
                        for b in range(2):
                            finish_conv(stage, i, b)

            dve.wait_ge(*at("x_kept", G6, T))
            OUT_STEPS = 5

            def out_pair(i):
                for b in range(2):
                    t = 2 * i + b
                    link = Chain(dve, sem("dve_out"), OUT_STEPS * t)
                    dve.wait_ge(*at("agg_done", NORM, t + 1))
                    V.scalar_tensor_tensor(yb, bank[:, b, 0:D], unscale_norm[:, bass.ds(t, 1)], X[:, t, :],
                                           ALU.mult, ALU.add).then_inc(sem("acc_read"), 1)
                    dve.wait_ge(*at("acc_read", NORM, t + 1))
                    split_x(link, 0, yb, row_factor[:, bass.ds(t, 1)])
                    dve.wait_ge(*at("prod_ready", NORM, t + 1))
                    V.scalar_tensor_tensor(yc, bank[:, 5, 0:D], out_factor[:, bass.ds(t, 1)], b_sb[:, :],
                                           ALU.mult, ALU.add).then_inc(sem("prod_read"), 1)
                    dve.wait_ge(*at("prod_read", NORM, t + 1))
                    link(V.scalar_tensor_tensor(y, yc, 0.0, X[:, t, :], ALU.max, ALU.add))
                    norm_ready(NORM, link, y)
                    if not isinstance(i, int):
                        dve.wait_ge(sem(f"out_done{b}"), 16 * i)
                    norm_rows(NORM, link, t, xs4[:, b, :], y, "rows_ready")
                    assert link.n == OUT_STEPS, link.n

            out_pair(0)
            with dve.Fori(1, T // 2) as i:
                out_pair(i)


_INS = ["x", "adj", "L1_gnn_W", "L2_gnn_W1", "L2_gnn_W2", "L2_gnn_W3", "L2_gnn_W4", "L2_gnn_W5", "L2_gnn_W6",
        "L3_gnn_W", "L3_gnn_b"]


def kernel(**inputs):
    import numpy as np
    import concourse.bacc as bacc
    from concourse.bass_utils import run_bass_kernel_spmd

    laid = {name: np.ascontiguousarray(inputs[name]) for name in _INS}
    laid["L3_gnn_W"] = np.ascontiguousarray(laid["L3_gnn_W"].T)
    laid["L3_gnn_b"] = np.ascontiguousarray(np.broadcast_to(laid["L3_gnn_b"], (P, laid["L3_gnn_b"].shape[0])))

    nc = bacc.Bacc("TRN2", target_bir_lowering=False, num_devices=1)
    arrays = {f"in_{n}": a for n, a in laid.items()}
    args = [nc.dram_tensor(f"in_{n}", a.shape, mybir.dt.from_np(a.dtype), kind="ExternalInput").ap()
            for n, a in laid.items()]
    out = nc.dram_tensor("out", laid["x"].shape, F32, kind="ExternalOutput").ap()
    build(nc, *args, out)
    result = run_bass_kernel_spmd(nc, [arrays], core_ids=[0])
    return result.results[0]["out"]
```
